# Optimizing a Trainium2 kernel written in Bass

```python
import numpy as np
import jax
import jax.numpy as jnp

def _softmax(x, axis=-1):
    return jax.nn.softmax(x, axis=axis)

def _gelu(x):
    return jax.nn.gelu(x, approximate=True)

def _silu(x):
    return jax.nn.silu(x)

def _sigmoid(x):
    return jax.nn.sigmoid(x)

def _layernorm(x, axis=-1, eps=1e-05):
    m = jnp.mean(x, axis=axis, keepdims=True)
    v = jnp.var(x, axis=axis, keepdims=True)
    return (x - m) / jnp.sqrt(v + eps)

def _scatter_add(tgt, idx, src, axis=0):
    return tgt.at[idx].add(src)

def _segment_sum(src, seg, n):
    return jax.ops.segment_sum(src, seg, n)
kernel_name = 'mk_vit_tower_postln_d4_tok_img256_r4_74540c'

def setup_inputs(seed: int=0):
    np.random.seed(seed)
    _w = jnp.asarray

    def _rec_inputs():
        import jax
        import jax.numpy as jnp
        _rk = jax.random.key(seed)
        x = -7.10856e-05 + 0.999911 * jax.random.normal(jax.random.fold_in(_rk, 1), (8, 64, 128, 64), jnp.float32)
        return x
    x = _rec_inputs()

    def _L0_tok_setup():
        import jax, jax.numpy as jnp
        import numpy as np
        PATCH_LEN = 16
        STRIDE = 8
        PAD = 8
        key = jax.random.key(seed)
        k1, k2 = jax.random.split(key)
        x = jax.random.normal(k1, (32, 64, 128, 64), dtype=jnp.float32)
        in_feat = 64 * (PATCH_LEN // 2 + 1) * 2
        W = jax.random.normal(k2, (64, in_feat), dtype=jnp.float32) * 0.02
        return {'x': x, 'W': W}
    _L0_tok_all = _L0_tok_setup()
    _L0_tok_in = {k: v for k, v in _L0_tok_all.items() if k in ('W',)}
    del _L0_tok_all

    def _L0_attn_setup():
        import jax, jax.numpy as jnp
        import numpy as np
        HEAD_SIZE = 64
        HEAD_SIZE_R = HEAD_SIZE // 4
        HEAD_SIZE_C = HEAD_SIZE - HEAD_SIZE_R
        N_EMBD = 64

        def rope(x, start_pos=0):
            B, T, d = x.shape
            half = d // 2
            theta = 1.0 / 10000.0 ** (jnp.arange(half, dtype=x.dtype) / half)
            idx = jnp.arange(start_pos, start_pos + T, dtype=x.dtype)[:, None] * theta[None, :]
            sin, cos = (jnp.sin(idx), jnp.cos(idx))
            xs = x.reshape(B, T, half, 2)
            x1, x2 = (xs[..., 0], xs[..., 1])
            rot = jnp.stack([x1 * cos - x2 * sin, x1 * sin + x2 * cos], axis=-1)
            return rot.reshape(B, T, d)

        def _reference_tuple_inner(x, Wq_comp, Wkv_comp, Wqc, Wqr, Wkc, Wkr, Wv):
            c_q = x @ Wq_comp
            c_kv = x @ Wkv_comp
            q_c = c_q @ Wqc
            q_r = rope(c_q @ Wqr, start_pos=0)
            q = jnp.concatenate([q_c, q_r], axis=-1)
            k_c = c_kv @ Wkc
            k_r = rope(c_kv @ Wkr, start_pos=0)
            k = jnp.concatenate([k_c, k_r], axis=-1)
            v = c_kv @ Wv
            scale = 1.0 / jnp.sqrt(jnp.asarray(HEAD_SIZE, dtype=x.dtype))
            wei = jnp.einsum('bqd,bkd->bqk', q, k) * scale
            T_q = q.shape[1]
            mask = jnp.tril(jnp.ones((T_q, T_q), dtype=bool))
            wei = jnp.where(mask, wei, jnp.asarray(-jnp.inf, dtype=wei.dtype))
            wei = jax.nn.softmax(wei, axis=-1)
            out = jnp.einsum('bqk,bkd->bqd', wei, v)
            return (out, (k, v))
        key = jax.random.key(seed)
        ks = jax.random.split(key, 8)
        B, T = (32, 512)
        s = 0.05
        return {'x': jax.random.normal(ks[0], (B, T, N_EMBD), dtype=jnp.float32), 'Wq_comp': jax.random.normal(ks[1], (N_EMBD, N_EMBD), dtype=jnp.float32) * s, 'Wkv_comp': jax.random.normal(ks[2], (N_EMBD, N_EMBD), dtype=jnp.float32) * s, 'Wqc': jax.random.normal(ks[3], (N_EMBD, HEAD_SIZE_C), dtype=jnp.float32) * s, 'Wqr': jax.random.normal(ks[4], (N_EMBD, HEAD_SIZE_R), dtype=jnp.float32) * s, 'Wkc': jax.random.normal(ks[5], (N_EMBD, HEAD_SIZE_C), dtype=jnp.float32) * s, 'Wkr': jax.random.normal(ks[6], (N_EMBD, HEAD_SIZE_R), dtype=jnp.float32) * s, 'Wv': jax.random.normal(ks[7], (N_EMBD, HEAD_SIZE), dtype=jnp.float32) * s}
    _L0_attn_all = _L0_attn_setup()
    _L0_attn_in = {k: v for k, v in _L0_attn_all.items() if k in ('Wq_comp', 'Wkv_comp', 'Wqc', 'Wqr', 'Wkc', 'Wkr', 'Wv')}
    del _L0_attn_all

    def _L0_ffn_setup():
        import jax, jax.numpy as jnp
        import numpy as np
        B, T, IN_DIM = (64, 64, 64)
        HID, OUT_DIM = (128, 64)
        N_LAYERS, N_EXPERTS, N_SHARED = (2, 16, 1)
        key = jax.random.key(seed)
        ks = jax.random.split(key, 10)
        s = 0.02
        x = jax.random.normal(ks[0], (B, T, IN_DIM), dtype=jnp.float32)
        route_id = jax.random.randint(ks[1], (B,), 0, N_EXPERTS)
        Wi = jax.random.normal(ks[2], (HID, IN_DIM), dtype=jnp.float32) * s
        bi = jnp.zeros((HID,), dtype=jnp.float32)
        Wr = jax.random.normal(ks[3], (N_LAYERS, N_EXPERTS, HID, HID), dtype=jnp.float32) * s
        br = jax.random.normal(ks[4], (N_LAYERS, N_EXPERTS, HID), dtype=jnp.float32) * s
        Ws = jax.random.normal(ks[5], (N_LAYERS, N_SHARED, HID, HID), dtype=jnp.float32) * s
        bs = jax.random.normal(ks[6], (N_LAYERS, N_SHARED, HID), dtype=jnp.float32) * s
        Wo = jax.random.normal(ks[7], (OUT_DIM, HID), dtype=jnp.float32) * s
        bo = jnp.zeros((OUT_DIM,), dtype=jnp.float32)
        return {'x': x, 'route_id': route_id, 'Wi': Wi, 'bi': bi, 'Wr': Wr, 'br': br, 'Ws': Ws, 'bs': bs, 'Wo': Wo, 'bo': bo}
    _L0_ffn_all = _L0_ffn_setup()
    _L0_ffn_in = {k: v for k, v in _L0_ffn_all.items() if k in ('route_id', 'Wi', 'bi', 'Wr', 'br', 'Ws', 'bs', 'Wo', 'bo')}
    del _L0_ffn_all

    def _L1_attn_setup():
        import jax, jax.numpy as jnp
        import numpy as np
        B, L, H, N, NLAYERS = (16, 512, 64, 64, 4)
        PRENORM = True

        def layer_norm(z, scale, bias, eps=1e-05):
            mu = jnp.mean(z, axis=-1, keepdims=True)
            var = jnp.var(z, axis=-1, keepdims=True)
            return (z - mu) * jax.lax.rsqrt(var + eps) * scale + bias

        def s4_block(u, log_dt, Alog, Aim, Cre, Cim, D, Wout, bout):
            Lq = u.shape[-1]
            dt = jnp.exp(log_dt)[:, None]
            A = -jnp.exp(Alog) + 1j * Aim
            C = Cre + 1j * Cim
            dtA = A * dt
            Cd = C * (jnp.exp(dtA) - 1.0) / A
            vand = jnp.exp(dtA[:, :, None] * jnp.arange(Lq))
            K = 2.0 * jnp.real(jnp.einsum('hn,hnl->hl', Cd, vand))
            n = 2 * Lq
            y = jnp.fft.irfft(jnp.fft.rfft(u, n=n) * jnp.fft.rfft(K, n=n), n=n)[..., :Lq]
            y = y + D[:, None] * u
            y = jax.nn.gelu(y)
            z = jnp.einsum('oh,bhl->bol', Wout, y) + bout[None, :, None]
            z1, z2 = jnp.split(z, 2, axis=1)
            return z1 * jax.nn.sigmoid(z2)
        key = jax.random.key(seed)
        ks = jax.random.split(key, 8)
        x = jax.random.normal(ks[0], (B, L, H), jnp.float32)
        log_dt = jnp.log(10.0 ** jax.random.uniform(ks[1], (NLAYERS, H), minval=-3.0, maxval=-1.0)).astype(jnp.float32)
        Alog = jnp.log(0.5 * jnp.ones((NLAYERS, H, N), jnp.float32))
        Aim = jnp.broadcast_to(np.pi * jnp.arange(N, dtype=jnp.float32), (NLAYERS, H, N)).copy()
        Cre = jax.random.normal(ks[2], (NLAYERS, H, N), jnp.float32) * 0.5 ** 0.5
        Cim = jax.random.normal(ks[3], (NLAYERS, H, N), jnp.float32) * 0.5 ** 0.5
        D = jax.random.normal(ks[4], (NLAYERS, H), jnp.float32)
        Wout = jax.random.normal(ks[5], (NLAYERS, 2 * H, H), jnp.float32) / jnp.sqrt(jnp.float32(H))
        bout = jnp.zeros((NLAYERS, 2 * H), jnp.float32)
        ln_scale = jnp.ones((NLAYERS, H), jnp.float32)
        ln_bias = jnp.zeros((NLAYERS, H), jnp.float32)
        return dict(x=x, log_dt=log_dt, Alog=Alog, Aim=Aim, Cre=Cre, Cim=Cim, D=D, Wout=Wout, bout=bout, ln_scale=ln_scale, ln_bias=ln_bias)
    _L1_attn_all = _L1_attn_setup()
    _L1_attn_in = {k: v for k, v in _L1_attn_all.items() if k in ('log_dt', 'Alog', 'Aim', 'Cre', 'Cim', 'D', 'Wout', 'bout', 'ln_scale', 'ln_bias')}
    del _L1_attn_all

    def _L1_ffn_setup():
        import jax, jax.numpy as jnp
        import numpy as np
        NUM_EXPERTS = 8
        TOP_K = 2
        B, S, D = (8, 2048, 64)

        def _moe(tokens, router_w, w1, b1, w2, b2):
            N = tokens.shape[0]
            E = router_w.shape[0]
            logits = tokens.astype(jnp.float32) @ router_w.astype(jnp.float32).T
            probs = jax.nn.softmax(logits, axis=-1)
            rw, re = jax.lax.top_k(probs, TOP_K)
            if TOP_K > 1:
                rw = rw / jnp.maximum(rw.sum(-1, keepdims=True), 1e-12)
            rw = rw.astype(tokens.dtype)
            combine = jnp.zeros((N, E), tokens.dtype).at[jnp.arange(N)[:, None], re].set(rw)
            out = tokens
            for e in range(E):
                h = jax.nn.gelu(tokens @ w1[e] + b1[e], approximate=False)
                y = h @ w2[e] + b2[e]
                out = out + combine[:, e:e + 1] * y
            return out
        key = jax.random.key(seed)
        ks = jax.random.split(key, 4)
        scale = 1.0 / np.sqrt(D).astype(np.float32)
        return {'input_embeddings': jax.random.normal(ks[0], (B, S, D), jnp.float32), 'router_w': jax.random.normal(ks[1], (NUM_EXPERTS, D), jnp.float32) * scale, 'w1': jax.random.normal(ks[2], (NUM_EXPERTS, D, D), jnp.float32) * scale, 'b1': jnp.zeros((NUM_EXPERTS, D), jnp.float32), 'w2': jax.random.normal(ks[3], (NUM_EXPERTS, D, D), jnp.float32) * scale, 'b2': jnp.zeros((NUM_EXPERTS, D), jnp.float32)}
    _L1_ffn_all = _L1_ffn_setup()
    _L1_ffn_in = {k: v for k, v in _L1_ffn_all.items() if k in ('router_w', 'w1', 'b1', 'w2', 'b2')}
    del _L1_ffn_all

    def _L2_attn_setup():
        import jax, jax.numpy as jnp
        import numpy as np
        import math
        B, L, D = (2, 2048, 64)
        DEPTH = 12
        FILT_ORDER = 64
        EMB_DIM = 3

        def _layernorm(x, g, b, eps=1e-05):
            m = x.mean(-1, keepdims=True)
            v = ((x - m) ** 2).mean(-1, keepdims=True)
            return (x - m) * jax.lax.rsqrt(v + eps) * g + b

        def _dwconv(x, w, pad):
            return jax.lax.conv_general_dilated(x, w, (1,), [pad], dimension_numbers=('NCH', 'OIH', 'NCH'), feature_group_count=x.shape[1])

        def _gelu(x):
            return jax.nn.gelu(x, approximate=False)

        def _fftconv(u, k, bias):
            l = u.shape[-1]
            n = 2 * l
            y = jnp.fft.irfft(jnp.fft.rfft(u, n=n) * jnp.fft.rfft(k, n=n), n=n)[..., :l]
            return y + u * bias[:, None]

        def _hyena_filter(l, mlp_w0, mlp_b0, mlp_w1, mlp_b1, mlp_w2, mlp_b2, mlp_w3, sin_freq):
            t01 = jnp.linspace(0.0, 1.0, l).astype(jnp.float32)
            tr = jnp.linspace(0.0, float(l - 1), l).astype(jnp.float32)
            ang = 2.0 * jnp.pi / l * tr * 0.0001
            z = jnp.stack([t01, jnp.cos(ang), -jnp.sin(ang)], axis=-1)
            h = jnp.sin((z @ mlp_w0.T + mlp_b0) * sin_freq)
            h = jnp.sin((h @ mlp_w1.T + mlp_b1) * sin_freq)
            h = jnp.sin((h @ mlp_w2.T + mlp_b2) * sin_freq)
            h = h @ mlp_w3.T
            max_decay = math.log(0.01) / 0.3
            min_decay = math.log(0.01) / 1.5
            deltas = jnp.linspace(min_decay, max_decay, h.shape[-1]).astype(jnp.float32)
            h = h * jnp.exp(-t01[:, None] * jnp.abs(deltas))
            return h.T
        key = jax.random.key(seed)
        ks = jax.random.split(key, 20)

        def n(k, shape, scale=0.02):
            return jax.random.normal(k, shape, dtype=jnp.float32) * scale
        return {'x': jax.random.normal(ks[0], (B, L, D), dtype=jnp.float32), 'ln_g': jnp.ones((D,), jnp.float32), 'ln_b': jnp.zeros((D,), jnp.float32), 'in_w': n(ks[1], (3 * D, D)), 'in_b': n(ks[2], (3 * D,)), 'sf_w': n(ks[3], (3 * D, 1, 3), 0.3), 'sf_b': n(ks[4], (3 * D,), 0.1), 'mlp_w0': n(ks[5], (FILT_ORDER, EMB_DIM), 0.3), 'mlp_b0': n(ks[6], (FILT_ORDER,), 0.3), 'mlp_w1': n(ks[7], (FILT_ORDER, FILT_ORDER), 0.1), 'mlp_b1': n(ks[8], (FILT_ORDER,), 0.1), 'mlp_w2': n(ks[9], (FILT_ORDER, FILT_ORDER), 0.1), 'mlp_b2': n(ks[10], (FILT_ORDER,), 0.1), 'mlp_w3': n(ks[11], (D, FILT_ORDER), 0.1), 'sin_freq': jnp.ones((FILT_ORDER,), jnp.float32), 'filt_bias': jax.random.normal(ks[12], (D,), dtype=jnp.float32), 'out_w': n(ks[13], (D, D)), 'out_b': n(ks[14], (D,)), 'conv_w': n(ks[15], (D, 1, 3))}
    _L2_attn_all = _L2_attn_setup()
    _L2_attn_in = {k: v for k, v in _L2_attn_all.items() if k in ('ln_g', 'ln_b', 'in_w', 'in_b', 'sf_w', 'sf_b', 'mlp_w0', 'mlp_b0', 'mlp_w1', 'mlp_b1', 'mlp_w2', 'mlp_b2', 'mlp_w3', 'sin_freq', 'filt_bias', 'out_w', 'out_b', 'conv_w')}
    del _L2_attn_all

    def _L2_ffn_setup():
        import jax, jax.numpy as jnp
        import numpy as np
        BN_EPS = 0.001

        def _bn(h, g, b, m, v):
            return g * (h - m) * jax.lax.rsqrt(v + BN_EPS) + b
        key = jax.random.key(seed)
        ks = jax.random.split(key, 8)
        B, F, Df = (64, 64, 64)
        E, H, D = (8, 64, 64)
        s1 = 1.0 / np.sqrt(Df)
        s2 = 1.0 / np.sqrt(H)
        return {'x': jax.random.normal(ks[0], (B, F, Df), jnp.float32), 'Wr': jax.random.normal(ks[1], (Df, E), jnp.float32) * s1, 'br': jnp.zeros((E,), jnp.float32), 'W1': jax.random.normal(ks[2], (E, Df, H), jnp.float32) * s1, 'b1': jnp.zeros((E, H), jnp.float32), 'g1': jnp.ones((E, H), jnp.float32), 'be1': jnp.zeros((E, H), jnp.float32), 'm1': jnp.zeros((E, H), jnp.float32), 'v1': jnp.ones((E, H), jnp.float32), 'W2': jax.random.normal(ks[3], (E, H, H), jnp.float32) * s2, 'b2': jnp.zeros((E, H), jnp.float32), 'g2': jnp.ones((E, H), jnp.float32), 'be2': jnp.zeros((E, H), jnp.float32), 'm2': jnp.zeros((E, H), jnp.float32), 'v2': jnp.ones((E, H), jnp.float32), 'Wo': jax.random.normal(ks[4], (E, H, D), jnp.float32) * s2, 'bo': jnp.zeros((E, D), jnp.float32)}
    _L2_ffn_all = _L2_ffn_setup()
    _L2_ffn_in = {k: v for k, v in _L2_ffn_all.items() if k in ('Wr', 'br', 'W1', 'b1', 'g1', 'be1', 'm1', 'v1', 'W2', 'b2', 'g2', 'be2', 'm2', 'v2', 'Wo', 'bo')}
    del _L2_ffn_all

    def _L3_attn_setup():
        import jax, jax.numpy as jnp
        import numpy as np
        S, B, D, H, DH = (128, 32, 64, 8, 32)
        LN_EPS = 1e-05

        def elu_p1(x):
            return jax.nn.elu(x) + 1.0

        def sum_norm(x):
            return x / jnp.sum(x, axis=-1, keepdims=True)

        def layer_norm(x, g, b):
            mu = jnp.mean(x, axis=-1, keepdims=True)
            var = jnp.mean(jnp.square(x - mu), axis=-1, keepdims=True)
            return (x - mu) * jax.lax.rsqrt(var + LN_EPS) * g + b

        def _fast_rnn_forward(x, slow_W, out_W, ln_g, ln_b):
            slen, bsz, _ = x.shape
            o = layer_norm(x, ln_g, ln_b)
            qkv = jnp.einsum('sbd,ed->sbe', o, slow_W)
            qkv = qkv.reshape(slen, bsz, H, 5 * DH + 2)
            q, k, v, rk, rv, beta, rbeta = jnp.split(qkv, [DH, 2 * DH, 3 * DH, 4 * DH, 5 * DH, 5 * DH + 1], axis=-1)
            beta = jax.nn.sigmoid(beta)
            rbeta = jax.nn.sigmoid(rbeta)
            q = sum_norm(elu_p1(q))
            k = sum_norm(elu_p1(k))
            rk = jax.nn.softmax(rk, axis=-1)

            def ff_step(W, inp):
                qt, kt, vt, bt = inp
                v_old = jnp.einsum('bhij,bhj->bhi', W, kt)
                W = W + (bt * (vt - v_old))[..., :, None] * kt[..., None, :]
                z = jnp.einsum('bhij,bhj->bhi', W, qt)
                return (W, z)
            W0 = jnp.zeros((bsz, H, DH, DH), x.dtype)
            _, z = jax.lax.scan(ff_step, W0, (q, k, v, beta))

            def rec_step(carry, inp):
                R, h = carry
                zt, kt, vt, bt = inp
                q_rec = jax.nn.softmax(h, axis=-1)
                v_old = jnp.einsum('bhij,bhj->bhi', R, kt)
                R = R + (bt * (vt - v_old))[..., :, None] * kt[..., None, :]
                h = zt + jnp.einsum('bhij,bhj->bhi', R, q_rec)
                return ((R, h), h)
            R0 = jnp.zeros((bsz, H, DH, DH), x.dtype)
            h0 = jnp.zeros((bsz, H, DH), x.dtype)
            _, hs = jax.lax.scan(rec_step, (R0, h0), (z, rk, rv, rbeta))
            out = hs.reshape(slen, bsz, H * DH)
            out = jnp.einsum('sbe,de->sbd', out, out_W)
            return x + out
        key = jax.random.key(seed)
        k1, k2, k3 = jax.random.split(key, 3)
        x = jax.random.normal(k1, (S, B, D), jnp.float32)
        slow_W = jax.random.normal(k2, (H * (5 * DH + 2), D), jnp.float32) * 0.02
        out_W = jax.random.normal(k3, (D, H * DH), jnp.float32) * 0.02
        ln_g = jnp.ones((D,), jnp.float32)
        ln_b = jnp.zeros((D,), jnp.float32)
        return {'x': x, 'slow_W': slow_W, 'out_W': out_W, 'ln_g': ln_g, 'ln_b': ln_b}
    _L3_attn_all = _L3_attn_setup()
    _L3_attn_in = {k: v for k, v in _L3_attn_all.items() if k in ('slow_W', 'out_W', 'ln_g', 'ln_b')}
    del _L3_attn_all

    def _L3_ffn_setup():
        import jax, jax.numpy as jnp
        import numpy as np
        E = 8
        K = 2
        D = 64
        H = 128
        DOUT = 64
        EPS = 1e-05
        key = jax.random.key(seed)
        ks = jax.random.split(key, 9)
        s = 0.02
        return {'x': jax.random.normal(ks[0], (4, 2048, D), jnp.float32), 'gamma': 1.0 + 0.05 * jax.random.normal(ks[1], (D,), jnp.float32), 'beta': 0.05 * jax.random.normal(ks[2], (D,), jnp.float32), 'Wr': 0.01 * jax.random.normal(ks[3], (D, E), jnp.float32), 'br': jnp.zeros((E,), jnp.float32), 'W1': s * jax.random.normal(ks[4], (E, D, H), jnp.float32), 'b1': s * jax.random.normal(ks[5], (E, H), jnp.float32), 'W2': s * jax.random.normal(ks[6], (E, H, DOUT), jnp.float32), 'b2': s * jax.random.normal(ks[7], (E, DOUT), jnp.float32)}
    _L3_ffn_all = _L3_ffn_setup()
    _L3_ffn_in = {k: v for k, v in _L3_ffn_all.items() if k in ('gamma', 'beta', 'Wr', 'br', 'W1', 'b1', 'W2', 'b2')}
    del _L3_ffn_all
    return {'x': x, 'L0_tok_W': _L0_tok_in['W'], 'L0_attn_Wq_comp': _L0_attn_in['Wq_comp'], 'L0_attn_Wkv_comp': _L0_attn_in['Wkv_comp'], 'L0_attn_Wqc': _L0_attn_in['Wqc'], 'L0_attn_Wqr': _L0_attn_in['Wqr'], 'L0_attn_Wkc': _L0_attn_in['Wkc'], 'L0_attn_Wkr': _L0_attn_in['Wkr'], 'L0_attn_Wv': _L0_attn_in['Wv'], 'L0_ffn_route_id': _L0_ffn_in['route_id'], 'L0_ffn_Wi': _L0_ffn_in['Wi'], 'L0_ffn_bi': _L0_ffn_in['bi'], 'L0_ffn_Wr': _L0_ffn_in['Wr'], 'L0_ffn_br': _L0_ffn_in['br'], 'L0_ffn_Ws': _L0_ffn_in['Ws'], 'L0_ffn_bs': _L0_ffn_in['bs'], 'L0_ffn_Wo': _L0_ffn_in['Wo'], 'L0_ffn_bo': _L0_ffn_in['bo'], 'L1_attn_log_dt': _L1_attn_in['log_dt'], 'L1_attn_Alog': _L1_attn_in['Alog'], 'L1_attn_Aim': _L1_attn_in['Aim'], 'L1_attn_Cre': _L1_attn_in['Cre'], 'L1_attn_Cim': _L1_attn_in['Cim'], 'L1_attn_D': _L1_attn_in['D'], 'L1_attn_Wout': _L1_attn_in['Wout'], 'L1_attn_bout': _L1_attn_in['bout'], 'L1_attn_ln_scale': _L1_attn_in['ln_scale'], 'L1_attn_ln_bias': _L1_attn_in['ln_bias'], 'L1_ffn_router_w': _L1_ffn_in['router_w'], 'L1_ffn_w1': _L1_ffn_in['w1'], 'L1_ffn_b1': _L1_ffn_in['b1'], 'L1_ffn_w2': _L1_ffn_in['w2'], 'L1_ffn_b2': _L1_ffn_in['b2'], 'L2_attn_ln_g': _L2_attn_in['ln_g'], 'L2_attn_ln_b': _L2_attn_in['ln_b'], 'L2_attn_in_w': _L2_attn_in['in_w'], 'L2_attn_in_b': _L2_attn_in['in_b'], 'L2_attn_sf_w': _L2_attn_in['sf_w'], 'L2_attn_sf_b': _L2_attn_in['sf_b'], 'L2_attn_mlp_w0': _L2_attn_in['mlp_w0'], 'L2_attn_mlp_b0': _L2_attn_in['mlp_b0'], 'L2_attn_mlp_w1': _L2_attn_in['mlp_w1'], 'L2_attn_mlp_b1': _L2_attn_in['mlp_b1'], 'L2_attn_mlp_w2': _L2_attn_in['mlp_w2'], 'L2_attn_mlp_b2': _L2_attn_in['mlp_b2'], 'L2_attn_mlp_w3': _L2_attn_in['mlp_w3'], 'L2_attn_sin_freq': _L2_attn_in['sin_freq'], 'L2_attn_filt_bias': _L2_attn_in['filt_bias'], 'L2_attn_out_w': _L2_attn_in['out_w'], 'L2_attn_out_b': _L2_attn_in['out_b'], 'L2_attn_conv_w': _L2_attn_in['conv_w'], 'L2_ffn_Wr': _L2_ffn_in['Wr'], 'L2_ffn_br': _L2_ffn_in['br'], 'L2_ffn_W1': _L2_ffn_in['W1'], 'L2_ffn_b1': _L2_ffn_in['b1'], 'L2_ffn_g1': _L2_ffn_in['g1'], 'L2_ffn_be1': _L2_ffn_in['be1'], 'L2_ffn_m1': _L2_ffn_in['m1'], 'L2_ffn_v1': _L2_ffn_in['v1'], 'L2_ffn_W2': _L2_ffn_in['W2'], 'L2_ffn_b2': _L2_ffn_in['b2'], 'L2_ffn_g2': _L2_ffn_in['g2'], 'L2_ffn_be2': _L2_ffn_in['be2'], 'L2_ffn_m2': _L2_ffn_in['m2'], 'L2_ffn_v2': _L2_ffn_in['v2'], 'L2_ffn_Wo': _L2_ffn_in['Wo'], 'L2_ffn_bo': _L2_ffn_in['bo'], 'L3_attn_slow_W': _L3_attn_in['slow_W'], 'L3_attn_out_W': _L3_attn_in['out_W'], 'L3_attn_ln_g': _L3_attn_in['ln_g'], 'L3_attn_ln_b': _L3_attn_in['ln_b'], 'L3_ffn_gamma': _L3_ffn_in['gamma'], 'L3_ffn_beta': _L3_ffn_in['beta'], 'L3_ffn_Wr': _L3_ffn_in['Wr'], 'L3_ffn_br': _L3_ffn_in['br'], 'L3_ffn_W1': _L3_ffn_in['W1'], 'L3_ffn_b1': _L3_ffn_in['b1'], 'L3_ffn_W2': _L3_ffn_in['W2'], 'L3_ffn_b2': _L3_ffn_in['b2']}

def reference(x, L0_tok_W, L0_attn_Wq_comp, L0_attn_Wkv_comp, L0_attn_Wqc, L0_attn_Wqr, L0_attn_Wkc, L0_attn_Wkr, L0_attn_Wv, L0_ffn_route_id, L0_ffn_Wi, L0_ffn_bi, L0_ffn_Wr, L0_ffn_br, L0_ffn_Ws, L0_ffn_bs, L0_ffn_Wo, L0_ffn_bo, L1_attn_log_dt, L1_attn_Alog, L1_attn_Aim, L1_attn_Cre, L1_attn_Cim, L1_attn_D, L1_attn_Wout, L1_attn_bout, L1_attn_ln_scale, L1_attn_ln_bias, L1_ffn_router_w, L1_ffn_w1, L1_ffn_b1, L1_ffn_w2, L1_ffn_b2, L2_attn_ln_g, L2_attn_ln_b, L2_attn_in_w, L2_attn_in_b, L2_attn_sf_w, L2_attn_sf_b, L2_attn_mlp_w0, L2_attn_mlp_b0, L2_attn_mlp_w1, L2_attn_mlp_b1, L2_attn_mlp_w2, L2_attn_mlp_b2, L2_attn_mlp_w3, L2_attn_sin_freq, L2_attn_filt_bias, L2_attn_out_w, L2_attn_out_b, L2_attn_conv_w, L2_ffn_Wr, L2_ffn_br, L2_ffn_W1, L2_ffn_b1, L2_ffn_g1, L2_ffn_be1, L2_ffn_m1, L2_ffn_v1, L2_ffn_W2, L2_ffn_b2, L2_ffn_g2, L2_ffn_be2, L2_ffn_m2, L2_ffn_v2, L2_ffn_Wo, L2_ffn_bo, L3_attn_slow_W, L3_attn_out_W, L3_attn_ln_g, L3_attn_ln_b, L3_ffn_gamma, L3_ffn_beta, L3_ffn_Wr, L3_ffn_br, L3_ffn_W1, L3_ffn_b1, L3_ffn_W2, L3_ffn_b2):
    import jax
    import jax.numpy as jnp

    def _L0_tok_ref(x, W):
        import jax, jax.numpy as jnp
        import numpy as np
        PATCH_LEN = 16
        STRIDE = 8
        PAD = 8
        B, C, T, V = x.shape
        xp = jnp.pad(x, ((0, 0), (0, 0), (0, PAD), (0, 0)), mode='edge')
        Tp = T + PAD
        N = (Tp - PATCH_LEN) // STRIDE + 1
        idx = jnp.arange(N)[:, None] * STRIDE + jnp.arange(PATCH_LEN)[None, :]
        patches = xp[:, :, idx, :]
        patches = jnp.transpose(patches, (0, 4, 2, 3, 1))
        xf = jnp.fft.rfft(patches, axis=-2, norm='ortho')
        F = xf.shape[-2]
        x_real = xf.real.reshape(B, V, N, F * C)
        x_imag = xf.imag.reshape(B, V, N, F * C)
        x_emb = jnp.concatenate([x_real, x_imag], axis=-1)
        x_emb = x_emb @ W.T
        return x_emb.reshape(B, V * N, -1)

    def _L0_attn_ref(x, Wq_comp, Wkv_comp, Wqc, Wqr, Wkc, Wkr, Wv):
        import jax, jax.numpy as jnp
        import numpy as np
        HEAD_SIZE = 64
        HEAD_SIZE_R = HEAD_SIZE // 4
        HEAD_SIZE_C = HEAD_SIZE - HEAD_SIZE_R
        N_EMBD = 64

        def rope(x, start_pos=0):
            B, T, d = x.shape
            half = d // 2
            theta = 1.0 / 10000.0 ** (jnp.arange(half, dtype=x.dtype) / half)
            idx = jnp.arange(start_pos, start_pos + T, dtype=x.dtype)[:, None] * theta[None, :]
            sin, cos = (jnp.sin(idx), jnp.cos(idx))
            xs = x.reshape(B, T, half, 2)
            x1, x2 = (xs[..., 0], xs[..., 1])
            rot = jnp.stack([x1 * cos - x2 * sin, x1 * sin + x2 * cos], axis=-1)
            return rot.reshape(B, T, d)

        def _reference_tuple_inner(x, Wq_comp, Wkv_comp, Wqc, Wqr, Wkc, Wkr, Wv):
            c_q = x @ Wq_comp
            c_kv = x @ Wkv_comp
            q_c = c_q @ Wqc
            q_r = rope(c_q @ Wqr, start_pos=0)
            q = jnp.concatenate([q_c, q_r], axis=-1)
            k_c = c_kv @ Wkc
            k_r = rope(c_kv @ Wkr, start_pos=0)
            k = jnp.concatenate([k_c, k_r], axis=-1)
            v = c_kv @ Wv
            scale = 1.0 / jnp.sqrt(jnp.asarray(HEAD_SIZE, dtype=x.dtype))
            wei = jnp.einsum('bqd,bkd->bqk', q, k) * scale
            T_q = q.shape[1]
            mask = jnp.tril(jnp.ones((T_q, T_q), dtype=bool))
            wei = jnp.where(mask, wei, jnp.asarray(-jnp.inf, dtype=wei.dtype))
            wei = jax.nn.softmax(wei, axis=-1)
            out = jnp.einsum('bqk,bkd->bqd', wei, v)
            return (out, (k, v))
        return _reference_tuple_inner(x, Wq_comp, Wkv_comp, Wqc, Wqr, Wkc, Wkr, Wv)[0]

    def _L0_ffn_ref(x, route_id, Wi, bi, Wr, br, Ws, bs, Wo, bo):
        import jax, jax.numpy as jnp
        import numpy as np
        B, T, IN_DIM = (64, 64, 64)
        HID, OUT_DIM = (128, 64)
        N_LAYERS, N_EXPERTS, N_SHARED = (2, 16, 1)
        flat = x.reshape(-1, x.shape[-1])
        n_tok = flat.shape[0]
        route = jnp.repeat(route_id, n_tok // route_id.shape[0])
        h = jax.nn.relu(flat @ Wi.T + bi)
        n_layers, n_experts = (Wr.shape[0], Wr.shape[1])
        for l in range(n_layers):
            shared = (jnp.einsum('nd,shd->snh', h, Ws[l]) + bs[l][:, None, :]).mean(axis=0)
            routed = jnp.zeros_like(h)
            for e in range(n_experts):
                ye = h @ Wr[l, e].T + br[l, e]
                routed = routed + jnp.where((route == e)[:, None], ye, 0.0)
            h = jax.nn.relu(shared + routed + h)
        out = h @ Wo.T + bo
        return out.reshape(*x.shape[:-1], out.shape[-1])

    def _L1_attn_ref(x, log_dt, Alog, Aim, Cre, Cim, D, Wout, bout, ln_scale, ln_bias):
        import jax, jax.numpy as jnp
        import numpy as np
        B, L, H, N, NLAYERS = (16, 512, 64, 64, 4)
        PRENORM = True

        def layer_norm(z, scale, bias, eps=1e-05):
            mu = jnp.mean(z, axis=-1, keepdims=True)
            var = jnp.var(z, axis=-1, keepdims=True)
            return (z - mu) * jax.lax.rsqrt(var + eps) * scale + bias

        def s4_block(u, log_dt, Alog, Aim, Cre, Cim, D, Wout, bout):
            Lq = u.shape[-1]
            dt = jnp.exp(log_dt)[:, None]
            A = -jnp.exp(Alog) + 1j * Aim
            C = Cre + 1j * Cim
            dtA = A * dt
            Cd = C * (jnp.exp(dtA) - 1.0) / A
            vand = jnp.exp(dtA[:, :, None] * jnp.arange(Lq))
            K = 2.0 * jnp.real(jnp.einsum('hn,hnl->hl', Cd, vand))
            n = 2 * Lq
            y = jnp.fft.irfft(jnp.fft.rfft(u, n=n) * jnp.fft.rfft(K, n=n), n=n)[..., :Lq]
            y = y + D[:, None] * u
            y = jax.nn.gelu(y)
            z = jnp.einsum('oh,bhl->bol', Wout, y) + bout[None, :, None]
            z1, z2 = jnp.split(z, 2, axis=1)
            return z1 * jax.nn.sigmoid(z2)
        h = jnp.swapaxes(x, -1, -2)
        for i in range(NLAYERS):
            z = h
            if PRENORM:
                z = jnp.swapaxes(layer_norm(jnp.swapaxes(z, -1, -2), ln_scale[i], ln_bias[i]), -1, -2)
            z = s4_block(z, log_dt[i], Alog[i], Aim[i], Cre[i], Cim[i], D[i], Wout[i], bout[i])
            h = z + h
            if not PRENORM:
                h = jnp.swapaxes(layer_norm(jnp.swapaxes(h, -1, -2), ln_scale[i], ln_bias[i]), -1, -2)
        return jnp.swapaxes(h, -1, -2)

    def _L1_ffn_ref(input_embeddings, router_w, w1, b1, w2, b2):
        import jax, jax.numpy as jnp
        import numpy as np
        NUM_EXPERTS = 8
        TOP_K = 2
        B, S, D = (8, 2048, 64)

        def _moe(tokens, router_w, w1, b1, w2, b2):
            N = tokens.shape[0]
            E = router_w.shape[0]
            logits = tokens.astype(jnp.float32) @ router_w.astype(jnp.float32).T
            probs = jax.nn.softmax(logits, axis=-1)
            rw, re = jax.lax.top_k(probs, TOP_K)
            if TOP_K > 1:
                rw = rw / jnp.maximum(rw.sum(-1, keepdims=True), 1e-12)
            rw = rw.astype(tokens.dtype)
            combine = jnp.zeros((N, E), tokens.dtype).at[jnp.arange(N)[:, None], re].set(rw)
            out = tokens
            for e in range(E):
                h = jax.nn.gelu(tokens @ w1[e] + b1[e], approximate=False)
                y = h @ w2[e] + b2[e]
                out = out + combine[:, e:e + 1] * y
            return out
        b, s, d = input_embeddings.shape
        tokens = input_embeddings.reshape(b * s, d)
        return _moe(tokens, router_w, w1, b1, w2, b2).reshape(b, s, d)

    def _L2_attn_ref(x, ln_g, ln_b, in_w, in_b, sf_w, sf_b, mlp_w0, mlp_b0, mlp_w1, mlp_b1, mlp_w2, mlp_b2, mlp_w3, sin_freq, filt_bias, out_w, out_b, conv_w):
        import jax, jax.numpy as jnp
        import numpy as np
        import math
        B, L, D = (2, 2048, 64)
        DEPTH = 12
        FILT_ORDER = 64
        EMB_DIM = 3

        def _layernorm(x, g, b, eps=1e-05):
            m = x.mean(-1, keepdims=True)
            v = ((x - m) ** 2).mean(-1, keepdims=True)
            return (x - m) * jax.lax.rsqrt(v + eps) * g + b

        def _dwconv(x, w, pad):
            return jax.lax.conv_general_dilated(x, w, (1,), [pad], dimension_numbers=('NCH', 'OIH', 'NCH'), feature_group_count=x.shape[1])

        def _gelu(x):
            return jax.nn.gelu(x, approximate=False)

        def _fftconv(u, k, bias):
            l = u.shape[-1]
            n = 2 * l
            y = jnp.fft.irfft(jnp.fft.rfft(u, n=n) * jnp.fft.rfft(k, n=n), n=n)[..., :l]
            return y + u * bias[:, None]

        def _hyena_filter(l, mlp_w0, mlp_b0, mlp_w1, mlp_b1, mlp_w2, mlp_b2, mlp_w3, sin_freq):
            t01 = jnp.linspace(0.0, 1.0, l).astype(jnp.float32)
            tr = jnp.linspace(0.0, float(l - 1), l).astype(jnp.float32)
            ang = 2.0 * jnp.pi / l * tr * 0.0001
            z = jnp.stack([t01, jnp.cos(ang), -jnp.sin(ang)], axis=-1)
            h = jnp.sin((z @ mlp_w0.T + mlp_b0) * sin_freq)
            h = jnp.sin((h @ mlp_w1.T + mlp_b1) * sin_freq)
            h = jnp.sin((h @ mlp_w2.T + mlp_b2) * sin_freq)
            h = h @ mlp_w3.T
            max_decay = math.log(0.01) / 0.3
            min_decay = math.log(0.01) / 1.5
            deltas = jnp.linspace(min_decay, max_decay, h.shape[-1]).astype(jnp.float32)
            h = h * jnp.exp(-t01[:, None] * jnp.abs(deltas))
            return h.T
        l = x.shape[1]
        d = x.shape[2]
        k = _hyena_filter(l, mlp_w0, mlp_b0, mlp_w1, mlp_b1, mlp_w2, mlp_b2, mlp_w3, sin_freq)

        def block(h):
            h = _layernorm(h, ln_g, ln_b)
            u = h @ in_w.T + in_b
            u = jnp.transpose(u, (0, 2, 1))
            uc = (_dwconv(u, sf_w, (2, 2)) + sf_b[None, :, None])[..., :l]
            x1, x2, v = (uc[:, :d], uc[:, d:2 * d], uc[:, 2 * d:])
            v = _fftconv(v * x2, k, filt_bias)
            y = jnp.transpose(v * x1, (0, 2, 1))
            y = y @ out_w.T + out_b
            y = jnp.transpose(y, (0, 2, 1))
            y = _gelu(_dwconv(y, conv_w, (1, 1)))
            y = jnp.transpose(y, (0, 2, 1))
            return _gelu(y)
        res = x
        for _ in range(DEPTH):
            x = block(x) + res
            res = x
        return x

    def _L2_ffn_ref(x, Wr, br, W1, b1, g1, be1, m1, v1, W2, b2, g2, be2, m2, v2, Wo, bo):
        import jax, jax.numpy as jnp
        import numpy as np
        BN_EPS = 0.001

        def _bn(h, g, b, m, v):
            return g * (h - m) * jax.lax.rsqrt(v + BN_EPS) + b
        feat = jnp.mean(x, axis=0)
        w = jax.nn.softmax(feat @ Wr + br, axis=-1)
        h = jnp.einsum('bfd,edh->bfeh', x, W1) + b1
        h = jax.nn.relu(_bn(h, g1, be1, m1, v1))
        h = jnp.einsum('bfeh,ehk->bfek', h, W2) + b2
        h = jax.nn.relu(_bn(h, g2, be2, m2, v2))
        y = jnp.einsum('bfeh,ehd->bfed', h, Wo) + bo
        return jnp.einsum('bfed,fe->bfd', y, w)

    def _L3_attn_ref(x, slow_W, out_W, ln_g, ln_b):
        import jax, jax.numpy as jnp
        import numpy as np
        S, B, D, H, DH = (128, 32, 64, 8, 32)
        LN_EPS = 1e-05

        def elu_p1(x):
            return jax.nn.elu(x) + 1.0

        def sum_norm(x):
            return x / jnp.sum(x, axis=-1, keepdims=True)

        def layer_norm(x, g, b):
            mu = jnp.mean(x, axis=-1, keepdims=True)
            var = jnp.mean(jnp.square(x - mu), axis=-1, keepdims=True)
            return (x - mu) * jax.lax.rsqrt(var + LN_EPS) * g + b

        def _fast_rnn_forward(x, slow_W, out_W, ln_g, ln_b):
            slen, bsz, _ = x.shape
            o = layer_norm(x, ln_g, ln_b)
            qkv = jnp.einsum('sbd,ed->sbe', o, slow_W)
            qkv = qkv.reshape(slen, bsz, H, 5 * DH + 2)
            q, k, v, rk, rv, beta, rbeta = jnp.split(qkv, [DH, 2 * DH, 3 * DH, 4 * DH, 5 * DH, 5 * DH + 1], axis=-1)
            beta = jax.nn.sigmoid(beta)
            rbeta = jax.nn.sigmoid(rbeta)
            q = sum_norm(elu_p1(q))
            k = sum_norm(elu_p1(k))
            rk = jax.nn.softmax(rk, axis=-1)

            def ff_step(W, inp):
                qt, kt, vt, bt = inp
                v_old = jnp.einsum('bhij,bhj->bhi', W, kt)
                W = W + (bt * (vt - v_old))[..., :, None] * kt[..., None, :]
                z = jnp.einsum('bhij,bhj->bhi', W, qt)
                return (W, z)
            W0 = jnp.zeros((bsz, H, DH, DH), x.dtype)
            _, z = jax.lax.scan(ff_step, W0, (q, k, v, beta))

            def rec_step(carry, inp):
                R, h = carry
                zt, kt, vt, bt = inp
                q_rec = jax.nn.softmax(h, axis=-1)
                v_old = jnp.einsum('bhij,bhj->bhi', R, kt)
                R = R + (bt * (vt - v_old))[..., :, None] * kt[..., None, :]
                h = zt + jnp.einsum('bhij,bhj->bhi', R, q_rec)
                return ((R, h), h)
            R0 = jnp.zeros((bsz, H, DH, DH), x.dtype)
            h0 = jnp.zeros((bsz, H, DH), x.dtype)
            _, hs = jax.lax.scan(rec_step, (R0, h0), (z, rk, rv, rbeta))
            out = hs.reshape(slen, bsz, H * DH)
            out = jnp.einsum('sbe,de->sbd', out, out_W)
            return x + out
        return _fast_rnn_forward(x, slow_W, out_W, ln_g, ln_b)

    def _L3_ffn_ref(x, gamma, beta, Wr, br, W1, b1, W2, b2):
        import jax, jax.numpy as jnp
        import numpy as np
        E = 8
        K = 2
        D = 64
        H = 128
        DOUT = 64
        EPS = 1e-05
        mu = jnp.mean(x, axis=-1, keepdims=True)
        var = jnp.mean(jnp.square(x - mu), axis=-1, keepdims=True)
        xn = (x - mu) * jax.lax.rsqrt(var + EPS) * gamma + beta
        logits = jnp.einsum('bsd,de->bse', xn, Wr) + br
        top_vals, top_idx = jax.lax.top_k(logits, K)
        w = jax.nn.softmax(top_vals, axis=-1)
        w_full = jnp.einsum('bsk,bske->bse', w, jax.nn.one_hot(top_idx, E, dtype=w.dtype))
        y = jnp.zeros(x.shape[:-1] + (DOUT,), x.dtype)
        for e in range(E):
            h = jax.nn.gelu(jnp.einsum('bsd,dh->bsh', xn, W1[e]) + b1[e], approximate=False)
            y_e = jnp.einsum('bsh,hd->bsd', h, W2[e]) + b2[e]
            y = y + y_e * w_full[..., e, None]
        return y
    h = _L0_tok_ref(x, L0_tok_W)
    h = _layernorm(h + _L0_attn_ref(h, L0_attn_Wq_comp, L0_attn_Wkv_comp, L0_attn_Wqc, L0_attn_Wqr, L0_attn_Wkc, L0_attn_Wkr, L0_attn_Wv), axis=-1)
    h = _layernorm(h + _L0_ffn_ref(h, L0_ffn_route_id, L0_ffn_Wi, L0_ffn_bi, L0_ffn_Wr, L0_ffn_br, L0_ffn_Ws, L0_ffn_bs, L0_ffn_Wo, L0_ffn_bo), axis=-1)
    h = _layernorm(h + _L1_attn_ref(h, L1_attn_log_dt, L1_attn_Alog, L1_attn_Aim, L1_attn_Cre, L1_attn_Cim, L1_attn_D, L1_attn_Wout, L1_attn_bout, L1_attn_ln_scale, L1_attn_ln_bias), axis=-1)
    h = _layernorm(h + _L1_ffn_ref(h, L1_ffn_router_w, L1_ffn_w1, L1_ffn_b1, L1_ffn_w2, L1_ffn_b2), axis=-1)
    h = _layernorm(h + _L2_attn_ref(h, L2_attn_ln_g, L2_attn_ln_b, L2_attn_in_w, L2_attn_in_b, L2_attn_sf_w, L2_attn_sf_b, L2_attn_mlp_w0, L2_attn_mlp_b0, L2_attn_mlp_w1, L2_attn_mlp_b1, L2_attn_mlp_w2, L2_attn_mlp_b2, L2_attn_mlp_w3, L2_attn_sin_freq, L2_attn_filt_bias, L2_attn_out_w, L2_attn_out_b, L2_attn_conv_w), axis=-1)
    h = _layernorm(h + _L2_ffn_ref(h, L2_ffn_Wr, L2_ffn_br, L2_ffn_W1, L2_ffn_b1, L2_ffn_g1, L2_ffn_be1, L2_ffn_m1, L2_ffn_v1, L2_ffn_W2, L2_ffn_b2, L2_ffn_g2, L2_ffn_be2, L2_ffn_m2, L2_ffn_v2, L2_ffn_Wo, L2_ffn_bo), axis=-1)
    h = _layernorm(h + _L3_attn_ref(h, L3_attn_slow_W, L3_attn_out_W, L3_attn_ln_g, L3_attn_ln_b), axis=-1)
    h = _layernorm(h + _L3_ffn_ref(h, L3_ffn_gamma, L3_ffn_beta, L3_ffn_Wr, L3_ffn_br, L3_ffn_W1, L3_ffn_b1, L3_ffn_W2, L3_ffn_b2), axis=-1)
    return h

_drawn_inputs = setup_inputs


def setup_inputs(seed=0):
    import zlib

    import numpy as np

    out = dict(_drawn_inputs(seed))
    spreads = {'L0_ffn_bi': (0.0, 0.1),
     'L0_ffn_bo': (0.0, 0.1),
     'L1_attn_Alog': (-0.6931471824645996, 0.2),
     'L1_attn_bout': (0.0, 0.1),
     'L1_attn_ln_scale': (1.0, 0.2),
     'L1_attn_ln_bias': (0.0, 0.1),
     'L1_ffn_b1': (0.0, 0.333),
     'L1_ffn_b2': (0.0, 0.1),
     'L2_attn_ln_g': (1.0, 0.6),
     'L2_attn_ln_b': (0.0, 0.8),
     'L2_attn_sin_freq': (1.0, 0.6),
     'L2_ffn_br': (0.0, 0.543),
     'L2_ffn_b1': (0.0, 0.354),
     'L2_ffn_g1': (1.0, 0.2),
     'L2_ffn_be1': (0.0, 0.437),
     'L2_ffn_m1': (0.0, 0.424),
     'L2_ffn_v1': (1.0, 0.6),
     'L2_ffn_b2': (0.0, 0.317),
     'L2_ffn_g2': (1.0, 0.2),
     'L2_ffn_be2': (0.0, 0.312),
     'L2_ffn_m2': (0.0, 0.291),
     'L2_ffn_v2': (1.0, 0.6),
     'L2_ffn_bo': (0.0, 0.1),
     'L3_attn_ln_g': (1.0, 0.6),
     'L3_attn_ln_b': (0.0, 0.8),
     'L3_ffn_br': (0.0, 0.431)}
    factors = {'L0_attn_Wq_comp': 8.0,
     'L0_attn_Wqc': 8.0,
     'L0_attn_Wqr': 8.0,
     'L0_attn_Wkc': 8.0,
     'L0_attn_Wkr': 8.0,
     'L0_ffn_Wr': 3.018,
     'L0_ffn_br': 3.994,
     'L0_ffn_Ws': 2.799,
     'L0_ffn_bs': 2.827,
     'L2_attn_in_w': 8.0,
     'L2_attn_in_b': 8.0,
     'L2_attn_sf_w': 8.0,
     'L2_attn_sf_b': 8.0,
     'L2_attn_mlp_w0': 8.0,
     'L2_attn_mlp_b0': 8.0,
     'L2_attn_mlp_w1': 8.0,
     'L2_attn_mlp_b1': 8.0,
     'L2_attn_mlp_w2': 8.0,
     'L2_attn_mlp_b2': 8.0,
     'L2_attn_mlp_w3': 8.0,
     'L2_attn_filt_bias': 8.0,
     'L2_attn_out_w': 8.0,
     'L2_attn_out_b': 8.0,
     'L2_attn_conv_w': 8.0,
     'L3_attn_slow_W': 8.0,
     'L3_attn_out_W': 8.0,
     'L3_ffn_gamma': 8.0,
     'L3_ffn_beta': 8.0,
     'L3_ffn_Wr': 5.02,
     'L3_ffn_W1': 4.403,
     'L3_ffn_b1': 8.0,
     'L3_ffn_W2': 4.326,
     'L3_ffn_b2': 4.148}
    for name, (base, spread) in spreads.items():
        noise = np.random.default_rng([zlib.crc32(name.encode()), seed]).standard_normal(out[name].shape)
        drawn = base * np.exp(spread * noise) if base else spread * noise
        out[name] = jnp.asarray(drawn.astype(out[name].dtype))
    for name, factor in factors.items():
        out[name] = (out[name] * factor).astype(out[name].dtype)
    return out
```

```python
from contextlib import ExitStack
import math
import numpy as np
import concourse.bass as bass
from concourse import mybir
from concourse.alu_op_type import AluOpType as ALU

F32 = mybir.dt.float32
I32 = mybir.dt.int32
ACT = mybir.ActivationFunctionType
AX = mybir.AxisListType.X

B, L, D = 8, 1024, 64
P = 128
NB = L // P
HALF = B // 2
W = B * D
EPS = 1e-5
NF = NB + 1
FORDER = [4, 0, 8, 2, 6, 1, 7, 5, 3]
SLOT = {0: 0, 8: 1, 4: 2, 2: 4, 6: 6, 1: 8, 5: 10, 7: 12, 3: 14}
REAL = (0, 8)
NEGATED = (4, 2, 1, 5)


def bcast(ap, axis, n):
    a = ap.unsqueeze(axis)
    shape = list(a.shape)
    shape[axis] = n
    return a.broadcast_to(shape)


def transform_constants():
    fwd, inv = np.zeros((P, 3 * NF, P)), np.zeros((P, 3 * NF, P))
    t, f2 = np.arange(P)[:, None], np.arange(P)[None, :]
    for f in range(NF):
        a = 2 * np.pi * ((t * (f + 2 * NB * f2)) % (2 * L)) / (2 * L)
        c, s = np.cos(a), np.sin(a)
        sign = -1.0 if f in NEGATED else 1.0
        fwd[:, 3 * f], fwd[:, 3 * f + 1], fwd[:, 3 * f + 2] = c, -s, (-c if sign < 0 else s)
        scale = (1.0 if f in REAL else 2.0) / (2 * L)
        inv[:, 3 * f], inv[:, 3 * f + 1], inv[:, 3 * f + 2] = c.T * scale, -s.T * scale, s.T * scale
    return fwd.reshape(P, -1).astype(np.float32), inv.reshape(P, -1).astype(np.float32)


class Pool2:

    def __init__(self, nc, ctx, size=19):
        self.nc = nc
        self.sets = [[ctx.enter_context(nc.semaphore(f"set{k}_{i}")) for i in range(size)] for k in range(2)]
        self.turn = 0
        self.tensors = 0

    def fresh(self):
        self.tensors += 1
        return self.tensors

    def open_loop(self):
        self.at = self.turn

    def even(self, nc):
        if self.turn != self.at:
            names, other = self.stage()
            with nc.Block(no_gpsimd_drain=True) as block:
                @block.sync
                def _(sync):
                    self.clear(sync, other)

    def stage(self):
        mine, other = self.sets[self.turn], self.sets[1 - self.turn]
        self.turn = 1 - self.turn
        return iter(mine), other

    def clear(self, sync, other):
        for s in other:
            sync.sem_clear(s)


class Steps:

    def __init__(self, eng, own):
        self.eng, self.own, self.n, self.counts = eng, own, 0, {}

    def do(self, ins):
        ins.then_inc(self.own, 1)
        self.n += 1
        self.eng.wait_ge(self.own, self.n)

    def go(self, ins):
        ins.then_inc(self.own, 1)
        self.n += 1

    def join(self):
        self.eng.wait_ge(self.own, self.n)

    def tell(self, ins, sem, key):
        ins.then_inc(sem, 1)
        self.counts[key] = self.counts.get(key, 0) + 1
        self.eng.wait_ge(sem, self.counts[key])



def fold_forward(v, st, U, S, T, w, fwd_ready):
    c8 = math.sqrt(0.5)

    def tt(out, a, b, op):
        return v.tensor_tensor(out, a, b, op)

    def fma(out, a, k, b):
        return v.scalar_tensor_tensor(out=out, in0=a, scalar=float(k), in1=b, op0=ALU.mult, op1=ALU.add)

    u, s, t = U[:, :, 0:w], S[:, :, 0:w], T[:, :, 0:w]
    st.go(tt(t[:, 0:4], u[:, 0:4], u[:, 4:8], ALU.add))
    st.do(tt(t[:, 4:8], u[:, 0:4], u[:, 4:8], ALU.subtract))
    st.go(tt(t[:, 8:10], t[:, 0:2], t[:, 2:4], ALU.add))
    st.tell(tt(s[:, 2:4], t[:, 0:2], t[:, 2:4], ALU.subtract), fwd_ready, "f")
    st.join()
    st.tell(tt(s[:, 0], t[:, 8], t[:, 9], ALU.add), fwd_ready, "f")
    st.tell(tt(s[:, 1], t[:, 8], t[:, 9], ALU.subtract), fwd_ready, "f")
    st.go(tt(t[:, 8], t[:, 5], t[:, 7], ALU.subtract))
    st.do(tt(t[:, 9], t[:, 5], t[:, 7], ALU.add))
    st.go(fma(s[:, 4], t[:, 8], c8, t[:, 4]))
    st.go(fma(s[:, 6], t[:, 8], -c8, t[:, 4]))
    st.join()
    st.tell(fma(s[:, 5], t[:, 9], c8, t[:, 6]), fwd_ready, "f")
    st.tell(fma(s[:, 7], t[:, 9], -c8, t[:, 6]), fwd_ready, "f")
    for j in range(1, 4):
        co, si = math.cos(math.pi * j / 8), math.sin(math.pi * j / 8)
        st.go(v.tensor_scalar(t[:, 8], u[:, 4 + j], -si, None, ALU.mult))
        st.do(v.tensor_scalar(t[:, 9], u[:, 4 + j], co, None, ALU.mult))
        st.go(fma(t[:, j], u[:, j], co, t[:, 8]))
        st.do(fma(t[:, 4 + j], u[:, j], si, t[:, 9]))
    st.do(tt(t[:, 8:10], u[:, 0:5:4], t[:, 2:7:4], ALU.add))
    st.do(tt(t[:, 2:7:4], u[:, 0:5:4], t[:, 2:7:4], ALU.subtract))
    st.do(tt(t[:, 10:12], t[:, 1:6:4], t[:, 3:8:4], ALU.add))
    st.do(tt(t[:, 3:8:4], t[:, 1:6:4], t[:, 3:8:4], ALU.subtract))
    st.tell(tt(s[:, 8:10], t[:, 8:10], t[:, 10:12], ALU.add), fwd_ready, "f")
    st.tell(tt(s[:, 12:14], t[:, 8:10], t[:, 10:12], ALU.subtract), fwd_ready, "f")
    st.go(tt(s[:, 10], t[:, 2], t[:, 7], ALU.subtract))
    st.join()
    st.tell(tt(s[:, 11], t[:, 6], t[:, 3], ALU.add), fwd_ready, "f")
    st.go(tt(s[:, 14], t[:, 2], t[:, 7], ALU.add))
    st.join()
    st.tell(tt(s[:, 15], t[:, 6], t[:, 3], ALU.subtract), fwd_ready, "f")


def unfold_inverse(v, st, U, S, T, need, done=None):
    c8 = math.sqrt(0.5)

    def tt(out, a, b, op):
        return v.tensor_tensor(out, a, b, op)

    def fma(out, a, k, b):
        return v.scalar_tensor_tensor(out=out, in0=a, scalar=float(k), in1=b, op0=ALU.mult, op1=ALU.add)

    need(5)
    st.go(tt(T[:, 0], S[:, 0], S[:, 1], ALU.add))
    st.go(tt(T[:, 1], S[:, 0], S[:, 1], ALU.subtract))
    st.go(tt(T[:, 6], S[:, 4], S[:, 6], ALU.subtract))
    st.go(tt(T[:, 7], S[:, 5], S[:, 7], ALU.add))
    st.go(tt(T[:, 8], S[:, 4], S[:, 6], ALU.add))
    st.do(tt(T[:, 9], S[:, 7], S[:, 5], ALU.subtract))
    st.go(tt(T[:, 2], T[:, 0], S[:, 2], ALU.add))
    st.go(tt(T[:, 4], T[:, 0], S[:, 2], ALU.subtract))
    st.go(tt(T[:, 3], T[:, 1], S[:, 3], ALU.subtract))
    st.go(tt(T[:, 5], T[:, 1], S[:, 3], ALU.add))
    st.go(tt(T[:, 10], T[:, 6], T[:, 7], ALU.subtract))
    st.do(tt(T[:, 11], T[:, 6], T[:, 7], ALU.add))
    st.go(tt(U[:, 0:3:2], T[:, 2:5:2], T[:, 8:10], ALU.add))
    st.go(tt(U[:, 4:7:2], T[:, 2:5:2], T[:, 8:10], ALU.subtract))
    st.go(fma(U[:, 1], T[:, 10], c8, T[:, 3]))
    st.go(fma(U[:, 5], T[:, 10], -c8, T[:, 3]))
    st.go(fma(U[:, 3], T[:, 11], -c8, T[:, 5]))
    st.do(fma(U[:, 7], T[:, 11], c8, T[:, 5]))
    need(9)
    st.go(tt(T[:, 0:2], S[:, 8:11:2], S[:, 12:15:2], ALU.add))
    st.go(tt(T[:, 2:4], S[:, 8:11:2], S[:, 12:15:2], ALU.subtract))
    st.go(tt(T[:, 4:6], S[:, 9:12:2], S[:, 13:16:2], ALU.subtract))
    st.do(tt(T[:, 6:8], S[:, 9:12:2], S[:, 13:16:2], ALU.add))
    st.go(tt(T[:, 8], T[:, 0], T[:, 1], ALU.add))
    st.go(tt(T[:, 9], T[:, 4], T[:, 5], ALU.add))
    st.go(tt(T[:, 10], T[:, 0], T[:, 1], ALU.subtract))
    st.do(tt(T[:, 11], T[:, 4], T[:, 5], ALU.subtract))
    st.go(tt(T[:, 0], T[:, 2], T[:, 7], ALU.subtract))
    st.go(tt(T[:, 1], T[:, 6], T[:, 3], ALU.add))
    st.go(tt(T[:, 4], T[:, 2], T[:, 7], ALU.add))
    st.do(tt(T[:, 5], T[:, 6], T[:, 3], ALU.subtract))
    st.go(tt(U[:, 0], U[:, 0], T[:, 8], ALU.add))
    st.go(tt(U[:, 4], U[:, 4], T[:, 9], ALU.subtract))
    rot = {1: (0, 1), 2: (10, 11), 3: (4, 5)}
    for part in (0, 1):
        for j, (re, im) in rot.items():
            co, si = math.cos(math.pi * j / 8), math.sin(math.pi * j / 8)
            if part == 0:
                st.go(fma(U[:, j], T[:, re], co, U[:, j]))
                st.go(fma(U[:, 4 + j], T[:, re], -si, U[:, 4 + j]))
            else:
                st.go(fma(U[:, j], T[:, im], -si, U[:, j]))
                st.go(fma(U[:, 4 + j], T[:, im], -co, U[:, 4 + j]))
        st.join()


def transform_residue(pe, M, f, S, w, out_re, out_im):
    c, ns, x = M[:, 3 * f], M[:, 3 * f + 1], M[:, 3 * f + 2]
    k = SLOT[f]
    if f in REAL:
        pe.matmul(out_re, c, S[:, k, 0:w], start=True, stop=True)
        return pe.matmul(out_im, ns, S[:, k, 0:w], start=True, stop=True)
    neg = f in NEGATED
    pe.matmul(out_re, c, S[:, k, 0:w], start=True, stop=False)
    pe.matmul(out_re, ns if neg else x, S[:, k + 1, 0:w], start=False, stop=True)
    pe.matmul(out_im, ns, S[:, k, 0:w], start=True, stop=False)
    return pe.matmul(out_im, x if neg else c, S[:, k + 1, 0:w], start=False, stop=True)


def inverse_residue(pe, M, f, Y, out_re, out_im):
    c, ns, s = M[:, 3 * f], M[:, 3 * f + 1], M[:, 3 * f + 2]
    yr, yi = Y[:, 0], Y[:, 1]
    pe.matmul(out_re, c, yr, start=True, stop=False)
    mm = pe.matmul(out_re, ns, yi, start=False, stop=True)
    if f not in REAL:
        pe.matmul(out_im, s, yr, start=True, stop=False)
        mm = pe.matmul(out_im, c, yi, start=False, stop=True)
    return mm


def stage_filter_spectrum(nc, pool, K, Kt, KH, S, T, M, ps):
    names, other = pool.stage()
    dve_step, fwd_ready, spec_ready, spec_out, act_step = (next(names) for _ in range(5))
    with nc.Block(no_gpsimd_drain=True) as block:
        @block.sync
        def _(sync):
            pool.clear(sync, other)

        @block.vector
        def _(v):
            fold_forward(v, Steps(v, dve_step), Kt, S, T, D, fwd_ready)

        @block.tensor
        def _(pe):
            for n, f in enumerate(FORDER):
                pe.wait_ge(fwd_ready, n + 1)
                if n >= 4:
                    pe.wait_ge(spec_out, 3 * (n - 3))
                b = ps[:, 2 * (n % 4):2 * (n % 4) + 2]
                transform_residue(pe, M, f, S, D, b[:, 0, 0:D], b[:, 1, 0:D]).then_inc(spec_ready, 1)

        @block.scalar
        def _(act):
            for n, f in enumerate(FORDER):
                act.wait_ge(spec_ready, n + 1)
                b = ps[:, 2 * (n % 4):2 * (n % 4) + 2]
                for k, part in enumerate((0, 1, 0)):
                    act.activation(KH[:, f, k, :], b[:, part, 0:D], ACT.Copy).then_inc(spec_out, 1)
            act.wait_ge(spec_out, 3 * NF)


def stage_long_conv(nc, pool, U, KH, S, T, MF, MI, ps):
    names, other = pool.stage()
    dve_step, fwd_ready, x_ready, y_ready, g_ready, g_out = (next(names) for _ in range(6))
    X = [ps[:, 0:2], ps[:, 2:4]]
    G = [ps[:, 4:6], ps[:, 6:8]]

    def product(n):
        f = FORDER[n]
        return T[:, 4 * (n % 3):4 * (n % 3) + 2] if f in REAL else S[:, SLOT[f]:SLOT[f] + 2]

    with nc.Block(no_gpsimd_drain=True) as block:
        @block.sync
        def _(sync):
            pool.clear(sync, other)

        @block.vector
        def _(v):
            st = Steps(v, dve_step)
            fold_forward(v, st, U, S, T, W, fwd_ready)
            for n, f in enumerate(FORDER):
                v.wait_ge(x_ready, n + 1)
                k = SLOT[f]
                t4 = T[:, 4 * (n % 3):4 * (n % 3) + 4].rearrange("p k (g d) -> p k g d", d=D)
                for part, (lo, hi) in enumerate(((0, 2), (1, 3))):
                    x = bcast(X[n % 2][:, part].rearrange("p (g d) -> p g d", d=D), 1, 2)
                    h = bcast(KH[:, f, lo:hi, :], 2, 8)
                    st.go(v.tensor_tensor(t4[:, 2 * part:2 * part + 2], x, h, ALU.mult))
                st.join()
                t = T[:, 4 * (n % 3):4 * (n % 3) + 4]
                y = product(n)
                st.go(v.tensor_tensor(y[:, 0], t[:, 0], t[:, 2], ALU.subtract))
                st.tell(v.tensor_tensor(y[:, 1], t[:, 1], t[:, 3], ALU.add), y_ready, "y")
                st.join()

            def need(n):
                v.wait_ge(g_out, sum(1 if f in REAL else 2 for f in FORDER[:n]))

            unfold_inverse(v, st, U, S, T, need)

        @block.tensor
        def _(pe):
            def inverse(n):
                f = FORDER[n]
                pe.wait_ge(y_ready, n + 1)
                if n >= 2:
                    pe.wait_ge(g_out, sum(1 if g in REAL else 2 for g in FORDER[:n - 1]))
                y, g = product(n), G[n % 2]
                inverse_residue(pe, MI, f, y, g[:, 0], g[:, 1]).then_inc(g_ready, 1)

            for n, f in enumerate(FORDER):
                pe.wait_ge(fwd_ready, n + 1)
                if n >= 2:
                    pe.wait_ge(y_ready, n - 1)
                x = X[n % 2]
                transform_residue(pe, MF, f, S, W, x[:, 0], x[:, 1]).then_inc(x_ready, 1)
                if n >= 1:
                    inverse(n - 1)
            inverse(NF - 1)

        @block.scalar
        def _(act):
            for n, f in enumerate(FORDER):
                act.wait_ge(g_ready, n + 1)
                for part in range(1 if f in REAL else 2):
                    act.activation(S[:, SLOT[f] + part], G[n % 2][:, part], ACT.Copy).then_inc(g_out, 1)
            act.wait_ge(g_out, 2 * NB)



def load(sync, sem, pairs):
    for dst, src in pairs:
        sync.dma_start(dst, src).then_inc(sem, 16)
    return 16 * len(pairs)


def stage_load(nc, pool, pairs):
    names, other = pool.stage()
    loaded = next(names)
    with nc.Block(no_gpsimd_drain=True) as block:
        @block.sync
        def _(sync):
            pool.clear(sync, other)
            n = load(sync, loaded, pairs)
            sync.wait_ge(loaded, n)


def stage_layernorm(nc, pool, src, dst, stats, T, add=None, gain=None, bias=None, src_scale=None):
    names, other = pool.stage()
    dve_step, centred, squared, var_ready, std_ready = (next(names) for _ in range(5))
    G = NB * B
    HB = NB // 2
    mean, var = stats[:, 0:G], stats[:, G:2 * G]

    def part(t, k):
        return t[:, HB * k:HB * (k + 1)].rearrange("p j (g d) -> p (j g) d", d=D)

    with nc.Block(no_gpsimd_drain=True) as block:
        @block.sync
        def _(sync):
            pool.clear(sync, other)

        @block.vector
        def _(v):
            st = Steps(v, dve_step)
            g = G // 2
            for k in range(2):
                x, y, m = part(src, k), part(dst, k), mean[:, g * k:g * (k + 1)]
                if add is not None:
                    st.do(v.scalar_tensor_tensor(out=dst[:, HB * k:HB * (k + 1)], in0=src[:, HB * k:HB * (k + 1)],
                                                 scalar=1.0 if src_scale is None else src_scale,
                                                 in1=add[:, HB * k:HB * (k + 1)], op0=ALU.mult, op1=ALU.add))
                    x = y
                st.do(v.tensor_reduce(m, x, AX, ALU.add))
                st.do(v.tensor_scalar(m, m, 1.0 / D, None, ALU.mult))
                st.tell(v.tensor_tensor(y, x, bcast(m, 2, D), ALU.subtract), centred, "c")
            for k in range(2):
                s = var[:, g * k:g * (k + 1)]
                v.wait_ge(squared, k + 1)
                st.do(v.tensor_reduce(s, part(T, k), AX, ALU.add))
                st.tell(v.tensor_scalar(s, s, 1.0 / D, EPS, ALU.mult, ALU.add), var_ready, "v")
            for k in range(2):
                y, s = part(dst, k), var[:, g * k:g * (k + 1)]
                v.wait_ge(std_ready, k + 1)
                st.do(v.reciprocal(s, s))
                st.do(v.tensor_tensor(y, y, bcast(s, 2, D), ALU.mult))
                if gain is not None:
                    st.do(v.tensor_tensor(y, y, bcast(gain, 1, g), ALU.mult))
                    st.do(v.tensor_tensor(y, y, bcast(bias, 1, g), ALU.add))

        @block.scalar
        def _(act):
            g = G // 2
            for k in range(2):
                act.wait_ge(centred, k + 1)
                act.activation(part(T, k), part(dst, k), ACT.Square).then_inc(squared, 1)
            for k in range(2):
                act.wait_ge(var_ready, k + 1)
                s = var[:, g * k:g * (k + 1)]
                act.activation(s, s, ACT.Sqrt).then_inc(std_ready, 1)
            act.wait_ge(std_ready, 2)


def stage_to_features(nc, pool, X, XF, ident, ps, gain=None, bias=None, pre=None):
    names, other = pool.stage()
    turned, copied = next(names), next(names)
    with nc.Block(no_gpsimd_drain=True) as block:
        @block.sync
        def _(sync):
            pool.clear(sync, other)

        @block.tensor
        def _(pe):
            turn_blocks(pe, X, ident, ps, turned, copied)

        @block.scalar
        def _(act):
            copy_blocks(act, XF, ps, turned, copied, gain, bias)
            act.wait_ge(copied, NB)


def turn_blocks(pe, X, ident, ps, turned, copied, ready=None):
    for j in range(NB):
        if ready is not None:
            pe.wait_ge(ready, j + 1)
        if j >= 4:
            pe.wait_ge(copied, j - 3)
        for b4 in range(HALF):
            mm = pe.transpose(ps[:, j % 4, P * b4:P * (b4 + 1)], X[:, j, P * b4:P * (b4 + 1)], ident)
        mm.then_inc(turned, 1)


def copy_blocks(act, XF, ps, turned, copied, gain=None, bias=None):
    for j in range(NB):
        act.wait_ge(turned, j + 1)
        out = XF[:, :, PAD + P * j:PAD + P * (j + 1)]
        src = ps[:, j % 4].rearrange("p (b t) -> p b t", b=HALF)
        if gain is None:
            act.activation(out, src, ACT.Copy).then_inc(copied, 1)
        else:
            act.activation(out, src, ACT.Identity, bias=bias, scale=gain).then_inc(copied, 1)


PAD = 2
LF = PAD + L + 2



def stage_patches(nc, pool, K, H, x, ps):
    NT, TH, STEP, PATCH = 64, 72, 8, 16
    with ExitStack() as ctx:
        wt = ctx.enter_context(nc.sbuf_tensor("tok_wt", [2 * (PATCH // 2 + 1), D, 2 * D], F32))
        dft = ctx.enter_context(nc.sbuf_tensor("tok_dft", [2 * (PATCH // 2 + 1), PATCH], F32))
        w = ctx.enter_context(nc.sbuf_tensor("tok_w", [P, PATCH, P], F32))
        xt = ctx.enter_context(nc.sbuf_tensor("tok_x", [P, 2, TH, NT], F32))
        E = ctx.enter_context(nc.sbuf_tensor("tok_e", [P, 2, NT, PATCH], F32))
        names, other = pool.stage()
        w_in, zeroed, w_made, w_out = (next(names) for _ in range(4))
        with nc.Block(no_gpsimd_drain=True) as block:
            @block.sync
            def _(sync):
                pool.clear(sync, other)
                load(sync, w_in, [(wt[:, :, :], K["tok_W"]), (dft[:, :], K["tok_dft"])])

            @block.gpsimd
            def _(g):
                g.memset(E[:, :, :, :], 0.0)
                g.memset(w[:, :, :], 0.0).then_inc(zeroed, 1)
                g.wait_ge(zeroed, 1)

            @block.tensor
            def _(pe):
                pe.wait_ge(w_in, 32)
                for o in range(D):
                    mm = pe.matmul(ps[:, o // 32, PATCH * (o % 32):PATCH * (o % 32 + 1)], wt[:, o, :], dft[:, :],
                                   start=True, stop=True)
                mm.then_inc(w_made, 1)

            @block.scalar
            def _(act):
                act.wait_ge(w_made, 1)
                act.wait_ge(zeroed, 1)
                for k in range(2):
                    h = slice(D * k, D * (k + 1))
                    for q in range(2):
                        src = ps[h, q].rearrange("p (o t) -> p t o", t=PATCH)
                        act.activation(w[h, :, D * k + 32 * q:D * k + 32 * (q + 1)], src,
                                       ACT.Copy).then_inc(w_out, 1)
                act.wait_ge(w_out, 4)

        names, other = pool.stage()
        x_free, padded, summed, e_ready, row_ready, row_free = (next(names) for _ in range(6))
        x_in = [next(names), next(names)]
        with nc.Block(no_gpsimd_drain=True) as block:
            @block.sync
            def _(sync):
                pool.clear(sync, other)
                with sync.Fori(0, HALF) as i:
                    for h in range(2):
                        sync.wait_ge(x_free, 2 * i + h + 1)
                        b = x[bass.ds(i + HALF * h, 1)].rearrange("o c t v -> (o c) t v")
                        sync.dma_start(xt[0:D, h], b[:, 0:TH]).then_inc(x_in[h], 16)
                        sync.dma_start(xt[D:P, h, 0:64], b[:, 64:128]).then_inc(x_in[h], 16)

            @block.tensor
            def _(pe):
                pe.sem_inc(x_free, 2)
                with pe.Fori(0, HALF) as i:
                    for h in range(2):
                        pe.wait_ge(padded, 2 * i + h + 1)
                        for p in range(PATCH):
                            rhs = xt[:, h, p:p + STEP * 7 + 1:STEP, :]
                            mm = pe.matmul(ps[:, h], w[:, p, :], rhs, start=(p == 0), stop=(p == PATCH - 1))
                        mm.then_inc(summed, 1)
                        pe.wait_ge(e_ready, 2 * i + h + 1)
                        pe.wait_ge(row_free, 2 * i + h + 1)
                        for j in range(NB):
                            mm = pe.matmul(ps[:, 2 + h, D * j:D * (j + 1)],
                                           E[:, h, 8 * j:8 * (j + 1), :], K["fold_halves"],
                                           start=True, stop=True)
                        mm.then_inc(row_ready, 1)

            @block.scalar
            def _(act):
                with act.Fori(0, HALF) as i:
                    for h in range(2):
                        act.wait_ge(summed, 2 * i + h + 1)
                        for k in range(2):
                            q = slice(D * k, D * (k + 1))
                            src = ps[q, h].rearrange("p (n v) -> p v n", v=NT)
                            act.activation(E[q, h, :, 8 * k:8 * (k + 1)], src, ACT.Copy).then_inc(
                                x_free if k == 0 else e_ready, 1)

            @block.vector
            def _(v):
                v.sem_inc(row_free, 2)
                with v.Fori(0, HALF) as i:
                    for h in range(2):
                        v.wait_ge(x_in[h], 32 * i + 32)
                        v.tensor_copy(xt[D:P, h, 64:TH], bcast(xt[D:P, h, 63, :], 1, STEP)).then_inc(padded, 1)
                        v.wait_ge(row_ready, 2 * i + h + 1)
                        v.tensor_copy(H[:, :, bass.ds(P * i + D * h, D)],
                                      ps[:, 2 + h].rearrange("p (j d) -> p j d", d=D)).then_inc(row_free, 1)
                v.wait_ge(row_free, 2 + 2 * HALF)


def stage_zero_pads(nc, pool, XF):
    names, other = pool.stage()
    zeroed = next(names)
    with nc.Block(no_gpsimd_drain=True) as block:
        @block.sync
        def _(sync):
            pool.clear(sync, other)

        @block.vector
        def _(v):
            v.memset(XF[:, :, 0:PAD], 0.0).then_inc(zeroed, 1)
            v.memset(XF[:, :, PAD + L:LF], 0.0).then_inc(zeroed, 1)
            v.wait_ge(zeroed, 2)



def stage_attention(nc, pool, K, H, ps):
    NEG = -1e30
    ident = K["ident"]
    with ExitStack() as ctx:
        def sb(name, shape):
            return ctx.enter_context(nc.sbuf_tensor(name, shape, F32))

        wl = sb("at_wl", [P, 2, P])
        wr = sb("at_wr", [P, 5, P])
        wp = sb("at_wp", [P, 5, P])
        rope = sb("at_rope", [P, 2, L])
        mask = sb("at_mask", [P, P])
        Hb, Xb = sb("at_hb", [P, NB, P]), sb("at_xb", [P, L])
        QZ, Kb, Vb = sb("at_qz", [P, 2, L]), sb("at_k", [P, L]), sb("at_v", [P, NB, P])
        tmp = sb("at_tmp", [P, 2, 512])
        Pr, Pt = sb("at_p", [P, 2, L]), sb("at_pt", [P, 2, L])
        nmax, rsum = sb("at_nmax", [P, 16]), sb("at_rsum", [P, 16])

        names, other = pool.stage()
        w_in, w_made, w_out, zeroed = (next(names) for _ in range(4))
        with nc.Block(no_gpsimd_drain=True) as block:
            @block.sync
            def _(sync):
                pool.clear(sync, other)
                load(sync, w_in, [(wl[:, :, :], K["at_wl"]), (wr[:, :, :], K["at_wr"]),
                                  (rope[:, :, :], K["at_rope"]), (mask[:, :], K["at_mask"])])
                sync.wait_ge(w_in, 64)

            @block.gpsimd
            def _(g):
                g.memset(QZ[:, :, :], 0.0).then_inc(zeroed, 1)
                g.wait_ge(zeroed, 1)

            @block.tensor
            def _(pe):
                pe.wait_ge(w_in, 64)
                for n in range(5):
                    mm = pe.matmul(ps[:, n // 4, P * (n % 4):P * (n % 4 + 1)], wl[:, 0 if n < 2 else 1, :],
                                   wr[:, n, :], start=True, stop=True)
                mm.then_inc(w_made, 1)

            @block.scalar
            def _(act):
                act.wait_ge(w_made, 1)
                act.activation(wp[:, 0:4, :].rearrange("p a b -> p (a b)"), ps[:, 0, :], ACT.Copy).then_inc(w_out, 1)
                act.activation(wp[:, 4, :], ps[:, 1, 0:P], ACT.Copy).then_inc(w_out, 1)
                act.wait_ge(w_out, 2)

        with nc.Fori(0, HALF) as b4:
            names, other = pool.stage()
            taken, turned, x_ready, roped, proj, v_made, v_ready, q_step = (next(names) for _ in range(8))
            with nc.Block(no_gpsimd_drain=True) as block:
                @block.sync
                def _(sync):
                    pool.clear(sync, other)

                @block.scalar
                def _(act):
                    act.activation(Hb[:, :, :], H[:, :, bass.ds(P * b4, P)], ACT.Copy).then_inc(taken, 1)
                    for k in range(2):
                        act.wait_ge(turned, k + 1)
                        act.activation(Xb[:, 512 * k:512 * (k + 1)], ps[:, k], ACT.Copy).then_inc(x_ready, 1)
                    for k in range(2):
                        act.wait_ge(v_made, k + 1)
                        act.activation(Vb[:, 4 * k:4 * (k + 1), :].rearrange("p a b -> p (a b)"), ps[:, k],
                                       ACT.Copy).then_inc(v_ready, 1)
                    act.wait_ge(v_ready, 2)

                @block.tensor
                def _(pe):
                    pe.wait_ge(taken, 1)
                    for j in range(NB):
                        mm = pe.transpose(ps[:, j // 4, P * (j % 4):P * (j % 4 + 1)], Hb[:, j, :], ident)
                        if j % 4 == 3:
                            mm.then_inc(turned, 1)
                    pe.wait_ge(x_ready, 2)
                    for j in range(NB):
                        mm = pe.matmul(ps[:, j // 4, P * (j % 4):P * (j % 4 + 1)], Xb[:, P * j:P * (j + 1)],
                                       wp[:, 4, :], start=True, stop=True)
                        if j % 4 == 3:
                            mm.then_inc(v_made, 1)
                    for n in range(4):
                        c, w = n % 2, 2 * (n // 2)
                        if n >= 2:
                            pe.wait_ge(roped, n - 1)
                        for s in range(2):
                            mm = pe.matmul(ps[:, 2 + 2 * c + s], wp[:, w + s, :], Xb[:, 512 * c:512 * (c + 1)],
                                           start=True, stop=True)
                        mm.then_inc(proj, 1)

                @block.vector
                def _(v):
                    st = Steps(v, q_step)
                    for n in range(4):
                        c, cols = n % 2, slice(512 * (n % 2), 512 * (n % 2 + 1))
                        v.wait_ge(proj, n + 1)
                        st.go(v.tensor_tensor(tmp[:, 0], ps[:, 2 + 2 * c], rope[:, 0, cols], ALU.mult))
                        st.do(v.tensor_tensor(tmp[:, 1], ps[:, 3 + 2 * c], rope[:, 1, cols], ALU.mult))
                        if n < 2:
                            st.go(v.tensor_tensor(QZ[0:D, 0, cols], tmp[0:D, 0], tmp[0:D, 1], ALU.add))
                            st.tell(v.tensor_tensor(QZ[D:P, 1, cols], tmp[D:P, 0], tmp[D:P, 1], ALU.add),
                                      roped, "r")
                        else:
                            st.tell(v.tensor_tensor(Kb[:, cols], tmp[:, 0], tmp[:, 1], ALU.add), roped, "r")
                        st.join()

            names, other = pool.stage()
            scored, maxed, exped, p_turned, pt_out, pt_act, p_read, pv, o_read, m_step = (
                next(names) for _ in range(10))
            tiles = [(q, h) for q in range(NB) for h in range(2)]
            banks = [q // 4 + 1 for q, _ in tiles]
            before = [sum(banks[:n]) for n in range(len(tiles) + 1)]
            S = [ps[:, 0:2], ps[:, 2:4]]
            with nc.Block(no_gpsimd_drain=True) as block:
                @block.sync
                def _(sync):
                    pool.clear(sync, other)

                @block.tensor
                def _(pe):
                    def scores(n):
                        q, h = tiles[n]
                        keys = P * (q + 1)
                        if n >= 2:
                            pe.wait_ge(exped, n - 1)
                        d = keys - P
                        qz = QZ[:, h, P * q:P * (q + 1)]
                        for lo in range(0, d, 512):
                            hi = min(d, lo + 512)
                            pe.matmul(S[n % 2][:, lo // 512, 0:hi - lo], qz, Kb[:, lo:hi], start=True, stop=True)
                        out = S[n % 2][:, d // 512, d % 512:d % 512 + P]
                        pe.matmul(out, qz, Kb[:, d:keys], start=True, stop=False)
                        mm = pe.matmul(out, ident, mask[:, :], start=False, stop=True)
                        mm.then_inc(scored, 1)

                    def output(n):
                        q, h = tiles[n]
                        pe.wait_ge(exped, n + 1)
                        for c in range(banks[n]):
                            k = before[n] + c
                            if k >= 2:
                                pe.wait_ge(pt_out, k - 1)
                            for b in range(4 * c, min(4 * c + 4, q + 1)):
                                mm = pe.transpose(ps[:, 4 + k % 2, P * (b % 4):P * (b % 4 + 1)],
                                                  Pr[:, n % 2, P * b:P * (b + 1)], ident)
                            mm.then_inc(p_turned, 1)
                        pe.wait_ge(pt_out, before[n + 1])
                        if n >= 2:
                            pe.wait_ge(o_read, n - 1)
                        for b in range(q + 1):
                            mm = pe.matmul(ps[:, 6 + n % 2, 0:P], Pt[:, n % 2, P * b:P * (b + 1)], Vb[:, b, :],
                                           start=(b == 0), stop=(b == q))
                        mm.then_inc(pv, 1)

                    scores(0)
                    for n in range(len(tiles)):
                        if n + 1 < len(tiles):
                            scores(n + 1)
                        output(n)

                @block.scalar
                def _(act):
                    for n, (q, h) in enumerate(tiles):
                        act.wait_ge(maxed, n + 1)
                        if n >= 2:
                            act.wait_ge(p_turned, before[n - 1])
                        src = S[n % 2].rearrange("p a b -> p (a b)")[:, 0:P * (q + 1)]
                        act.activation(Pr[:, n % 2, 0:P * (q + 1)], src, ACT.Exp, bias=nmax[:, n:n + 1],
                                       scale=1 / math.sqrt(D), accum_out=rsum[:, n:n + 1]).then_inc(exped, 1)

                @block.vector
                def _(v):
                    st = Steps(v, m_step)

                    def top(n):
                        q, h = tiles[n]
                        v.wait_ge(scored, n + 1)
                        src = S[n % 2].rearrange("p a b -> p (a b)")[:, 0:P * (q + 1)]
                        st.do(v.tensor_reduce(nmax[:, n:n + 1], src, AX, ALU.max))
                        st.tell(v.tensor_scalar(nmax[:, n:n + 1], nmax[:, n:n + 1], -1 / math.sqrt(D), None,
                                                  ALU.mult), maxed, "m")

                    def copy(n):
                        q, h = tiles[n]
                        for c in range(banks[n]):
                            k = before[n] + c
                            v.wait_ge(p_turned, k + 1)
                            if c == 0 and n >= 2:
                                v.wait_ge(pv, n - 1)
                            w = P * (min(4 * c + 4, q + 1) - 4 * c)
                            st.tell(v.tensor_copy(Pt[:, n % 2, 512 * c:512 * c + w], ps[:, 4 + k % 2, 0:w]),
                                      pt_out, "p")

                    def finish(n):
                        q, h = tiles[n]
                        v.wait_ge(exped, n + 1)
                        st.do(v.reciprocal(rsum[:, n:n + 1], rsum[:, n:n + 1]))
                        v.wait_ge(pv, n + 1)
                        o = H[:, q, bass.ds(P * b4 + D * h, D)]
                        st.tell(v.scalar_tensor_tensor(out=o, in0=ps[:, 6 + n % 2, D * h:D * (h + 1)],
                                                         scalar=rsum[:, n:n + 1], in1=Hb[:, q, D * h:D * (h + 1)],
                                                         op0=ALU.mult, op1=ALU.add), o_read, "o")

                    top(0)
                    for n in range(len(tiles)):
                        if n + 1 < len(tiles):
                            top(n + 1)
                        copy(n)
                        if n >= 1:
                            finish(n - 1)
                    finish(len(tiles) - 1)



def stage_routed(nc, pool, K, H, XF, ps):
    HID, EXPERTS, NL = 128, 16, 2
    GROUPS = 2 * NB
    wr_dram = K["f0_wr"]
    with ExitStack() as ctx:
        def sb(name, shape, dt=F32):
            return ctx.enter_context(nc.sbuf_tensor(name, shape, dt))

        ri, rf, rm = sb("f0_ri", [1, 64], I32), sb("f0_rf", [1, 64]), sb("f0_rm", [1, 2, 64])
        wi = sb("f0_wi", [P, 2, HID])
        ws, wo = sb("f0_ws", [P, NL, HID]), sb("f0_wo", [P, D])
        bi, bs, bo = sb("f0_bi", [P, 1]), sb("f0_bs", [P, NL]), sb("f0_bo", [P, D])
        wr = sb("f0_wrs", [P, NL, GROUPS, HID + 1])
        bias = sb("f0_bias", [P, NL, GROUPS])
        h0, h1 = sb("f0_h0", [P, GROUPS, P]), sb("f0_h1", [P, GROUPS, P])

        names, other = pool.stage()
        w_in, r_step, routes = (next(names) for _ in range(3))
        with nc.Block(no_gpsimd_drain=True) as block:
            @block.sync
            def _(sync):
                pool.clear(sync, other)
                load(sync, w_in, [(ri[:, :], K["f0_route"]), (wi[:, :, :], K["f0_wi"]), (ws[:, :, :], K["f0_ws"]),
                                  (wo[:, :], K["f0_wo"]), (bi[:, :], K["f0_bi"]), (bs[:, :], K["f0_bs"]),
                                  (bo[:, :], K["f0_bo"].partition_broadcast(P))])
                sync.wait_ge(w_in, 7 * 16)

            @block.vector
            def _(v):
                st = Steps(v, r_step)
                v.wait_ge(w_in, 7 * 16)
                st.do(v.tensor_copy(rf[:, :], ri[:, :]))
                st.go(v.tensor_scalar(rm[:, 0], rf[:, :], 0.0, None, ALU.is_ge))
                st.do(v.tensor_scalar(rm[:, 1], rf[:, :], float(EXPERTS - 1), None, ALU.is_le))
                st.go(v.tensor_tensor(rm[:, 0], rm[:, 0], rm[:, 1], ALU.mult))
                st.do(v.tensor_scalar(rf[:, :], rf[:, :], -float(EXPERTS), None, ALU.add))
                st.do(v.tensor_tensor(rf[:, :], rf[:, :], rm[:, 0], ALU.mult))
                st.do(v.tensor_scalar(rf[:, :], rf[:, :], float(EXPERTS), None, ALU.add))
                st.do(v.tensor_copy(ri[:, :], rf[:, :]))
                for l in range(NL):
                    st.do(v.tensor_tensor(ws[:, l, :], ws[:, l, :], K["ident"], ALU.add))

        with nc.Fori(0, HALF) as b4:
            names, other = pool.stage()
            r_in = [next(names) for _ in range(NL)]
            with nc.Block(no_gpsimd_drain=True) as block:
                @block.sync
                def _(sync):
                    pool.clear(sync, other)
                    for l in range(NL):
                        for g in range(GROUPS):
                            at = b4 * NB + (g // NB) * HALF * NB + g % NB
                            e = sync.value_load(ri[0:1, bass.ds(at, 1)], min_val=0, max_val=EXPERTS)
                            sync.dma_start(wr[:, l, g, :], wr_dram[bass.ds(e + l * (EXPERTS + 1), 1)].rearrange(
                                "o d h -> (o d) h")).then_inc(r_in[l], 16)
                    for l in range(NL):
                        sync.wait_ge(r_in[l], 16 * GROUPS)

            names, other = pool.stage()
            hid, h_out, biased, outs, o_step, h_step = (next(names) for _ in range(6))
            with nc.Block(no_gpsimd_drain=True) as block:
                @block.sync
                def _(sync):
                    pool.clear(sync, other)

                @block.tensor
                def _(pe):
                    def bank(n):
                        return ps[:, n % 4]

                    for n in range(4):
                        x = XF[:, bass.ds(b4, 1), PAD + 512 * (n % 2):PAD + 512 * (n % 2 + 1)]
                        pe.matmul(bank(n), wi[:, n // 2, :], x.rearrange("p o t -> p (o t)"),
                                  start=True, stop=True).then_inc(hid, 1)
                    for l in range(NL):
                        src = h0 if l == 0 else h1
                        for n in range(4):
                            pe.wait_ge(h_out, 4 + 16 * (l - 1) + 4 * n + 4 if l else n + 1)
                            pe.matmul(bank(n), ws[:, l, :], src[:, 4 * n:4 * n + 4, :].rearrange("p g t -> p (g t)"),
                                      start=True, stop=False)
                            for g in range(4 * n, 4 * n + 4):
                                mm = pe.matmul(bank(n)[:, P * (g % 4):P * (g % 4 + 1)], wr[:, l, g, 0:HID],
                                               src[:, g, :], start=False, stop=(g % 4 == 3))
                            mm.then_inc(hid, 1)
                    for g in range(GROUPS):
                        if g % 4 == 0:
                            pe.wait_ge(h_out, 4 + 16 + g + 4)
                        mm = pe.matmul(ps[:, 4 + g // NB, D * (g % NB):D * (g % NB + 1)], h0[:, g, :], wo[:, :],
                                       start=True, stop=True)
                        if g % NB == NB - 1:
                            mm.then_inc(outs, 1)

                @block.scalar
                def _(act):
                    for n in range(4):
                        act.wait_ge(hid, n + 1)
                        act.activation(h0[:, 4 * n:4 * n + 4, :].rearrange("p g t -> p (g t)"), ps[:, n % 4],
                                       ACT.Relu, bias=bi[:, 0:1]).then_inc(h_out, 1)
                    act.wait_ge(biased, NL)
                    for l in range(NL):
                        dst = h1 if l == 0 else h0
                        for g in range(GROUPS):
                            if g % 4 == 0:
                                act.wait_ge(hid, 4 * (l + 1) + g // 4 + 1)
                            act.activation(dst[:, g, :], ps[:, (g // 4) % 4, P * (g % 4):P * (g % 4 + 1)],
                                           ACT.Relu, bias=bias[:, l, g:g + 1]).then_inc(h_out, 1)

                @block.vector
                def _(v):
                    st = Steps(v, o_step)
                    for l in range(NL):
                        st.tell(v.tensor_scalar(bias[:, l, :], wr[:, l, :, HID], bs[:, l:l + 1], None, ALU.add),
                                  biased, "b")
                    for h in range(2):
                        x = H[:, :, bass.ds(P * b4 + D * h, D)]
                        v.wait_ge(outs, h + 1)
                        st.do(v.tensor_tensor(x, x, ps[:, 4 + h].rearrange("p (j d) -> p j d", d=D), ALU.add))
                        st.do(v.tensor_tensor(x, x, bcast(bo[:, :], 1, NB), ALU.add))



TWO_PI = 6.2831845
ROUND = 1.5 * 2.0 ** 23


def stage_state_filter(nc, pool, K, layer, Kt, table, ps, C):
    NPAR = 5
    with ExitStack() as ctx:
        def sb(name, shape):
            return ctx.enter_context(nc.sbuf_tensor(name + "_" + str(pool.fresh()), shape, F32))

        par, dk = sb("s4_par", [P, NPAR, D]), sb("s4_d", [1, D])
        a = sb("s4_small", [P, 16, D])
        sc = sb("s4_exp", [P, 4, D])
        big = sb("s4_big", [P, 2, 16, P])
        rj = sb("s4_rj", [P, 4, D, NB])
        names, other = pool.stage()
        p_in, v_step, a_step, prod, sined, exped, t_ready, k_made, k_out, d_in, asked = (
            next(names) for _ in range(11))
        dt, are, lr, tr, er, ei, cr, ci, den, x, y, z = (a[:, k] for k in range(12))
        em1, hs = a[:, 13], a[:, 14]
        aim, cre, cim = par[:, 2], par[:, 3], par[:, 4]
        lv, jv = C["lv"], C["jv"]
        ph, ph2, sg = C["cols"][:, 0:1], C["cols"][:, 1:2], C["cols"][:, 2:3]
        ph_a, ph2_a = C["cols"][:, 3:4], C["cols"][:, 4:5]
        CH = 16
        with nc.Block(no_gpsimd_drain=True) as block:
            @block.sync
            def _(sync):
                pool.clear(sync, other)
                load(sync, p_in, [(par[:, :, :], K["s4_par"][bass.ds(layer, 1)].rearrange("o p k h -> (o p) k h")),
                                  (dk[:, :], K["s4_D"][bass.ds(layer, 1)])])

            @block.scalar
            def _(act):
                act.wait_ge(asked, 2)
                act.activation(rj[:, 2], rj[:, 2], ACT.Exp).then_inc(a_step, 1)
                act.wait_ge(asked, 3)
                act.activation(y, tr, ACT.Sin, scale=-TWO_PI, bias=C["quarter"]).then_inc(a_step, 1)
                act.activation(z, x, ACT.Sin, scale=-TWO_PI).then_inc(a_step, 1)
                act.activation(hs, x, ACT.Sin, scale=-TWO_PI / 2).then_inc(a_step, 1)
                act.wait_ge(asked, 4)
                act.activation(rj[:, 0], rj[:, 0], ACT.Sin, scale=-TWO_PI, bias=ph_a).then_inc(a_step, 1)
                act.activation(rj[:, 1], rj[:, 1], ACT.Sin, scale=-TWO_PI, bias=ph2_a).then_inc(a_step, 1)
                for c in range(D // CH):
                    act.wait_ge(sined, c + 1)
                    cols = table[:, CH * c:CH * (c + 1), :]
                    act.activation(cols, cols, ACT.Sin, scale=-TWO_PI, bias=ph_a).then_inc(exped, 1)
                    act.wait_ge(prod, 2 * c + 2)
                    act.activation(big[:, 1], big[:, 1], ACT.Exp).then_inc(exped, 1)
                act.wait_ge(k_made, 1)
                act.activation(Kt[:, :, :], ps[:, 0].rearrange("p (h j) -> p j h", j=NB), ACT.Copy,
                               scale=2.0).then_inc(k_out, 1)

            @block.gpsimd
            def _(g):
                for c in range(D // CH):
                    if c >= 1:
                        g.wait_ge(t_ready, c)
                    else:
                        g.wait_ge(asked, 1)
                    lo = slice(CH * c, CH * (c + 1))
                    g.tensor_tensor(big[:, 0], bcast(tr0(a)[:, lo], 2, P), bcast(lv, 1, CH), ALU.mult).then_inc(prod, 1)
                    g.tensor_tensor(big[:, 1], bcast(lr[:, lo], 2, P), bcast(lv, 1, CH), ALU.mult).then_inc(prod, 1)

            @block.vector
            def _(v):
                st = Steps(v, v_step)

                def tt(out, p, q, op):
                    st.do(v.tensor_tensor(out, p, q, op))

                def ts(out, p, s1, s2, op0, op1=None):
                    st.do(v.tensor_scalar(out, p, s1, s2, op0, op1) if op1 is not None
                          else v.tensor_scalar(out, p, s1, None, op0))

                def reduce_turns(out, n, q, phase):
                    ts(n, q, phase, ROUND, ALU.add, ALU.add)
                    st.do(v.scalar_tensor_tensor(out=out, in0=n, scalar=-ROUND, in1=q, op0=ALU.add,
                                                 op1=ALU.subtract))

                def exponential(q, e, m1):
                    n, r, p = sc[:, 0], sc[:, 1], sc[:, 2]
                    two_n = sc[:, 3]
                    ts(n, q, 1 / math.log(2), ROUND, ALU.mult, ALU.add)
                    ts(n, n, -ROUND, None, ALU.add)
                    st.do(v.scalar_tensor_tensor(out=r, in0=n, scalar=-0.693359375, in1=q, op0=ALU.mult, op1=ALU.add))
                    st.do(v.scalar_tensor_tensor(out=r, in0=n, scalar=2.12194440e-4, in1=r, op0=ALU.mult, op1=ALU.add))
                    ts(p, r, 1 / math.factorial(8), None, ALU.mult)
                    for k in range(7, 0, -1):
                        st.do(v.scalar_tensor_tensor(out=p, in0=p, scalar=1 / math.factorial(k), in1=r,
                                                     op0=ALU.add, op1=ALU.mult))
                    ts(n, n, -126.0, None, ALU.max)
                    ts(two_n.bitcast(I32), n, 127.0, 2.0 ** 23, ALU.add, ALU.mult)
                    tt(p, p, two_n, ALU.mult)
                    if m1 is not None:
                        st.do(v.scalar_tensor_tensor(out=m1, in0=two_n, scalar=-1.0, in1=p, op0=ALU.add, op1=ALU.add))
                    tt(e, p, two_n, ALU.add)

                v.wait_ge(p_in, 32)
                exponential(par[:, 0], dt, None)
                exponential(par[:, 1], x, None)
                ts(are, x, -1.0, None, ALU.mult)
                tt(lr, are, dt, ALU.mult)
                exponential(lr, den, em1)
                tt(tr, aim, dt, ALU.mult)
                ts(tr, tr, 1 / (2 * math.pi), None, ALU.mult)
                reduce_turns(y, x, tr, 0.0)
                ts(tr0(a), y, -1.0, None, ALU.mult)
                v.sem_inc(asked, 1)
                tt(rj[:, 2], bcast(lr, 2, NB), bcast(jv, 1, D), ALU.mult)
                v.sem_inc(asked, 1)
                reduce_turns(tr, z, tr0(a), 0.25)
                reduce_turns(x, z, tr0(a), 0.0)
                v.sem_inc(asked, 1)
                tt(rj[:, 3], bcast(tr0(a), 2, NB), bcast(jv, 1, D), ALU.mult)
                reduce_turns(rj[:, 0], rj[:, 1], rj[:, 3], ph)
                ts(rj[:, 1], rj[:, 3], ph2, ROUND, ALU.add, ALU.add)
                st.do(v.scalar_tensor_tensor(out=rj[:, 1], in0=rj[:, 1], scalar=-ROUND, in1=rj[:, 3],
                                             op0=ALU.add, op1=ALU.subtract))
                v.sem_inc(asked, 1)
                v.wait_ge(a_step, 4)
                tt(er, em1, y, ALU.mult)
                tt(hs, hs, hs, ALU.mult)
                st.do(v.scalar_tensor_tensor(out=er, in0=hs, scalar=-2.0, in1=er, op0=ALU.mult, op1=ALU.add))
                tt(ei, den, z, ALU.mult)
                tt(den, are, are, ALU.mult)
                tt(x, aim, aim, ALU.mult)
                tt(den, den, x, ALU.add)
                st.do(v.reciprocal(den, den))
                tt(cr, er, are, ALU.mult)
                tt(x, ei, aim, ALU.mult)
                tt(cr, cr, x, ALU.add)
                tt(cr, cr, den, ALU.mult)
                tt(ci, ei, are, ALU.mult)
                tt(x, er, aim, ALU.mult)
                tt(ci, ci, x, ALU.subtract)
                tt(ci, ci, den, ALU.mult)
                tt(x, cre, cr, ALU.mult)
                tt(z, cim, ci, ALU.mult)
                tt(x, x, z, ALU.subtract)
                tt(y, cre, ci, ALU.mult)
                tt(z, cim, cr, ALU.mult)
                tt(y, y, z, ALU.add)
                ts(x, x, sg, None, ALU.mult)
                v.wait_ge(a_step, 6)
                tt(rj[:, 0], rj[:, 0], rj[:, 2], ALU.mult)
                tt(rj[:, 1], rj[:, 1], rj[:, 2], ALU.mult)
                tt(rj[:, 0], rj[:, 0], bcast(x, 2, NB), ALU.mult)
                tt(rj[:, 1], rj[:, 1], bcast(y, 2, NB), ALU.mult)
                tt(rj[:, 0], rj[:, 0], rj[:, 1], ALU.subtract)
                for c in range(D // CH):
                    cols = table[:, CH * c:CH * (c + 1), :]
                    v.wait_ge(prod, 2 * c + 1)
                    ts(cols, big[:, 0], ph, ROUND, ALU.add, ALU.add)
                    st.tell(v.scalar_tensor_tensor(out=cols, in0=cols, scalar=-ROUND, in1=big[:, 0],
                                                     op0=ALU.add, op1=ALU.subtract), sined, "s")
                    v.wait_ge(exped, 2 * c + 2)
                    st.tell(v.tensor_tensor(cols, cols, big[:, 1], ALU.mult), t_ready, "t")
                v.wait_ge(k_out, 1)
                tt(Kt[0:1, 0, :], Kt[0:1, 0, :], dk[:, :], ALU.add)

            @block.tensor
            def _(pe):
                for h in range(D):
                    if h % CH == 0:
                        pe.wait_ge(t_ready, h // CH + 1)
                    mm = pe.matmul(ps[:, 0, NB * h:NB * (h + 1)], table[:, h, :], rj[:, 0, h, :],
                                   start=True, stop=True)
                mm.then_inc(k_made, 1)


def tr0(a):
    return a[:, 12]


def stage_glu(nc, pool, K, C, layer, U, X, XF, Wout, bout, ident, ps):
    names, other = pool.stage()
    acted, turned, copied, w_in = (next(names) for _ in range(4))
    with nc.Block(no_gpsimd_drain=True) as block:
        @block.sync
        def _(sync):
            pool.clear(sync, other)
            load(sync, w_in, [(Wout, K["s4_wout"][bass.ds(layer, 1)].rearrange("o p n -> (o p) n")),
                              (bout, K["s4_bout"][bass.ds(layer, 1)].rearrange("o n -> (o n)").partition_broadcast(P))])
            sync.wait_ge(w_in, 32)

        @block.scalar
        def _(act):
            for j in range(NB):
                act.activation(U[:, j], U[:, j], ACT.Gelu_apprx_tanh).then_inc(acted, 1)
            copy_blocks(act, XF, ps, turned, copied)
            act.wait_ge(copied, NB)

        @block.tensor
        def _(pe):
            turn_blocks(pe, U, ident, ps, turned, copied, ready=acted)

    names, other = pool.stage()
    made, gated, t_free, summed, v_step = (next(names) for _ in range(5))
    with nc.Block(no_gpsimd_drain=True) as block:
        @block.sync
        def _(sync):
            pool.clear(sync, other)

        @block.tensor
        def _(pe):
            for n in range(2 * NB):
                j, b = n // 2, 2 * (n % 2)
                if n >= 8:
                    pe.wait_ge(t_free, n - 7)
                for k in range(2):
                    lhs = XF[:, b + k, PAD + P * j:PAD + P * (j + 1)]
                    mm = pe.matmul(ps[:, n % 8, 256 * k:256 * (k + 1)], lhs, Wout, start=True, stop=True)
                mm.then_inc(made, 1)

        @block.vector
        def _(v):
            st = Steps(v, v_step)

            def gate(n):
                j, b = n // 2, 2 * (n % 2)
                v.wait_ge(gated, n + 1)
                t = C["glu"][:, n % 4].rearrange("p (k z c) -> p k z c", k=2, z=2)
                x = X[:, j, P * b:P * (b + 2)].rearrange("p (k c) -> p k c", k=2)
                st.do(v.tensor_tensor(t[:, :, 0], t[:, :, 0], t[:, :, 1], ALU.mult))
                st.do(v.tensor_tensor(x, x, t[:, :, 0], ALU.add))

            for n in range(2 * NB):
                v.wait_ge(made, n + 1)
                st.tell(v.tensor_tensor(C["glu"][:, n % 4].rearrange("p (k c) -> p k c", k=2),
                                          ps[:, n % 8].rearrange("p (k c) -> p k c", k=2),
                                          bcast(bout, 1, 2), ALU.add), t_free, "t")
                if n >= 1:
                    gate(n - 1)
            gate(2 * NB - 1)

        @block.scalar
        def _(act):
            for n in range(2 * NB):
                act.wait_ge(t_free, n + 1)
                t = C["glu"][:, n % 4].rearrange("p (k z c) -> p k z c", k=2, z=2)[:, :, 1]
                act.activation(t, t, ACT.Sigmoid).then_inc(gated, 1)


def stages_state_space(nc, pool, K, H, X, XF, U, S, T, KH, MF, MI, stats, ident, ps):
    with ExitStack() as ctx:
        def sb(name, shape):
            return ctx.enter_context(nc.sbuf_tensor(name, shape, F32))

        lv, jv, cols = sb("s4_lv", [P, P]), sb("s4_jv", [P, NB]), sb("s4_cols", [P, 6])
        Kt, Wout, bout, gb = sb("s4_kt", [P, NB, D]), sb("s4_wout", [P, 256]), sb("s4_bout", [P, 256]), sb("s4_gb", [P, 2, D])
        C = {"lv": lv[:, :], "jv": jv[:, :], "cols": cols, "quarter": cols[:, 5:6], "glu": T}
        stage_load(nc, pool, [(lv[:, :], K["s4_lv"]), (jv[:, :], K["s4_jv"]), (cols[:, :], K["s4_cols"])])
        stage_copy(nc, pool, X, H)
        pool.open_loop()
        with nc.Fori(0, 4) as layer:
            stage_load(nc, pool, [(gb[:, :, :], K["s4_gb"][bass.ds(layer, 1)].rearrange("o k d -> (o k d)")
                                   .partition_broadcast(P).rearrange("p (k d) -> p k d", k=2))])
            stage_state_filter(nc, pool, K, layer, Kt, S[:, :, :].rearrange("p a (b l) -> p (a b) l", l=P), ps, C)
            stage_filter_spectrum(nc, pool, None, Kt, KH, S, T, MF, ps)
            stage_layernorm(nc, pool, X, U, stats, T, gain=gb[:, 0], bias=gb[:, 1])
            stage_long_conv(nc, pool, U, KH, S, T, MF, MI, ps)
            stage_glu(nc, pool, K, C, layer, U, X, XF, Wout[:, :], bout[:, :], ident, ps)
            pool.even(nc)
        stage_layernorm(nc, pool, X, H, stats, T, add=H)


def stage_copy(nc, pool, dst, src):
    names, other = pool.stage()
    copied = next(names)
    with nc.Block(no_gpsimd_drain=True) as block:
        @block.sync
        def _(sync):
            pool.clear(sync, other)

        @block.vector
        def _(v):
            v.tensor_copy(dst[:, :, :], src[:, :, :]).then_inc(copied, 1)
            v.wait_ge(copied, 1)



def stage_top2(nc, pool, XF, router, rbias, rank, gates, gF, sc, ident, ps, on_probs):
    E = 8
    G = NB * B
    names, other = pool.stage()
    made, v_step, centred, exped, weighed, turned, copied, zeroed = (next(names) for _ in range(8))
    with nc.Block(no_gpsimd_drain=True) as block:
        @block.sync
        def _(sync):
            pool.clear(sync, other)

        @block.gpsimd
        def _(g):
            g.memset(gF[:, :, :], 0.0).then_inc(zeroed, 1)
            g.wait_ge(zeroed, 1)

        @block.tensor
        def _(pe):
            for n in range(NB * HALF):
                j, b4 = n // HALF, n % HALF
                mm = pe.matmul(ps[:, 0, 2 * E * n:2 * E * (n + 1)], XF[:, b4, PAD + P * j:PAD + P * (j + 1)],
                               router, start=True, stop=True)
            mm.then_inc(made, 1)
            pe.wait_ge(weighed, 1)
            for n in range(NB * HALF):
                j, b4 = n // HALF, n % HALF
                if n >= 28:
                    pe.wait_ge(copied, n // 4 - 6)
                mm = pe.transpose(ps[0:2 * E, 1 + (n // 4) % 7, P * b4:P * (b4 + 1)],
                                  gates[:, 2 * E * n:2 * E * (n + 1)], ident)
                if b4 == HALF - 1:
                    mm.then_inc(turned, 1)

        @block.scalar
        def _(act):
            act.wait_ge(centred, 1)
            act.activation(sc[:, 1], sc[:, 1], ACT.Exp).then_inc(exped, 1)
            act.wait_ge(zeroed, 1)
            for j in range(NB):
                act.wait_ge(turned, j + 1)
                src = ps[0:2 * E, 1 + j % 7].rearrange("p (b t) -> p b t", b=HALF)
                act.activation(gF[0:2 * E, :, P * j:P * (j + 1)], src, ACT.Copy).then_inc(copied, 1)
            act.wait_ge(copied, NB)

        @block.vector
        def _(v):
            st = Steps(v, v_step)

            def g8(k):
                return sc[:, k].rearrange("p (g e) -> p g e", e=E)

            def tt(out, a, b, op):
                st.do(v.tensor_tensor(out, a, b, op))

            def top(out, a, op=ALU.max):
                st.do(v.tensor_reduce(out, a, AX, op))

            m, r = sc[:, 6, 0:G], sc[:, 6, G:2 * G]
            v.wait_ge(made, 1)
            if rbias is None:
                st.do(v.tensor_copy(sc[:, 0], ps[:, 0]))
            else:
                tt(g8(0), ps[:, 0].rearrange("p (g e) -> p g e", e=E), bcast(rbias, 1, G), ALU.add)
            top(m, g8(0))
            st.tell(v.tensor_tensor(g8(1), g8(0), bcast(m, 2, E), ALU.subtract), centred, "c")
            v.wait_ge(exped, 1)
            if on_probs:
                top(m, g8(1), ALU.add)
                st.do(v.reciprocal(m, m))
                tt(g8(1), g8(1), bcast(m, 2, E), ALU.mult)
            val = g8(1) if on_probs else g8(0)
            for k in (2, 3):
                top(m, val)
                tt(g8(4), val, bcast(m, 2, E), ALU.is_equal)
                tt(g8(4), g8(4), bcast(rank, 1, G), ALU.mult)
                top(r, g8(4))
                tt(g8(k), g8(4), bcast(r, 2, E), ALU.is_equal)
                if k == 2:
                    st.do(v.scalar_tensor_tensor(out=g8(5), in0=g8(2), scalar=-1e30, in1=val, op0=ALU.mult,
                                                 op1=ALU.add))
                    val = g8(5)
            tt(g8(2), g8(2), g8(3), ALU.add)
            tt(g8(1), g8(1), g8(2), ALU.mult)
            top(m, g8(1), ALU.add)
            if on_probs:
                st.do(v.tensor_scalar(m, m, 1e-12, None, ALU.max))
            st.do(v.reciprocal(m, m))
            st.tell(v.tensor_tensor(gates[:, :].rearrange("p (g e) -> p g e", e=E), g8(1), bcast(m, 2, E),
                                      ALU.mult), weighed, "w")


def stage_experts(nc, pool, H, XF, gF, w1, b1, w2, b2, sel, ident, ps, buf, nq, alpha, func, middle=None,
                  gate_of=None):
    GA, GB_, OF = buf
    units = [(c, h, q) for c in range(2) for h in range(2) for q in range(nq)]
    NU = len(units)
    per = 2 * nq
    pool.open_loop()
    with nc.Fori(0, HALF) as b4:
        names, other = pool.stage()
        hid, hid2, acted, mid_done, gated, used, o_done, of_out, o_turned, h_out = (
            next(names) for _ in range(10))
        with nc.Block(no_gpsimd_drain=True) as block:
            @block.sync
            def _(sync):
                pool.clear(sync, other)

            @block.tensor
            def _(pe):
                def first(n):
                    c, h, q = units[n]
                    if n >= 2:
                        pe.wait_ge(acted, n - 1)
                        if gate_of is None:
                            pe.wait_ge(gated, n - 1)
                    x = XF[:, bass.ds(b4, 1), PAD + 512 * c:PAD + 512 * (c + 1)].rearrange("p o t -> p (o t)")
                    mm = pe.matmul(ps[:, n % 2], w1[:, h, q], x, start=True, stop=True)
                    mm.then_inc(hid, 1)
                    if gate_of is None:
                        g = gF[:, bass.ds(b4, 1), 512 * c:512 * (c + 1)].rearrange("p o t -> p (o t)")
                        pe.matmul(ps[:, 2 + n % 2], sel[:, h, q], g, start=True, stop=True).then_inc(hid2, 1)

                def mid(n):
                    c, h, q = units[n]
                    pe.wait_ge(acted, n + 1)
                    if n >= 2:
                        pe.wait_ge(mid_done, n - 1)
                    pe.matmul(ps[:, 2 + n % 2], middle[0][:, q], GA[:, n % 2], start=True, stop=True).then_inc(hid2, 1)

                def second(n):
                    c, h, q = units[n]
                    pe.wait_ge(gated, n + 1)
                    k = n % per
                    pe.matmul(ps[:, 4 + c], w2[:, h, q], GB_[:, n % 2], start=(k == 0),
                              stop=False).then_inc(used, 1)
                    if k == per - 1:
                        if gate_of is not None:
                            g = gF[:, 512 * c:512 * (c + 1)]
                        else:
                            g = gF[:, bass.ds(b4, 1), 512 * c:512 * (c + 1)].rearrange("p o t -> p (o t)")
                        pe.matmul(ps[:, 4 + c], b2, g, start=False, stop=True).then_inc(o_done, 1)

                def back(c):
                    pe.wait_ge(of_out, c + 1)
                    for k in range(4):
                        mm = pe.transpose(ps[:, 6 + c, P * k:P * (k + 1)], OF[:, c, P * k:P * (k + 1)], ident)
                    mm.then_inc(o_turned, 1)

                lag = 2 if middle is not None else 1
                for n in range(NU + lag):
                    if n < NU:
                        first(n)
                    if middle is not None and 1 <= n <= NU:
                        mid(n - 1)
                    if n >= lag:
                        second(n - lag)
                    if n == per + lag + 1:
                        back(0)
                back(1)

            @block.scalar
            def _(act):
                def middle_act(n):
                    act.wait_ge(hid2, n + 1)
                    q = units[n][2]
                    if n >= 2:
                        act.wait_ge(gated, n - 1)
                    act.activation(OFX(buf)[:, n % 2], ps[:, 2 + n % 2], ACT.Relu, bias=middle[2][:, q:q + 1],
                                   scale=middle[1][:, q:q + 1]).then_inc(mid_done, 1)

                def out(c):
                    act.wait_ge(o_done, c + 1)
                    act.activation(OF[:, c], ps[:, 4 + c], ACT.Copy).then_inc(of_out, 1)

                for n, (c, h, q) in enumerate(units):
                    act.wait_ge(hid, n + 1)
                    if n >= 2:
                        act.wait_ge(gated if middle is None else mid_done, n - 1)
                    if middle is None:
                        act.activation(GA[:, n % 2], ps[:, n % 2], func, bias=b1[:, q:q + 1]).then_inc(acted, 1)
                    else:
                        act.activation(GA[:, n % 2], ps[:, n % 2], func, bias=b1[1][:, q:q + 1],
                                       scale=b1[0][:, q:q + 1]).then_inc(acted, 1)
                        if n >= 1:
                            middle_act(n - 1)
                    if n == per + 2:
                        out(0)
                if middle is not None:
                    middle_act(NU - 1)
                out(1)

            @block.vector
            def _(v):
                st = Steps(v, None)

                def update(c):
                    v.wait_ge(o_turned, c + 1)
                    x = H[:, 4 * c:4 * (c + 1), bass.ds(P * b4, P)]
                    st.tell(v.scalar_tensor_tensor(out=x, in0=x, scalar=float(alpha),
                                                     in1=ps[:, 6 + c].rearrange("p (j d) -> p j d", d=P),
                                                     op0=ALU.mult, op1=ALU.add), h_out, "h")

                for n, (c, h, q) in enumerate(units):
                    if middle is None:
                        v.wait_ge(acted, n + 1)
                        v.wait_ge(hid2, n + 1)
                        g, src = ps[:, 2 + n % 2], GA
                    else:
                        v.wait_ge(mid_done, n + 1)
                        g, src = gate_of[:, q, 512 * c:512 * (c + 1)], OFX(buf)
                    if n >= 2:
                        v.wait_ge(used, n - 1)
                    st.tell(v.tensor_tensor(GB_[:, n % 2], src[:, n % 2], g, ALU.mult), gated, "g")
                    if n == per + 4:
                        update(0)
                update(1)
        pool.even(nc)


def OFX(buf):
    return buf[2][:, 2:4]


def stage_gate_spread(nc, pool, gF, sel, GT, nq, ps):
    names, other = pool.stage()
    made, out = next(names), next(names)
    with nc.Block(no_gpsimd_drain=True) as block:
        @block.sync
        def _(sync):
            pool.clear(sync, other)

        @block.tensor
        def _(pe):
            for n in range(2 * nq):
                q, c = n // 2, n % 2
                pe.matmul(ps[:, n], sel[:, 0, q], gF[:, 512 * c:512 * (c + 1)], start=True,
                          stop=True).then_inc(made, 1)

        @block.scalar
        def _(act):
            for n in range(2 * nq):
                q, c = n // 2, n % 2
                act.wait_ge(made, n + 1)
                act.activation(GT[:, q, 512 * c:512 * (c + 1)], ps[:, n], ACT.Copy).then_inc(out, 1)
            act.wait_ge(out, 2 * nq)


def stages_moe(nc, pool, K, pre, H, XF, ident, ps, nq, on_probs, alpha):
    with ExitStack() as ctx:
        def sb(name, shape):
            return ctx.enter_context(nc.sbuf_tensor(pre + name, shape, F32))

        router, rb, rank = sb("rt", [P, 16]), sb("rb", [P, 8]), sb("rank", [P, 8])
        w1, w2 = sb("w1", [P, 2, nq, P]), sb("w2", [P, 2, nq, P])
        sel, b1, b2 = sb("sel", [P, 2, nq, P]), sb("b1", [P, nq]), sb("b2", [P, P])
        gates, gF, sc = sb("gates", [P, 512]), sb("gf", [P, HALF, L]), sb("sc", [P, 7, 512])
        GA, GB_, OF = sb("ga", [P, 2, 512]), sb("gb", [P, 2, 512]), sb("of", [P, 4, 512])
        pairs = [(router[:, :], K[pre + "router"]), (rank[:, :], K["rank"]), (w1[:, :, :, :], K[pre + "w1"]),
                 (w2[:, :, :, :], K[pre + "w2"]), (sel[:, :, :, :], K[pre + "sel"]), (b1[:, :], K[pre + "b1"]),
                 (b2[:, :], K[pre + "b2"])]
        if not on_probs:
            pairs.append((rb[:, :], K[pre + "rb"].partition_broadcast(P)))
        stage_load(nc, pool, pairs)
        stage_top2(nc, pool, XF, router[:, :], None if on_probs else rb[:, :], rank[:, :], gates, gF, sc, ident,
                   ps, on_probs)
        stage_experts(nc, pool, H, XF, gF, w1, b1, w2, b2[:, :], sel, ident, ps, (GA, GB_, OF), nq, alpha,
                      ACT.Gelu)



def stage_hyena_filter(nc, pool, K, Kt, ps):
    with ExitStack() as ctx:
        def sb(name, shape):
            return ctx.enter_context(nc.sbuf_tensor("hy_" + name, shape, F32))

        z, w0, w12, w3 = sb("z", [3, L]), sb("w0", [3, D]), sb("w12", [D, 2, D]), sb("w3", [D, D])
        bf, decay, fb = sb("bf", [D, 4]), sb("decay", [P, NB, D]), sb("fb", [1, D])
        h, q, n = sb("h", [D, L]), sb("q", [D, L]), sb("n", [D, L])
        names, other = pool.stage()
        w_in, made, reduced, sined, v_step, k_made = (next(names) for _ in range(6))
        with nc.Block(no_gpsimd_drain=True) as block:
            @block.sync
            def _(sync):
                pool.clear(sync, other)
                load(sync, w_in, [(z[:, :], K["hy_z"]), (w0[:, :], K["hy_w0"]), (w12[:, :, :], K["hy_w12"]),
                                  (w3[:, :], K["hy_w3"]), (bf[:, :], K["hy_bf"]), (fb[:, :], K["hy_fb"]),
                                  (decay[:, :, :], K["hy_decay"].rearrange("p (j d) -> p j d", j=NB))])

            @block.tensor
            def _(pe):
                pe.wait_ge(w_in, 7 * 16)
                for k in range(3):
                    if k >= 1:
                        pe.wait_ge(sined, k)
                    for c in range(2):
                        cols = slice(512 * c, 512 * (c + 1))
                        mm = (pe.matmul(ps[0:D, c], w0[:, :], z[:, cols], start=True, stop=True) if k == 0 else
                              pe.matmul(ps[0:D, c], w12[:, k - 1], h[:, cols], start=True, stop=True))
                    mm.then_inc(made, 1)
                pe.wait_ge(sined, 3)
                for j in range(NB):
                    mm = pe.matmul(ps[:, 2, D * j:D * (j + 1)], h[:, P * j:P * (j + 1)], w3[:, :],
                                   start=True, stop=True)
                mm.then_inc(k_made, 1)

            @block.scalar
            def _(act):
                for k in range(3):
                    act.wait_ge(reduced, k + 1)
                    act.activation(h[:, :], q[:, :], ACT.Sin).then_inc(sined, 1)

            @block.vector
            def _(v):
                st = Steps(v, v_step)
                for k in range(3):
                    v.wait_ge(made, k + 1)
                    src = ps[0:D, 0:2].rearrange("p a b -> p (a b)")
                    st.do(v.tensor_scalar(n[:, :], src, bf[:, k:k + 1], bf[:, 3:4], ALU.add, ALU.mult))
                    if k >= 1:
                        v.wait_ge(sined, k)
                    st.do(v.tensor_scalar(q[:, :], n[:, :], 1 / (2 * math.pi), ROUND, ALU.mult, ALU.add))
                    st.do(v.tensor_scalar(q[:, :], q[:, :], -ROUND, None, ALU.add))
                    st.do(v.scalar_tensor_tensor(out=n[:, :], in0=q[:, :], scalar=-6.28125, in1=n[:, :],
                                                 op0=ALU.mult, op1=ALU.add))
                    st.do(v.scalar_tensor_tensor(out=q[:, :], in0=q[:, :], scalar=-(2 * math.pi - 6.28125),
                                                 in1=n[:, :], op0=ALU.mult, op1=ALU.add))
                    st.tell(v.tensor_scalar(q[:, :], q[:, :], -3.1415925, 3.1415925, ALU.max, ALU.min),
                              reduced, "r")
                v.wait_ge(k_made, 1)
                st.do(v.tensor_tensor(Kt[:, :, :], ps[:, 2].rearrange("p (j d) -> p j d", j=NB), decay[:, :, :],
                                      ALU.mult))
                st.do(v.tensor_tensor(Kt[0:1, 0, :], Kt[0:1, 0, :], fb[:, :], ALU.add))


def stage_hyena_weights(nc, pool, K, Win, Bin, Wout, Bout, ps):
    NI = 3 * P
    with ExitStack() as ctx:
        def sb(name, shape):
            return ctx.enter_context(nc.sbuf_tensor("hw_" + name, shape, F32))

        w, wo = sb("w", [P, NI]), sb("wo", [P, P])
        taps, otaps = sb("taps", [P, 3, NI]), sb("otaps", [P, 3, P])
        rows, orow, edge, t = sb("rows", [P, 2, NI]), sb("orow", [P, P]), sb("edge", [P, 4]), sb("t", [P, NI])
        names, other = pool.stage()
        w_in, v_step = next(names), next(names)
        with nc.Block(no_gpsimd_drain=True) as block:
            @block.sync
            def _(sync):
                pool.clear(sync, other)
                load(sync, w_in, [(w[:, :], K["hw_w"]), (wo[:, :], K["hw_wo"]), (edge[:, :], K["hw_edge"])] +
                     [(d[:, :, :], K[k].partition_broadcast(P)) for d, k in
                      ((taps, "hw_taps"), (otaps, "hw_otaps"), (rows, "hw_rows"))] +
                     [(orow[:, :], K["hw_orow"].partition_broadcast(P))])

            @block.vector
            def _(v):
                st = Steps(v, v_step)

                def tt(out, a, b, op):
                    st.do(v.tensor_tensor(out, a, b, op))

                def fma(out, a, col, b):
                    st.do(v.scalar_tensor_tensor(out=out, in0=a, scalar=edge[:, col:col + 1], in1=b, op0=ALU.mult,
                                                 op1=ALU.add))

                v.wait_ge(w_in, 7 * 16)
                tt(Win[:, :, :], bcast(w[:, :], 1, 3), taps[:, :, :], ALU.mult)
                tt(Wout[:, :, :], bcast(wo[:, :], 1, 3), otaps[:, :, :], ALU.mult)
                tt(taps[:, :, :], bcast(rows[:, 0], 1, 3), taps[:, :, :], ALU.mult)
                tt(t[:, :], taps[:, 2], rows[:, 1], ALU.add)
                fma(Bin[:, 0], taps[:, 1], 0, t[:, :])
                fma(Bin[:, 0], taps[:, 0], 1, Bin[:, 0])
                tt(Bin[:, 1], t[:, :], taps[:, 1], ALU.add)
                tt(Bin[:, 1], Bin[:, 1], taps[:, 0], ALU.add)
                tt(otaps[:, :, :], bcast(orow[:, :], 1, 3), otaps[:, :, :], ALU.mult)
                tt(t[:, 0:P], otaps[:, 1], otaps[:, 2], ALU.add)
                fma(Bout[:, 0], otaps[:, 0], 0, t[:, 0:P])
                tt(Bout[:, 1], t[:, 0:P], otaps[:, 0], ALU.add)
                tt(t[:, 0:P], otaps[:, 0], otaps[:, 1], ALU.add)
                fma(Bout[:, 2], otaps[:, 2], 2, t[:, 0:P])


def stage_gates_in(nc, pool, XN, XF, U, X1, V, Win, Bin, gb, ident, ps):
    names, other = pool.stage()
    turned, copied, made, taken, v_step = (next(names) for _ in range(5))
    with nc.Block(no_gpsimd_drain=True) as block:
        @block.sync
        def _(sync):
            pool.clear(sync, other)

        @block.tensor
        def _(pe):
            def turn(j):
                if j >= 2:
                    pe.wait_ge(copied, j - 1)
                for b4 in range(HALF):
                    mm = pe.transpose(ps[:, j % 2, P * b4:P * (b4 + 1)], XN[:, j, P * b4:P * (b4 + 1)], ident)
                mm.then_inc(turned, 1)

            def project(j):
                pe.wait_ge(copied, j + 1)
                for pair in range(2):
                    n = 2 * j + pair
                    if n >= 3:
                        pe.wait_ge(taken, n - 2)
                    for k in range(2):
                        b4 = 2 * pair + k
                        for tap in range(3):
                            at = PAD + P * j - 2 + tap
                            mm = pe.matmul(ps[:, 2 + 2 * (n % 3) + k, 0:3 * P], XF[:, b4, at:at + P],
                                           Win[:, tap], start=(tap == 0), stop=(tap == 2))
                    mm.then_inc(made, 1)

            turn(0)
            for j in range(NB):
                if j + 1 < NB:
                    turn(j + 1)
                project(j)

        @block.scalar
        def _(act):
            for j in range(NB):
                act.wait_ge(turned, j + 1)
                act.activation(XF[:, :, PAD + P * j:PAD + P * (j + 1)],
                               ps[:, j % 2].rearrange("p (b t) -> p b t", b=HALF), ACT.Identity,
                               bias=gb[:, 1:2], scale=gb[:, 0:1]).then_inc(copied, 1)

        @block.vector
        def _(v):
            st = Steps(v, v_step)
            for n in range(2 * NB):
                j, b = n // 2, 2 * (n % 2)
                v.wait_ge(made, n + 1)
                src = ps[:, 2 + 2 * (n % 3):4 + 2 * (n % 3)]
                bias = Bin[:, 0 if j == 0 else 1]
                cols = slice(P * b, P * (b + 2))
                st.go(v.tensor_tensor(X1[:, j, cols].rearrange("p (k c) -> p k c", k=2), src[:, :, 0:P],
                                      bcast(bias[:, 0:P], 1, 2), ALU.add))
                t = V[:, n % 2]
                st.tell(v.tensor_tensor(t, src[:, :, P:3 * P], bcast(bias[:, P:3 * P], 1, 2), ALU.add), taken, "t")
                st.do(v.tensor_tensor(U[:, j, cols].rearrange("p (k c) -> p k c", k=2), t[:, :, 0:P],
                                      t[:, :, P:2 * P], ALU.mult))
            st.join()


def stage_gates_out(nc, pool, U, X1, X, XF, Wout, Bout, V, ident, ps):
    names, other = pool.stage()
    gated, turned, copied, made, biased, acted, v_step = (next(names) for _ in range(7))
    with nc.Block(no_gpsimd_drain=True) as block:
        @block.sync
        def _(sync):
            pool.clear(sync, other)

        @block.tensor
        def _(pe):
            def turn(j):
                pe.wait_ge(gated, j + 1)
                if j >= 3:
                    pe.wait_ge(copied, j - 2)
                for b4 in range(HALF):
                    mm = pe.transpose(ps[:, j % 3, P * b4:P * (b4 + 1)], U[:, j, P * b4:P * (b4 + 1)], ident)
                mm.then_inc(turned, 1)

            def project(j):
                pe.wait_ge(copied, min(j + 2, NB))
                if j >= 4:
                    pe.wait_ge(biased, j - 3)
                for b4 in range(HALF):
                    for tap in range(3):
                        at = PAD + P * j - 1 + tap
                        mm = pe.matmul(ps[:, 3 + j % 4, P * b4:P * (b4 + 1)], XF[:, b4, at:at + P],
                                       Wout[:, tap], start=(tap == 0), stop=(tap == 2))
                mm.then_inc(made, 1)

            turn(0)
            turn(1)
            for j in range(NB):
                if j + 2 < NB:
                    turn(j + 2)
                project(j)

        @block.scalar
        def _(act):
            def gelu(j):
                act.wait_ge(biased, j + 1)
                t = V[:, j % 4]
                act.activation(t, t, ACT.Gelu).then_inc(acted, 1)
                act.wait_ge(acted, 2 * j + 1)
                act.activation(t, t, ACT.Gelu).then_inc(acted, 1)

            for j in range(NB):
                act.wait_ge(turned, j + 1)
                act.activation(XF[:, :, PAD + P * j:PAD + P * (j + 1)],
                               ps[:, j % 3].rearrange("p (b t) -> p b t", b=HALF), ACT.Copy).then_inc(copied, 1)
                if j >= 2:
                    gelu(j - 2)
            gelu(NB - 2)
            gelu(NB - 1)

        @block.vector
        def _(v):
            st = Steps(v, v_step)
            for j in range(NB):
                st.tell(v.tensor_tensor(U[:, j], U[:, j], X1[:, j], ALU.mult), gated, "g")

            def finish(j):
                v.wait_ge(acted, 2 * j + 2)
                st.do(v.tensor_tensor(X[:, j], X[:, j], V[:, j % 4], ALU.add))

            for j in range(NB):
                v.wait_ge(made, j + 1)
                bias = Bout[:, 0 if j == 0 else 2 if j == NB - 1 else 1]
                st.tell(v.tensor_tensor(V[:, j % 4].rearrange("p (b c) -> p b c", b=HALF),
                                          ps[:, 3 + j % 4].rearrange("p (b c) -> p b c", b=HALF),
                                          bcast(bias, 1, HALF), ALU.add), biased, "b")
                if j >= 2:
                    finish(j - 2)
            finish(NB - 2)
            finish(NB - 1)


def stages_hyena(nc, pool, K, H, X, XF, U, S, T, KH, MF, MI, stats, ident, ps):
    DEPTH = 12
    with ExitStack() as ctx:
        def sb(name, shape):
            return ctx.enter_context(nc.sbuf_tensor("hs_" + name, shape, F32))

        Kt, Win, Bin = sb("kt", [P, NB, D]), sb("win", [P, 3, 3 * P]), sb("bin", [P, 2, 3 * P])
        Wout, Bout, gb, X1 = sb("wout", [P, 3, P]), sb("bout", [P, 3, P]), sb("gb", [P, 2]), sb("x1", [P, NB, W])
        stage_load(nc, pool, [(gb[:, :], K["hy_gb"])])
        stage_hyena_filter(nc, pool, K, Kt, ps)
        stage_filter_spectrum(nc, pool, None, Kt, KH, S, T, MF, ps)
        stage_hyena_weights(nc, pool, K, Win, Bin, Wout, Bout, ps)
        stage_copy(nc, pool, X, H)
        V = T[:, 0:4]
        V2 = T[:, 0:2].rearrange("p n (k c) -> p n k c", k=2)
        pool.open_loop()
        with nc.Fori(0, DEPTH) as _:
            stage_layernorm(nc, pool, X, U, stats, T)
            stage_gates_in(nc, pool, U, XF, U, X1, V2, Win, Bin, gb, ident, ps)
            stage_long_conv(nc, pool, U, KH, S, T, MF, MI, ps)
            stage_gates_out(nc, pool, U, X1, X, XF, Wout, Bout, V, ident, ps)
            pool.even(nc)
        stage_layernorm(nc, pool, X, H, stats, T, add=H)



def stages_mean_gated(nc, pool, K, H, XF, ident, ps):
    E, NQ = 8, 4
    with ExitStack() as ctx:
        def sb(name, shape):
            return ctx.enter_context(nc.sbuf_tensor("f2_" + name, shape, F32))

        wr, br = sb("wr", [P, E]), sb("br", [P, E])
        w1, wm, w2 = sb("w1", [P, 2, NQ, P]), sb("wm", [P, NQ, P]), sb("w2", [P, 2, NQ, P])
        sel, b2 = sb("sel", [P, 2, NQ, P]), sb("b2", [P, P])
        bn, aff = sb("bn", [P, 2, 5, NQ]), sb("aff", [P, 2, 3, NQ])
        g, m = sb("g", [P, NB, E]), sb("m", [P, NB])
        gF, GT = sb("gf", [P, L]), sb("gt", [P, NQ, L])
        GA, GB_, OF = sb("ga", [P, 2, 512]), sb("gb", [P, 2, 512]), sb("of", [P, 4, 512])
        names, other = pool.stage()
        w_in, made, v_step, for_sqrt, rooted, centred, exped, weighed, turned, copied, zeroed = (
            next(names) for _ in range(11))
        with nc.Block(no_gpsimd_drain=True) as block:
            @block.sync
            def _(sync):
                pool.clear(sync, other)
                load(sync, w_in, [(wr[:, :], K["f2_wr"]), (br[:, :], K["f2_br"].partition_broadcast(P)),
                                  (bn[:, :, :, :], K["f2_bn"]), (w1[:, :, :, :], K["f2_w1"]),
                                  (wm[:, :, :], K["f2_wm"]), (w2[:, :, :, :], K["f2_w2"]),
                                  (sel[:, :, :, :], K["m1_sel"]), (b2[:, :], K["f2_b2"])])
                sync.wait_ge(w_in, 8 * 16)

            @block.gpsimd
            def _(gp):
                gp.memset(gF[:, :], 0.0).then_inc(zeroed, 1)
                gp.wait_ge(zeroed, 1)

            @block.tensor
            def _(pe):
                pe.wait_ge(w_in, 8 * 16)
                for j in range(NB):
                    for b4 in range(HALF):
                        mm = pe.matmul(ps[:, 0, E * j:E * (j + 1)], XF[:, b4, PAD + P * j:PAD + P * (j + 1)],
                                       wr[:, :], start=(b4 == 0), stop=(b4 == HALF - 1))
                mm.then_inc(made, 1)
                pe.wait_ge(weighed, 1)
                for j in range(NB):
                    mm = pe.transpose(ps[0:E, 1 + j // 4, P * (j % 4):P * (j % 4 + 1)], g[:, j], ident)
                mm.then_inc(turned, 1)

            @block.scalar
            def _(act):
                act.wait_ge(for_sqrt, 1)
                act.activation(aff[:, :, 0], aff[:, :, 0], ACT.Sqrt).then_inc(rooted, 1)
                act.wait_ge(centred, 1)
                act.activation(g[:, :, :], g[:, :, :], ACT.Exp).then_inc(exped, 1)
                act.wait_ge(turned, 1)
                act.wait_ge(zeroed, 1)
                for k in range(2):
                    act.activation(gF[0:E, 512 * k:512 * (k + 1)], ps[0:E, 1 + k], ACT.Copy).then_inc(copied, 1)
                act.wait_ge(copied, 2)

            @block.vector
            def _(v):
                st = Steps(v, v_step)

                def tt(out, a, b, op):
                    st.do(v.tensor_tensor(out, a, b, op))

                v.wait_ge(w_in, 8 * 16)
                scale, shift = aff[:, :, 1], aff[:, :, 2]
                st.tell(v.tensor_scalar(aff[:, :, 0], bn[:, :, 4], 1e-3, None, ALU.add), for_sqrt, "s")
                v.wait_ge(rooted, 1)
                st.do(v.reciprocal(scale, aff[:, :, 0]))
                tt(scale, scale, bn[:, :, 1], ALU.mult)
                tt(shift, bn[:, :, 0], bn[:, :, 3], ALU.subtract)
                tt(shift, shift, scale, ALU.mult)
                tt(shift, shift, bn[:, :, 2], ALU.add)
                v.wait_ge(made, 1)
                src = ps[:, 0, 0:E * NB].rearrange("p (j e) -> p j e", e=E)
                st.do(v.scalar_tensor_tensor(out=g[:, :, :], in0=src, scalar=1.0 / B, in1=bcast(br[:, :], 1, NB),
                                             op0=ALU.mult, op1=ALU.add))
                st.do(v.tensor_reduce(m[:, :], g[:, :, :], AX, ALU.max))
                st.tell(v.tensor_tensor(g[:, :, :], g[:, :, :], bcast(m[:, :], 2, E), ALU.subtract), centred, "c")
                v.wait_ge(exped, 1)
                st.do(v.tensor_reduce(m[:, :], g[:, :, :], AX, ALU.add))
                st.do(v.reciprocal(m[:, :], m[:, :]))
                st.tell(v.tensor_tensor(g[:, :, :], g[:, :, :], bcast(m[:, :], 2, E), ALU.mult), weighed, "w")

        stage_gate_spread(nc, pool, gF, sel, GT, NQ, ps)
        stage_experts(nc, pool, H, XF, gF, w1, (aff[:, 0, 1], aff[:, 0, 2]), w2, b2[:, :], sel, ident, ps,
                      (GA, GB_, OF), NQ, 1.0, ACT.Relu, middle=(wm, aff[:, 1, 1], aff[:, 1, 2]), gate_of=GT)



def stages_fast_weights(nc, pool, K, H, X, XF, stats, T, ident, ps):
    S, NH, DH = B, 8, 32
    C = NH * DH
    NE = 5 * C + 2 * NH
    with ExitStack() as ctx:
        def sb(name, shape):
            return ctx.enter_context(nc.sbuf_tensor("fw_" + name, shape, F32))

        wq, wo, gb = sb("wq", [P, 2, NE]), sb("wo", [P, 2, D]), sb("gb", [P, 2])
        QKV = [sb("qkv0", [P, S, NE]), sb("qkv1", [P, S, NE])]
        XJ = sb("xj", [P, HALF, P])
        G = sb("g", [P, S, S, 3, NH])
        GQ = sb("gq", [P, S, NH])
        M, MZ = sb("m", [P, S - 1, 2 * C]), sb("mz", [P, S, C])
        ns, mx = sb("ns", [P, 2, 3 * NH]), sb("mx", [P, NH])
        qs, hm, E = sb("qs", [P, C]), sb("hm", [P, 2, NH]), sb("e", [P, 2, 2 * C])
        hT = sb("ht", [P, 2, 2, P])
        stage_load(nc, pool, [(gb[:, :], K["fw_gb"]), (wq[:, :, :], K["fw_wq"]), (wo[:, :, :], K["fw_wo"])])
        stage_layernorm(nc, pool, H, X, stats, T)
        stage_to_features(nc, pool, X, XF, ident, ps, gain=gb[:, 0:1], bias=gb[:, 1:2])
        slot = [(s % HALF, s // HALF) for s in range(S)]
        parts = [(0, 512), (512, 1024), (1024, NE)]
        PROJ, AB_BANK, OUT_BANK = 4, 3, 7
        QK_PROD = X
        RK_PROD = T[:, 0:NB // 2].rearrange("p a (b c) -> p (a b) c", c=C)
        H_PROD = T[:, NB // 2:NB].rearrange("p a (b c) -> p (a b) c", c=C)

        def heads(ap):
            n = len(ap.shape)
            return ap.rearrange("p (h d) -> p h d", d=DH) if n == 2 else ap.rearrange("p s (h d) -> p s h d", d=DH)

        def h_bank(t):
            return ps[:, t % 3, 0:C]

        def project(pe, s, made, copied, readied):
            b4, h = slot[s]
            for i, (lo, hi) in enumerate(parts):
                if s >= 1:
                    pe.wait_ge(copied, 4 * (s - 1) + (1, 3, 4)[i])
                    if i == 0:
                        pe.wait_ge(readied, 2 * (s - 1) + 1)
                pe.matmul(ps[:, PROJ + i, 0:hi - lo], XJ[:, b4], wq[:, h, lo:hi], start=True,
                          stop=True).then_inc(made, 1)

        def take(act, j, taken):
            act.activation(XJ[:, :, :], XF[:, :, bass.ds(PAD + P * j, P)], ACT.Copy).then_inc(taken, 1)

        def keep(act, Q, s, made, copied, readied):
            act.wait_ge(made, 3 * s + 1)
            if s >= 2:
                act.wait_ge(readied, 2 * (s - 2) + 1)
            e = E[:, s % 2]
            act.activation(e, ps[:, PROJ, 0:2 * C], ACT.Relu, scale=-1.0).then_inc(copied, 1)
            act.wait_ge(copied, 4 * s + 1)
            act.activation(e, e, ACT.Exp, scale=-1.0).then_inc(copied, 1)
            for i, (lo, hi) in list(enumerate(parts))[1:]:
                act.wait_ge(made, 3 * s + i + 1)
                act.activation(Q[:, s, lo:hi], ps[:, PROJ + i, 0:hi - lo], ACT.Copy).then_inc(copied, 1)

        def exp_rk(act, Q, s, readied, rk_exped):
            act.wait_ge(readied, 2 * s + 2)
            rk = Q[:, s, 2 * C:3 * C]
            act.activation(rk, rk, ACT.Exp).then_inc(rk_exped, 1)

        def ready(v, st, Q, s, copied, readied):
            rk = heads(Q[:, s, 2 * C:3 * C])
            v.wait_ge(copied, 4 * s + 2)
            st.tell(v.scalar_tensor_tensor(out=Q[:, s, 0:2 * C], in0=ps[:, PROJ, 0:2 * C], scalar=0.0,
                                           in1=E[:, s % 2], op0=ALU.max, op1=ALU.add), readied, "readied")
            v.wait_ge(copied, 4 * s + 3)
            st.do(v.tensor_reduce(mx[:, :], rk, AX, ALU.max))
            st.tell(v.tensor_tensor(rk, rk, bcast(mx[:, :], 2, DH), ALU.subtract), readied, "readied")

        def normalise(v, st, Q, s, rk_exped):
            v.wait_ge(rk_exped, s + 1)
            qkr, n = heads(Q[:, s, 0:3 * C]), ns[:, s % 2]
            st.do(v.tensor_reduce(n, qkr, AX, ALU.add))
            st.do(v.reciprocal(n, n))
            st.do(v.tensor_tensor(qkr, qkr, bcast(n, 2, DH), ALU.mult))

        def stage_project(Q):
            names, other = pool.stage()
            taken, made, copied, readied, rk_exped, v_step = (next(names) for _ in range(6))
            with nc.Block(no_gpsimd_drain=True) as block:
                @block.sync
                def _(sync):
                    pool.clear(sync, other)

                @block.tensor
                def _(pe):
                    pe.wait_ge(taken, 1)
                    for s in range(S):
                        project(pe, s, made, copied, readied)

                @block.scalar
                def _(act):
                    take(act, 0, taken)
                    for s in range(S):
                        keep(act, Q, s, made, copied, readied)
                        exp_rk(act, Q, s, readied, rk_exped)
                    act.wait_ge(copied, 4 * S)

                @block.vector
                def _(v):
                    st = Steps(v, v_step)
                    for s in range(S):
                        ready(v, st, Q, s, copied, readied)
                        normalise(v, st, Q, s, rk_exped)

        def stage_memories(Q, j, Qn, jn):
            names, other = pool.stage()
            (taken, made, copied, turned, in_sbuf, kept, projected, acted, shifted, g_made, dots, weighted, summed,
             corrected, read_ready, h_made, v_step, readied, rk_exped) = (next(names) for _ in range(19))
            qk, q_, k_, rk = Q[:, :, 0:2 * C], Q[:, :, 0:C], Q[:, :, C:2 * C], Q[:, :, 2 * C:3 * C]
            vv, v_, rv = Q[:, :, 3 * C:5 * C], Q[:, :, 3 * C:4 * C], Q[:, :, 4 * C:5 * C]
            betas = Q[:, :, 5 * C:NE]
            hs = q_
            with nc.Block(no_gpsimd_drain=True) as block:
                @block.sync
                def _(sync):
                    pool.clear(sync, other)

                @block.scalar
                def _(act):
                    if Qn is not None:
                        take(act, jn, taken)
                    act.activation(betas, betas, ACT.Sigmoid).then_inc(acted, 1)

                    def to_sbuf(t):
                        act.wait_ge(h_made, t + 1)
                        act.activation(hs[:, t], h_bank(t), ACT.Copy).then_inc(in_sbuf, 1)

                    def keep_turned(t):
                        act.wait_ge(turned, t + 1)
                        if t >= 2:
                            act.wait_ge(projected, t - 1)
                        act.activation(hT[:, t % 2].rearrange("p k t -> p (k t)"),
                                       ps[:, t % 3, C:2 * C], ACT.Copy).then_inc(kept, 1)

                    for t in range(S):
                        if t >= 1:
                            act.wait_ge(shifted, t)
                            act.activation(qs[:, :], qs[:, :], ACT.Exp).then_inc(acted, 1)
                            to_sbuf(t - 1)
                        if t >= 1 and Qn is not None:
                            exp_rk(act, Qn, t - 1, readied, rk_exped)
                        if Qn is not None:
                            keep(act, Qn, t, made, copied, readied)
                        if t >= 2:
                            keep_turned(t - 2)
                    if Qn is not None:
                        exp_rk(act, Qn, S - 1, readied, rk_exped)
                    to_sbuf(S - 1)
                    keep_turned(S - 2)
                    keep_turned(S - 1)

                @block.gpsimd
                def _(g):
                    def products(t):
                        if t >= 1:
                            g.wait_ge(g_made, t)
                        g.tensor_tensor(QK_PROD[:, 0:t + 1].rearrange("p s (n c) -> p s n c", n=2),
                                        bcast(k_[:, 0:t + 1], 2, 2),
                                        bcast(qk[:, t].rearrange("p (n c) -> p n c", n=2), 1, t + 1),
                                        ALU.mult).then_inc(dots, 1)
                        if t:
                            g.tensor_tensor(RK_PROD[:, 0:t], rk[:, 0:t], bcast(rk[:, t], 1, t),
                                            ALU.mult).then_inc(dots, 1)

                    def weigh_old(t):
                        g.wait_ge(g_made, t + 1)
                        if t >= 2:
                            g.wait_ge(summed, 2 * (t - 1))
                        g.tensor_tensor(heads(M[:, 0:t]), heads(vv[:, 0:t]),
                                        bcast(G[:, 0:t, t, 1:3].rearrange("p s n h -> p s (n h)"), 3, DH),
                                        ALU.mult).then_inc(weighted, 1)

                    def weigh_read(t):
                        g.wait_ge(corrected, t + 1)
                        if t:
                            g.wait_ge(summed, 2 * t - 1)
                        g.tensor_tensor(heads(MZ[:, 0:t + 1]), heads(v_[:, 0:t + 1]),
                                        bcast(G[:, 0:t + 1, t, 0], 3, DH), ALU.mult).then_inc(weighted, 1)

                    products(0)
                    products(1)
                    for t in range(S):
                        if t + 2 < S:
                            products(t + 2)
                        weigh_read(t)
                        if t + 1 < S:
                            weigh_old(t + 1)

                @block.tensor
                def _(pe):
                    def sum_old(t):
                        pe.wait_ge(weighted, 2 * t)
                        for s in range(t):
                            mm = pe.matmul(ps[:, AB_BANK], ident, M[:, s], start=(s == 0), stop=(s == t - 1))
                        mm.then_inc(summed, 1)

                    def sum_read(t):
                        pe.wait_ge(weighted, 2 * t + 1)
                        if t >= 3:
                            pe.wait_ge(kept, t - 2)
                            pe.wait_ge(shifted, t - 2)
                        for s in range(t + 1):
                            mm = pe.matmul(h_bank(t), ident, MZ[:, s], start=(s == 0), stop=False)
                        mm.then_inc(summed, 1)

                    def sum_recurrent(t):
                        pe.wait_ge(read_ready, t + 1)
                        for s in range(t + 1):
                            mm = pe.matmul(h_bank(t), ident, H_PROD[:, s], start=False, stop=(s == t))
                        mm.then_inc(h_made, 1)

                    def turn(t):
                        pe.wait_ge(in_sbuf, t + 1)
                        for k in range(2):
                            at = C + P * k
                            mm = pe.transpose(ps[:, t % 3, at:at + P], hs[:, t, P * k:P * (k + 1)], ident)
                        mm.then_inc(turned, 1)

                    def out(t):
                        pe.wait_ge(kept, t + 1)
                        b4, h = slot[t]
                        at = P * b4 + D * h
                        for k in range(2):
                            mm = pe.matmul(ps[:, OUT_BANK, at:at + D], hT[:, t % 2, k], wo[:, k], start=(k == 0),
                                           stop=(k == 1))
                        mm.then_inc(projected, 1)

                    if Qn is not None:
                        pe.wait_ge(taken, 1)
                        project(pe, 0, made, copied, readied)
                    for t in range(S):
                        sum_read(t)
                        sum_recurrent(t)
                        if t >= 1:
                            turn(t - 1)
                        if Qn is not None and t + 1 < S:
                            project(pe, t + 1, made, copied, readied)
                        if t + 1 < S:
                            sum_old(t + 1)
                        if t >= 2:
                            out(t - 2)
                    turn(S - 1)
                    out(S - 2)
                    out(S - 1)

                @block.vector
                def _(v):
                    st = Steps(v, v_step)

                    def tt(out, a, b, op):
                        st.do(v.tensor_tensor(out, a, b, op))

                    def sum_dots(t):
                        v.wait_ge(dots, max(2 * t, 1))
                        qk_dots = v.tensor_reduce(G[:, 0:t + 1, t, 0:2].rearrange("p s n h -> p s (n h)"),
                                                  heads(QK_PROD[:, 0:t + 1]), AX, ALU.add)
                        if t:
                            st.do(qk_dots)
                            v.wait_ge(dots, 2 * t + 1)
                            st.tell(v.tensor_reduce(G[:, 0:t, t, 2], heads(RK_PROD[:, 0:t]), AX, ALU.add), g_made, "g")
                        else:
                            st.tell(qk_dots, g_made, "g")

                    def correct(t):
                        if t:
                            v.wait_ge(summed, 2 * t)
                            tt(vv[:, t], vv[:, t], ps[:, AB_BANK], ALU.subtract)
                        st.tell(v.tensor_tensor(heads(vv[:, t]), heads(vv[:, t]), bcast(betas[:, t], 2, DH),
                                                ALU.mult), corrected, "corrected")

                    sum_dots(0)
                    v.wait_ge(acted, 1)
                    sum_dots(1)
                    for t in range(S):
                        if t == 0:
                            st.do(v.memset(qs[:, :], 1.0))
                        else:
                            v.wait_ge(h_made, t)
                            h = heads(h_bank(t - 1))
                            st.do(v.tensor_reduce(hm[:, 0], h, AX, ALU.max))
                            st.tell(v.tensor_tensor(heads(qs[:, :]), h, bcast(hm[:, 0], 2, DH), ALU.subtract),
                                    shifted, "shifted")
                            v.wait_ge(acted, 1 + t)
                        st.do(v.tensor_reduce(hm[:, 1], heads(qs[:, :]), AX, ALU.add))
                        st.go(v.reciprocal(hm[:, 1], hm[:, 1]))
                        tt(H_PROD[:, 0:t + 1], rk[:, 0:t + 1], bcast(qs[:, :], 1, t + 1), ALU.mult)
                        g = GQ[:, 0:t + 1]
                        st.do(v.tensor_reduce(g, heads(H_PROD[:, 0:t + 1]), AX, ALU.add))
                        tt(g, g, bcast(hm[:, 1], 1, t + 1), ALU.mult)
                        correct(t)
                        st.tell(v.tensor_tensor(heads(H_PROD[:, 0:t + 1]), heads(rv[:, 0:t + 1]), bcast(g, 3, DH),
                                                ALU.mult), read_ready, "read")
                        if Qn is not None:
                            ready(v, st, Qn, t, copied, readied)
                        if t + 2 < S:
                            sum_dots(t + 2)
                        if t >= 1 and Qn is not None:
                            normalise(v, st, Qn, t - 1, rk_exped)
                    if Qn is not None:
                        normalise(v, st, Qn, S - 1, rk_exped)
                    v.wait_ge(projected, S)
                    hh = H[:, bass.ds(j, 1)].rearrange("p o c -> p (o c)")
                    st.do(v.scalar_tensor_tensor(out=hh, in0=hh, scalar=2.0, in1=ps[:, OUT_BANK], op0=ALU.mult,
                                                 op1=ALU.add))

        stage_project(QKV[0])
        pool.open_loop()
        with nc.Fori(0, NB // 2 - 1) as pair:
            stage_memories(QKV[0], pair * 2, QKV[1], pair * 2 + 1)
            stage_memories(QKV[1], pair * 2 + 1, QKV[0], pair * 2 + 2)
            pool.even(nc)
        stage_memories(QKV[0], NB - 2, QKV[1], NB - 1)
        stage_memories(QKV[1], NB - 1, None, None)



def stage_store(nc, pool, H, out):
    names, other = pool.stage()
    stored = next(names)
    with nc.Block() as block:
        @block.sync
        def _(sync):
            pool.clear(sync, other)
            for b in range(B):
                at = P * (b % HALF) + D * (b // HALF)
                sync.dma_start(out[b].rearrange("(j p) d -> p j d", p=P), H[:, :, at:at + D]).then_inc(stored, 16)
            sync.wait_ge(stored, 16 * B)


def tower(nc, K, out):
    with ExitStack() as ctx:
        def sb(name, shape):
            return ctx.enter_context(nc.sbuf_tensor(name, shape, F32))

        H, X, XF = sb("H", [P, NB, W]), sb("X", [P, NB, W]), sb("XF", [P, HALF, LF])
        stats, ident_t, fold = sb("stats", [P, 2 * NB * B]), sb("ident", [P, P]), sb("fold_halves", [P, D])
        ps = ctx.enter_context(nc.psum_tensor("ps", [P, 8, 512], F32))
        pool = Pool2(nc, ctx)
        K = dict(K)
        stage_load(nc, pool, [(ident_t[:, :], K["ident"]), (fold[:, :], K["fold_halves"])])
        ident = K["ident"] = ident_t[:, :]
        K["fold_halves"] = fold[:, :]
        stage_zero_pads(nc, pool, XF)

        stage_patches(nc, pool, K, H, K["x"], ps)
        stage_attention(nc, pool, K, H, ps)
        with ExitStack() as inner:
            T = inner.enter_context(nc.sbuf_tensor("T0", [P, NB, W], F32))
            stage_layernorm(nc, pool, H, H, stats, T)
            stage_to_features(nc, pool, H, XF, ident, ps)
            stage_routed(nc, pool, K, H, XF, ps)
            stage_layernorm(nc, pool, H, H, stats, T)
        with ExitStack() as inner:
            def sb2(name, shape):
                return inner.enter_context(nc.sbuf_tensor(name, shape, F32))

            T, U, S, KH = sb2("T", [P, 12, W]), sb2("U", [P, NB, W]), sb2("S", [P, 16, W]), sb2("KH", [P, NF, 3, D])
            MF, MI = sb2("MF", [P, 3 * NF, P]), sb2("MI", [P, 3 * NF, P])
            matrices = [(m[:, :, :], K[k].rearrange("p (a b) -> p a b", b=P)) for m, k in ((MF, "fwd"), (MI, "inv"))]
            stage_load(nc, pool, matrices)
            stages_state_space(nc, pool, K, H, X, XF, U, S, T, KH, MF, MI, stats, ident, ps)
        with ExitStack() as inner:
            T = inner.enter_context(nc.sbuf_tensor("T1", [P, NB, W], F32))
            stage_to_features(nc, pool, H, XF, ident, ps)
            stages_moe(nc, pool, K, "m1_", H, XF, ident, ps, 4, True, 2.0)
            stage_layernorm(nc, pool, H, H, stats, T)
        with ExitStack() as inner:
            def sb3(name, shape):
                return inner.enter_context(nc.sbuf_tensor(name, shape, F32))

            T, U, S, KH = sb3("T_", [P, 12, W]), sb3("U_", [P, NB, W]), sb3("S_", [P, 16, W]), sb3("KH_", [P, NF, 3, D])
            MF, MI = sb3("MF_", [P, 3 * NF, P]), sb3("MI_", [P, 3 * NF, P])
            matrices = [(m[:, :, :], K[k].rearrange("p (a b) -> p a b", b=P)) for m, k in ((MF, "fwd"), (MI, "inv"))]
            stage_load(nc, pool, matrices)
            stages_hyena(nc, pool, K, H, X, XF, U, S, T, KH, MF, MI, stats, ident, ps)
        with ExitStack() as inner:
            T = inner.enter_context(nc.sbuf_tensor("T2", [P, NB, W], F32))
            gb = inner.enter_context(nc.sbuf_tensor("gb3", [P, 2], F32))
            stage_to_features(nc, pool, H, XF, ident, ps)
            stages_mean_gated(nc, pool, K, H, XF, ident, ps)
            stage_layernorm(nc, pool, H, H, stats, T)
            stages_fast_weights(nc, pool, K, H, X, XF, stats, T, ident, ps)
            stage_layernorm(nc, pool, H, H, stats, T)
            stage_load(nc, pool, [(gb[:, :], K["m3_gb"])])
            stage_layernorm(nc, pool, H, X, stats, T)
            stage_to_features(nc, pool, X, XF, ident, ps, gain=gb[:, 0:1], bias=gb[:, 1:2])
            stages_moe(nc, pool, K, "m3_", H, XF, ident, ps, 8, False, 1.0)
            stage_layernorm(nc, pool, H, H, stats, T)
        stage_store(nc, pool, H, out)



def block_diagonal(a):
    k, n = a.shape[-2:]
    out = np.zeros(a.shape[:-2] + (2 * k, 2 * n), a.dtype)
    out[..., :k, :n], out[..., k:, n:] = a, a
    return out


def constants():
    f32 = np.float32
    c = {}
    c["ident"] = np.eye(P, dtype=f32)
    c["fold_halves"] = np.concatenate([np.eye(D), np.eye(D)]).astype(f32)
    f, p = np.arange(9)[:, None], np.arange(16)[None, :]
    a = 2 * np.pi * ((f * p) % 16) / 16
    c["tok_dft"] = (np.concatenate([np.cos(a), -np.sin(a)]) / 4).astype(f32)
    c["fwd"], c["inv"] = transform_constants()
    attention_constants(c)
    state_constants(c)
    moe_constants(c)
    hyena_constants(c)
    return c


def lay_out(i):
    o = {}
    w = i["L0_tok_W"].reshape(D, 2 * 9, D).transpose(1, 0, 2)
    o["tok_W"] = np.concatenate([w, w], 2)
    o["x"] = i["x"]
    attention_layout(i, o)
    routed_layout(i, o)
    state_layout(i, o)
    moe1_layout(i, o)
    hyena_layout(i, o)
    mean_gated_layout(i, o)
    fast_weights_layout(i, o)
    return o


def rope_tables():
    half = 8
    theta = (np.float32(1.0) / np.float32(10000.0) ** (np.arange(half, dtype=np.float32) / np.float32(half)))
    a = np.arange(L, dtype=np.float32)[None, :] * theta.astype(np.float32)[:, None]
    cos, sin = np.ones((D, L), np.float32), np.zeros((D, L), np.float32)
    cos[48::2], cos[49::2] = np.cos(a), np.cos(a)
    sin[48::2], sin[49::2] = -np.sin(a), np.sin(a)
    t = np.stack([cos, sin], 1)
    return np.concatenate([t, t]).astype(np.float32)


def attention_constants(c):
    c["at_rope"] = rope_tables()
    c["at_mask"] = np.triu(np.full((P, P), -1e30, np.float32), 1)


def attention_layout(i, o):
    swap = np.arange(D)
    swap[48::2], swap[49::2] = np.arange(49, D, 2), np.arange(48, D, 2)
    q = np.concatenate([i["L0_attn_Wqc"], i["L0_attn_Wqr"]], 1)
    k = np.concatenate([i["L0_attn_Wkc"], i["L0_attn_Wkr"]], 1)
    o["at_wl"] = np.stack([block_diagonal(i["L0_attn_Wq_comp"].T), block_diagonal(i["L0_attn_Wkv_comp"].T)], 1)
    o["at_wr"] = np.stack([block_diagonal(m) for m in (q, q[:, swap], k, k[:, swap], i["L0_attn_Wv"])], 1)


def halves(a):
    z = np.zeros_like(a)
    return np.stack([np.concatenate([a, z]), np.concatenate([z, a])], 1)


def routed_layout(i, o):
    wr, br = i["L0_ffn_Wr"], i["L0_ffn_br"]
    w = np.concatenate([wr.transpose(0, 1, 3, 2), br[..., None]], 3)
    w = np.concatenate([w, np.zeros_like(w[:, :1])], 1)
    o["f0_wr"] = w.reshape(-1, 128, 129)
    o["f0_route"] = i["L0_ffn_route_id"].reshape(1, 64)
    o["f0_wi"] = halves(i["L0_ffn_Wi"].T)
    o["f0_ws"] = i["L0_ffn_Ws"][:, 0].transpose(2, 0, 1)
    o["f0_wo"] = i["L0_ffn_Wo"].T
    o["f0_bi"], o["f0_bs"] = i["L0_ffn_bi"][:, None], i["L0_ffn_bs"][:, 0].T
    o["f0_bo"] = i["L0_ffn_bo"]


def state_constants(c):
    c["s4_lv"] = np.tile(np.arange(P, dtype=np.float32), (P, 1))
    c["s4_jv"] = np.tile(P * np.arange(NB, dtype=np.float32), (P, 1))
    cos_rows = (np.arange(P) < D).astype(np.float32)
    ph, ph2 = 0.25 * cos_rows, 0.25 * (1 - cos_rows)
    a = 0.25 * 6.2831845
    c["s4_cols"] = np.stack([ph, ph2, 2 * cos_rows - 1, a * cos_rows, a * (1 - cos_rows),
                             np.full(P, a)], 1).astype(np.float32)


def state_layout(i, o):
    n = 4
    dt = np.broadcast_to(i["L1_attn_log_dt"][:, None, :], (n, D, D))
    par = [dt] + [i["L1_attn_" + k].transpose(0, 2, 1) for k in ("Alog", "Aim", "Cre", "Cim")]
    par = np.stack(par, 2)
    o["s4_par"] = np.concatenate([par, par], 1)
    o["s4_D"] = i["L1_attn_D"]
    w, b = i["L1_attn_Wout"], i["L1_attn_bout"]
    w1, w2 = (block_diagonal(w[:, D * k:D * (k + 1)].transpose(0, 2, 1)) for k in range(2))
    o["s4_wout"] = np.concatenate([w1, w2], 2)
    o["s4_bout"] = np.concatenate([b[:, :D], b[:, :D], b[:, D:], b[:, D:]], 1)
    o["s4_gb"] = np.stack([i["L1_attn_ln_scale"], i["L1_attn_ln_bias"]], 1)


def to_half(a):
    z = np.zeros_like(a)
    return np.stack([np.concatenate([a, z], 1), np.concatenate([z, a], 1)], 1)


def spread(per):
    s = np.zeros((P, 2, 8 // per, P), np.float32)
    for h in range(2):
        for e in range(8):
            w = P // per
            s[h * 8 + e, h, e // per, w * (e % per):w * (e % per + 1)] = 1
    return s


def experts_layout(o, pre, w1, b1, w2, b2):
    k = w1.shape[2]
    per = P // k
    nq = 8 // per
    a = w1.reshape(nq, per, D, k).transpose(0, 2, 1, 3).reshape(nq, D, P)
    o[pre + "w1"] = np.stack([halves(m) for m in a], 2)
    o[pre + "w2"] = np.stack([to_half(m) for m in w2.reshape(nq, P, D)], 2)
    o[pre + "b1"] = b1.reshape(nq, P).T
    z = np.zeros((P, P), np.float32)
    z[0:8, 0:D], z[8:16, D:] = b2, b2
    o[pre + "b2"] = z


def moe1_layout(i, o):
    experts_layout(o, "m1_", i["L1_ffn_w1"], i["L1_ffn_b1"], i["L1_ffn_w2"], i["L1_ffn_b2"])
    o["m1_router"] = block_diagonal(i["L1_ffn_router_w"].T)
    experts_layout(o, "m3_", i["L3_ffn_W1"], i["L3_ffn_b1"], i["L3_ffn_W2"], i["L3_ffn_b2"])
    o["m3_router"] = block_diagonal(i["L3_ffn_Wr"])
    o["m3_rb"] = i["L3_ffn_br"]
    o["m3_gb"] = np.stack([np.tile(i["L3_ffn_gamma"], 2), np.tile(i["L3_ffn_beta"], 2)], 1)


def moe_constants(c):
    c["rank"] = np.tile(np.arange(8, 0, -1, dtype=np.float32), (P, 1))
    c["m1_sel"], c["m3_sel"] = spread(2), spread(1)


def hyena_constants(c):
    f32 = np.float32
    t01 = np.linspace(0.0, 1.0, L).astype(f32)
    tr = np.linspace(0.0, float(L - 1), L).astype(f32)
    ang = (f32(2.0 * np.pi / L) * tr * f32(0.0001)).astype(f32)
    c["hy_z"] = np.stack([t01, np.cos(ang), -np.sin(ang)]).astype(f32)
    deltas = np.linspace(math.log(0.01) / 1.5, math.log(0.01) / 0.3, D).astype(f32)
    decay = np.exp(-t01[:, None] * np.abs(deltas)).astype(f32)
    c["hy_decay"] = decay.reshape(NB, P, D).transpose(1, 0, 2).reshape(P, -1)
    p = np.arange(P)
    c["hw_edge"] = np.stack([p >= 1, p >= 2, p < P - 1, p >= 0], 1).astype(f32)


def hyena_layout(i, o):
    g = {k[8:]: v for k, v in i.items() if k.startswith("L2_attn_")}
    o["hy_w0"] = g["mlp_w0"].T
    o["hy_w12"] = np.stack([g["mlp_w1"].T, g["mlp_w2"].T], 1)
    o["hy_w3"] = g["mlp_w3"].T
    o["hy_bf"] = np.stack([g["mlp_b0"], g["mlp_b1"], g["mlp_b2"], g["sin_freq"]], 1)
    o["hy_fb"] = g["filt_bias"][None]
    o["hy_gb"] = np.stack([np.tile(g["ln_g"], 2), np.tile(g["ln_b"], 2)], 1)

    def both(a):
        a = a.reshape(a.shape[:-1] + (3, 1, D))
        return np.concatenate([a, a], -2).reshape(a.shape[:-3] + (3 * P,))

    w = [block_diagonal(g["in_w"][D * k:D * (k + 1)].T) for k in range(3)]
    o["hw_w"] = np.concatenate(w, 1)
    o["hw_wo"] = block_diagonal(g["out_w"].T)
    o["hw_taps"] = both(np.ascontiguousarray(g["sf_w"][:, 0].T))
    o["hw_otaps"] = np.tile(g["conv_w"][:, 0].T, (1, 2))
    o["hw_rows"] = both(np.stack([g["in_b"], g["sf_b"]]))
    o["hw_orow"] = np.tile(g["out_b"], 2)


def mean_gated_layout(i, o):
    g = {k[7:]: v for k, v in i.items() if k.startswith("L2_ffn_")}
    experts_layout(o, "f2_", g["W1"], g["b1"], g["Wo"], g["bo"])
    z = np.zeros((P, P), np.float32)
    z[0:8] = np.tile(g["bo"], (1, 2))
    o["f2_b2"] = z
    o["f2_wr"], o["f2_br"] = np.tile(g["Wr"], (2, 1)), g["br"]
    w = g["W2"].reshape(4, 2, D, D)
    wm = np.zeros((P, 4, P), np.float32)
    for k in range(2):
        wm[D * k:D * (k + 1), :, D * k:D * (k + 1)] = w[:, k].transpose(1, 0, 2)
    o["f2_wm"] = wm
    o["f2_bn"] = np.stack([np.stack([g[k + n].reshape(4, P).T for k in ("b", "g", "be", "m", "v")], 1)
                           for n in "12"], 1)


def fast_weights_layout(i, o):
    g = {k[8:]: v for k, v in i.items() if k.startswith("L3_attn_")}
    w = g["slow_W"].reshape(8, 162, D)
    w = np.concatenate([w[:, 32 * n:32 * (n + 1)].reshape(-1, D) for n in (0, 1, 3, 2, 4)] + [w[:, 160], w[:, 161]])
    o["fw_wq"] = halves(w.T)
    o["fw_wo"] = g["out_W"].T.reshape(2, P, D).transpose(1, 0, 2)
    o["fw_gb"] = np.stack([np.tile(g["ln_g"], 2), np.tile(g["ln_b"], 2)], 1)




def kernel(**inputs):
    import concourse.bacc as _bacc
    from concourse.bass_utils import run_bass_kernel_spmd as _run

    nc = _bacc.Bacc("TRN2", target_bir_lowering=False, num_devices=1)
    host = lay_out({k: np.asarray(v) for k, v in inputs.items()})
    host.update(constants())
    arrays, K = {}, {}
    for name, a in host.items():
        a = np.ascontiguousarray(a)
        arrays["in_" + name] = a
        K[name] = nc.dram_tensor("in_" + name, a.shape, mybir.dt.from_np(a.dtype), kind="ExternalInput").ap()
    out = nc.dram_tensor("out_0", (B, L, D), F32, kind="ExternalOutput").ap()
    tower(nc, K, out)
    r = _run(nc, [arrays], core_ids=[0])
    return r.results[0]["out_0"]
```

```python
from contextlib import ExitStack
import math
import numpy as np
import concourse.bass as bass
from concourse import mybir
from concourse.alu_op_type import AluOpType as ALU

F32 = mybir.dt.float32
I32 = mybir.dt.int32
BF16 = mybir.dt.bfloat16
ACT = mybir.ActivationFunctionType
AX = mybir.AxisListType.X

B, L, D = 8, 1024, 64
P = 128
NB = L // P
HALF = B // 2
W = B * D
EPS = 1e-5
PAD = 2
LF = PAD + L + 2
NF = NB + 1
FORDER = [4, 0, 8, 2, 6, 1, 7, 5, 3]
SLOT = {0: 0, 8: 1, 4: 2, 2: 4, 6: 6, 1: 8, 5: 10, 7: 12, 3: 14}
REAL = (0, 8)
NEGATED = (4, 2, 1, 5)


def bcast(ap, axis, n):
    a = ap.unsqueeze(axis)
    shape = list(a.shape)
    shape[axis] = n
    return a.broadcast_to(shape)


def transform_constants():
    fwd, inv = np.zeros((P, 3 * NF, P)), np.zeros((P, 3 * NF, P))
    t, f2 = np.arange(P)[:, None], np.arange(P)[None, :]
    for f in range(NF):
        a = 2 * np.pi * ((t * (f + 2 * NB * f2)) % (2 * L)) / (2 * L)
        c, s = np.cos(a), np.sin(a)
        sign = -1.0 if f in NEGATED else 1.0
        fwd[:, 3 * f], fwd[:, 3 * f + 1], fwd[:, 3 * f + 2] = c, -s, (-c if sign < 0 else s)
        scale = (1.0 if f in REAL else 2.0) / (2 * L)
        inv[:, 3 * f], inv[:, 3 * f + 1], inv[:, 3 * f + 2] = c.T * scale, -s.T * scale, s.T * scale
    return fwd.reshape(P, -1).astype(np.float32), inv.reshape(P, -1).astype(np.float32)


class Pool2:

    def __init__(self, nc, ctx, size=19):
        self.nc = nc
        self.sets = [[ctx.enter_context(nc.semaphore(f"set{k}_{i}")) for i in range(size)] for k in range(2)]
        self.turn = 0
        self.tensors = 0

    def fresh(self):
        self.tensors += 1
        return self.tensors

    def open_loop(self):
        self.at = self.turn

    def even(self, nc):
        if self.turn != self.at:
            names, other = self.stage()
            with nc.Block(no_gpsimd_drain=True) as block:
                @block.sync
                def _(sync):
                    self.clear(sync, other)

    def stage(self):
        mine, other = self.sets[self.turn], self.sets[1 - self.turn]
        self.turn = 1 - self.turn
        return iter(mine), other

    def clear(self, sync, other):
        for s in other:
            sync.sem_clear(s)


class Steps:

    def __init__(self, eng, own):
        self.eng, self.own, self.n, self.counts = eng, own, 0, {}

    def do(self, ins):
        ins.then_inc(self.own, 1)
        self.n += 1
        self.eng.wait_ge(self.own, self.n)

    def go(self, ins):
        ins.then_inc(self.own, 1)
        self.n += 1

    def join(self):
        self.eng.wait_ge(self.own, self.n)

    def tell(self, ins, sem, key):
        ins.then_inc(sem, 1)
        self.counts[key] = self.counts.get(key, 0) + 1
        self.eng.wait_ge(sem, self.counts[key])



def scale_for_fold(act, U, S, w, scaled):
    for n, j in enumerate((1, 3)):
        co, si = math.cos(math.pi * j / 8), math.sin(math.pi * j / 8)
        for k, scale in enumerate((-si, co)):
            act.activation(S[:, 8 + 2 * n + k, 0:w], U[:, 4 + j, 0:w], ACT.Copy, scale=scale).then_inc(scaled, 1)


class Fold:

    def __init__(self, v, st, U, S, T, w, fwd_ready, scaled):
        self.v, self.st, self.fwd_ready, self.scaled = v, st, fwd_ready, scaled
        self.u, self.s, self.t = U[:, :, 0:w], S[:, :, 0:w], T[:, :, 0:w]

    def tt(self, out, a, b, op):
        return self.v.tensor_tensor(out, a, b, op)

    def fma(self, out, a, k, b):
        return self.v.scalar_tensor_tensor(out=out, in0=a, scalar=float(k), in1=b, op0=ALU.mult, op1=ALU.add)

    def ready(self, ins):
        self.st.tell(ins, self.fwd_ready, "f")

    def residues_4_0_8(self):
        st, tt, u, s, t = self.st, self.tt, self.u, self.s, self.t
        st.go(tt(t[:, 0:4], u[:, 0:4], u[:, 4:8], ALU.add))
        st.do(tt(t[:, 4:8], u[:, 0:4], u[:, 4:8], ALU.subtract))
        st.go(tt(t[:, 8:10], t[:, 0:2], t[:, 2:4], ALU.add))
        self.ready(tt(s[:, 2:4], t[:, 0:2], t[:, 2:4], ALU.subtract))
        st.join()
        self.ready(tt(s[:, 0], t[:, 8], t[:, 9], ALU.add))
        self.ready(tt(s[:, 1], t[:, 8], t[:, 9], ALU.subtract))

    def residues_2_6(self):
        st, tt, fma, s, t, c8 = self.st, self.tt, self.fma, self.s, self.t, math.sqrt(0.5)
        st.go(tt(t[:, 8], t[:, 5], t[:, 7], ALU.subtract))
        st.do(tt(t[:, 9], t[:, 5], t[:, 7], ALU.add))
        st.go(fma(s[:, 4], t[:, 8], c8, t[:, 4]))
        st.go(fma(s[:, 6], t[:, 8], -c8, t[:, 4]))
        st.join()
        self.ready(fma(s[:, 5], t[:, 9], c8, t[:, 6]))
        self.ready(fma(s[:, 7], t[:, 9], -c8, t[:, 6]))

    def rotate(self):
        st, fma, u, s, t, c8 = self.st, self.fma, self.u, self.s, self.t, math.sqrt(0.5)
        st.go(fma(t[:, 8], t[:, 6], c8, u[:, 0]))
        st.go(fma(t[:, 9], t[:, 2], c8, u[:, 4]))
        st.go(fma(t[:, 0], t[:, 6], -c8, u[:, 0]))
        st.go(fma(t[:, 4], t[:, 2], -c8, u[:, 4]))
        self.v.wait_ge(self.scaled, 4)
        for n, j in enumerate((1, 3)):
            co, si = math.cos(math.pi * j / 8), math.sin(math.pi * j / 8)
            st.go(fma(t[:, j], u[:, j], co, s[:, 8 + 2 * n]))
            st.go(fma(t[:, 4 + j], u[:, j], si, s[:, 9 + 2 * n]))
        st.join()

    def residues_1_7(self):
        st, tt, s, t = self.st, self.tt, self.s, self.t
        st.go(tt(t[:, 10:12], t[:, 1:6:4], t[:, 3:8:4], ALU.add))
        st.do(tt(t[:, 3:8:4], t[:, 1:6:4], t[:, 3:8:4], ALU.subtract))
        self.ready(tt(s[:, 8:10], t[:, 8:10], t[:, 10:12], ALU.add))
        self.ready(tt(s[:, 12:14], t[:, 8:10], t[:, 10:12], ALU.subtract))

    def residues_5_3(self):
        st, tt, s, t = self.st, self.tt, self.s, self.t
        st.go(tt(s[:, 10], t[:, 0], t[:, 7], ALU.subtract))
        st.join()
        self.ready(tt(s[:, 11], t[:, 4], t[:, 3], ALU.add))
        st.go(tt(s[:, 14], t[:, 0], t[:, 7], ALU.add))
        st.join()
        self.ready(tt(s[:, 15], t[:, 4], t[:, 3], ALU.subtract))


class Unfold:

    def __init__(self, v, st, U, S, T):
        self.v, self.st, self.U, self.S, self.T = v, st, U, S, T

    def tt(self, out, a, b, op):
        return self.v.tensor_tensor(out, a, b, op)

    def fma(self, out, a, k, b):
        return self.v.scalar_tensor_tensor(out=out, in0=a, scalar=float(k), in1=b, op0=ALU.mult, op1=ALU.add)

    def even_pairs(self):
        st, tt, S, T = self.st, self.tt, self.S, self.T
        st.go(tt(T[:, 0], S[:, 0], S[:, 1], ALU.add))
        st.go(tt(T[:, 1], S[:, 0], S[:, 1], ALU.subtract))
        st.go(tt(T[:, 6], S[:, 4], S[:, 6], ALU.subtract))
        st.go(tt(T[:, 7], S[:, 5], S[:, 7], ALU.add))
        st.go(tt(T[:, 8], S[:, 4], S[:, 6], ALU.add))
        st.do(tt(T[:, 9], S[:, 7], S[:, 5], ALU.subtract))

    def even_fours(self):
        st, tt, S, T = self.st, self.tt, self.S, self.T
        st.go(tt(T[:, 2], T[:, 0], S[:, 2], ALU.add))
        st.go(tt(T[:, 4], T[:, 0], S[:, 2], ALU.subtract))
        st.go(tt(T[:, 3], T[:, 1], S[:, 3], ALU.subtract))
        st.go(tt(T[:, 5], T[:, 1], S[:, 3], ALU.add))
        st.go(tt(T[:, 10], T[:, 6], T[:, 7], ALU.subtract))
        st.do(tt(T[:, 11], T[:, 6], T[:, 7], ALU.add))

    def even_blocks(self):
        st, tt, fma, U, T, c8 = self.st, self.tt, self.fma, self.U, self.T, math.sqrt(0.5)
        st.go(tt(U[:, 0:3:2], T[:, 2:5:2], T[:, 8:10], ALU.add))
        st.go(tt(U[:, 4:7:2], T[:, 2:5:2], T[:, 8:10], ALU.subtract))
        st.go(fma(U[:, 1], T[:, 10], c8, T[:, 3]))
        st.go(fma(U[:, 5], T[:, 10], -c8, T[:, 3]))
        st.go(fma(U[:, 3], T[:, 11], -c8, T[:, 5]))
        st.do(fma(U[:, 7], T[:, 11], c8, T[:, 5]))

    def odd_1_7_pairs(self):
        st, tt, S, T = self.st, self.tt, self.S, self.T
        st.go(tt(T[:, 0], S[:, 8], S[:, 12], ALU.add))
        st.go(tt(T[:, 2], S[:, 8], S[:, 12], ALU.subtract))
        st.go(tt(T[:, 4], S[:, 9], S[:, 13], ALU.subtract))
        st.do(tt(T[:, 6], S[:, 9], S[:, 13], ALU.add))

    def odd_1_7_blocks(self):
        self.add_rotated(((0, 1, 4, 1), (2, 1, 6, 1), (0, 1, 4, 1), (2, 1, 6, 1)))

    def odd_5_3(self):
        st, tt, S, T = self.st, self.tt, self.S, self.T
        st.go(tt(T[:, 1], S[:, 10], S[:, 14], ALU.add))
        st.go(tt(T[:, 3], S[:, 10], S[:, 14], ALU.subtract))
        st.go(tt(T[:, 5], S[:, 11], S[:, 15], ALU.subtract))
        st.do(tt(T[:, 7], S[:, 11], S[:, 15], ALU.add))
        self.add_rotated(((1, 1, 5, 1), (7, -1, 3, 1), (1, -1, 5, -1), (7, 1, 3, -1)))

    def add_rotated(self, parts):
        st, tt, fma, U, T = self.st, self.tt, self.fma, self.U, self.T
        re, re_sign, im, im_sign = parts[0]
        st.go(tt(U[:, 0], U[:, 0], T[:, re], ALU.add if re_sign > 0 else ALU.subtract))
        st.go(tt(U[:, 4], U[:, 4], T[:, im], ALU.subtract if im_sign > 0 else ALU.add))
        for imaginary in (False, True):
            for j in (1, 2, 3):
                co, si = math.cos(math.pi * j / 8), math.sin(math.pi * j / 8)
                re, re_sign, im, im_sign = parts[j]
                if imaginary:
                    st.go(fma(U[:, j], T[:, im], -si * im_sign, U[:, j]))
                    st.go(fma(U[:, 4 + j], T[:, im], -co * im_sign, U[:, 4 + j]))
                else:
                    st.go(fma(U[:, j], T[:, re], co * re_sign, U[:, j]))
                    st.go(fma(U[:, 4 + j], T[:, re], -si * re_sign, U[:, 4 + j]))
            st.join()


def transform_residue(pe, M, f, S, w, out_re, out_im):
    c, ns, x = M[:, 3 * f], M[:, 3 * f + 1], M[:, 3 * f + 2]
    k = SLOT[f]
    if f in REAL:
        pe.matmul(out_re, c, S[:, k, 0:w], start=True, stop=True)
        return pe.matmul(out_im, ns, S[:, k, 0:w], start=True, stop=True)
    neg = f in NEGATED
    pe.matmul(out_re, c, S[:, k, 0:w], start=True, stop=False)
    pe.matmul(out_re, ns if neg else x, S[:, k + 1, 0:w], start=False, stop=True)
    pe.matmul(out_im, ns, S[:, k, 0:w], start=True, stop=False)
    return pe.matmul(out_im, x if neg else c, S[:, k + 1, 0:w], start=False, stop=True)


def inverse_residue(pe, M, f, Y, out_re, out_im):
    c, ns, s = M[:, 3 * f], M[:, 3 * f + 1], M[:, 3 * f + 2]
    yr, yi = Y[:, 0], Y[:, 1]
    pe.matmul(out_re, c, yr, start=True, stop=False)
    mm = pe.matmul(out_re, ns, yi, start=False, stop=True)
    if f not in REAL:
        pe.matmul(out_im, s, yr, start=True, stop=False)
        mm = pe.matmul(out_im, c, yi, start=False, stop=True)
    return mm


def stage_filter_spectrum(nc, pool, Kt, KH, S, T, M, ps):
    w = Kt.shape[2]
    names, other = pool.stage()
    dve_step, fwd_ready, spec_ready, spec_out, scaled = (next(names) for _ in range(5))
    with nc.Block(no_gpsimd_drain=True) as block:
        @block.sync
        def _(sync):
            pool.clear(sync, other)

        @block.vector
        def _(v):
            fold = Fold(v, Steps(v, dve_step), Kt, S, T, w, fwd_ready, scaled)
            fold.residues_4_0_8()
            fold.residues_2_6()
            fold.rotate()
            fold.residues_1_7()
            fold.residues_5_3()

        @block.tensor
        def _(pe):
            for n, f in enumerate(FORDER):
                pe.wait_ge(fwd_ready, n + 1)
                if n >= 4:
                    pe.wait_ge(spec_out, 3 * (n - 3))
                b = ps[:, 2 * (n % 4):2 * (n % 4) + 2]
                transform_residue(pe, M, f, S, w, b[:, 0, 0:w], b[:, 1, 0:w]).then_inc(spec_ready, 1)

        @block.scalar
        def _(act):
            scale_for_fold(act, Kt, S, w, scaled)
            for n, f in enumerate(FORDER):
                act.wait_ge(spec_ready, n + 1)
                b = ps[:, 2 * (n % 4):2 * (n % 4) + 2]
                for k, (part, sign) in enumerate(((1, -1.0), (0, 1.0), (1, 1.0))):
                    act.activation(KH[:, :, f, k, :], b[:, part, 0:w].rearrange("p (l d) -> p l d", d=D), ACT.Copy,
                                   scale=sign).then_inc(spec_out, 1)
            act.wait_ge(spec_out, 3 * NF)


def stage_long_conv(nc, pool, U, XF, KH, layer, S, T, MF, MI, ps):
    names, other = pool.stage()
    dve_step, fwd_ready, x_ready, scaled, multiplied, y_ready, g_ready, g_out = (next(names) for _ in range(8))
    X = [ps[:, 0:2], ps[:, 2:4]]
    G = [ps[:, 4:6], ps[:, 6:8]]

    def terms(n, part):
        return XF[:, 2 * (n % 2) + part, PAD:PAD + L].rearrange("p (k c) -> p k c", k=2)

    def product(n):
        f = FORDER[n]
        return terms(n, 0) if f in REAL else S[:, SLOT[f]:SLOT[f] + 2]

    with nc.Block(no_gpsimd_drain=True) as block:
        @block.sync
        def _(sync):
            pool.clear(sync, other)

        @block.vector
        def _(v):
            st = Steps(v, dve_step)
            fold, unfold = Fold(v, st, U, S, T, W, fwd_ready, scaled), Unfold(v, st, U, S, T)

            def multiply(n):
                v.wait_ge(x_ready, n + 1)
                if n >= 2:
                    v.wait_ge(y_ready, n - 1)
                for part in range(2):
                    x = bcast(X[n % 2][:, part].rearrange("p (g d) -> p g d", d=D), 1, 2)
                    lo = 1 - part
                    h = bcast(KH[:, bass.ds(layer, 1), FORDER[n], lo:lo + 2, :].rearrange("p o k d -> p (o k) d"), 2, 8)
                    v.tensor_tensor(terms(n, part).rearrange("p k (g d) -> p k g d", d=D), x, h,
                                    ALU.mult).then_inc(multiplied, 1)

            def need(n):
                v.wait_ge(g_out, sum(1 if f in REAL else 2 for f in FORDER[:n]))

            fold.residues_4_0_8()
            fold.residues_2_6()
            multiply(0)
            multiply(1)
            fold.rotate()
            multiply(2)
            multiply(3)
            fold.residues_1_7()
            multiply(4)
            fold.residues_5_3()
            multiply(5)
            need(5)
            unfold.even_pairs()
            multiply(6)
            unfold.even_fours()
            multiply(7)
            unfold.even_blocks()
            multiply(8)
            need(7)
            unfold.odd_1_7_pairs()
            unfold.odd_1_7_blocks()
            need(9)
            unfold.odd_5_3()
            v.wait_ge(multiplied, 2 * NF)

        @block.gpsimd
        def _(g):
            for n, f in enumerate(FORDER):
                g.wait_ge(multiplied, 2 * n + 2)
                g.tensor_tensor(product(n), terms(n, 0), terms(n, 1), ALU.add).then_inc(y_ready, 1)

        @block.tensor
        def _(pe):
            def inverse(n):
                f = FORDER[n]
                pe.wait_ge(y_ready, n + 1)
                if n >= 2:
                    pe.wait_ge(g_out, sum(1 if g in REAL else 2 for g in FORDER[:n - 1]))
                y, g = product(n), G[n % 2]
                inverse_residue(pe, MI, f, y, g[:, 0], g[:, 1]).then_inc(g_ready, 1)

            for n, f in enumerate(FORDER):
                pe.wait_ge(fwd_ready, n + 1)
                if n >= 2:
                    pe.wait_ge(multiplied, 2 * (n - 1))
                x = X[n % 2]
                transform_residue(pe, MF, f, S, W, x[:, 0], x[:, 1]).then_inc(x_ready, 1)
                if n >= 1:
                    inverse(n - 1)
            inverse(NF - 1)

        @block.scalar
        def _(act):
            scale_for_fold(act, U, S, W, scaled)
            for n, f in enumerate(FORDER):
                act.wait_ge(g_ready, n + 1)
                for part in range(1 if f in REAL else 2):
                    act.activation(S[:, SLOT[f] + part], G[n % 2][:, part], ACT.Copy).then_inc(g_out, 1)
            act.wait_ge(g_out, 2 * NB)



def load(sync, sem, pairs):
    for dst, src in pairs:
        sync.dma_start(dst, src).then_inc(sem, 16)
    return 16 * len(pairs)


def stage_load(nc, pool, pairs):
    names, other = pool.stage()
    loaded = next(names)
    with nc.Block(no_gpsimd_drain=True) as block:
        @block.sync
        def _(sync):
            pool.clear(sync, other)
            n = load(sync, loaded, pairs)
            sync.wait_ge(loaded, n)


def stage_layernorm(nc, pool, src, dst, stats, T, add=None, gain=None, bias=None, features=None):
    names, other = pool.stage()
    dve_step, centred, squared, var_ready, std_ready, normalised, turned, copied = (next(names) for _ in range(8))
    G = NB * B
    HB = NB // 2
    mean, var = stats[:, 0:G], stats[:, G:2 * G]

    def part(t, k):
        return t[:, HB * k:HB * (k + 1)].rearrange("p j (g d) -> p (j g) d", d=D)

    with nc.Block(no_gpsimd_drain=True) as block:
        @block.sync
        def _(sync):
            pool.clear(sync, other)

        @block.vector
        def _(v):
            st = Steps(v, dve_step)
            g = G // 2
            for k in range(2):
                x, y, m = part(src, k), part(dst, k), mean[:, g * k:g * (k + 1)]
                if add is not None:
                    st.do(v.tensor_tensor(dst[:, HB * k:HB * (k + 1)], src[:, HB * k:HB * (k + 1)],
                                          add[:, HB * k:HB * (k + 1)], ALU.add))
                    x = y
                st.do(v.tensor_reduce(m, x, AX, ALU.add))
                st.do(v.tensor_scalar(m, m, 1.0 / D, None, ALU.mult))
                st.tell(v.tensor_tensor(y, x, bcast(m, 2, D), ALU.subtract), centred, "c")
            for k in range(2):
                s = var[:, g * k:g * (k + 1)]
                v.wait_ge(squared, k + 1)
                st.do(v.tensor_reduce(s, part(T, k), AX, ALU.add))
                st.tell(v.tensor_scalar(s, s, 1.0 / D, EPS, ALU.mult, ALU.add), var_ready, "v")
            for k in range(2):
                y, s = part(dst, k), var[:, g * k:g * (k + 1)]
                v.wait_ge(std_ready, k + 1)
                st.do(v.reciprocal(s, s))
                st.tell(v.tensor_tensor(y, y, bcast(s, 2, D), ALU.mult), normalised, "n")
                if gain is not None:
                    st.do(v.tensor_tensor(y, y, bcast(gain, 1, g), ALU.mult))
                    st.do(v.tensor_tensor(y, y, bcast(bias, 1, g), ALU.add))

        @block.scalar
        def _(act):
            g = G // 2
            for k in range(2):
                act.wait_ge(centred, k + 1)
                act.activation(part(T, k), part(dst, k), ACT.Square).then_inc(squared, 1)
            for k in range(2):
                act.wait_ge(var_ready, k + 1)
                s = var[:, g * k:g * (k + 1)]
                act.activation(s, s, ACT.Sqrt).then_inc(std_ready, 1)
            act.wait_ge(std_ready, 2)
            if features is not None:
                XF, ident, ps, f_gain, f_bias = features
                copy_blocks(act, XF, ps, turned, copied, f_gain, f_bias)
                act.wait_ge(copied, NB)

        if features is not None:
            @block.tensor
            def _(pe):
                XF, ident, ps, f_gain, f_bias = features
                turn_blocks(pe, dst, ident, ps, turned, copied, ready=normalised, per=HB)


def turn_blocks(pe, X, ident, ps, turned, copied, ready=None, per=1):
    for j in range(NB):
        if ready is not None:
            pe.wait_ge(ready, j // per + 1)
        if j >= 4:
            pe.wait_ge(copied, j - 3)
        for b4 in range(HALF):
            mm = pe.transpose(ps[:, j % 4, P * b4:P * (b4 + 1)], X[:, j, P * b4:P * (b4 + 1)], ident)
        mm.then_inc(turned, 1)


def copy_blocks(act, XF, ps, turned, copied, gain=None, bias=None):
    for j in range(NB):
        act.wait_ge(turned, j + 1)
        out = XF[:, :, PAD + P * j:PAD + P * (j + 1)]
        src = ps[:, j % 4].rearrange("p (b t) -> p b t", b=HALF)
        if gain is None:
            act.activation(out, src, ACT.Copy).then_inc(copied, 1)
        else:
            act.activation(out, src, ACT.Identity, bias=bias, scale=gain).then_inc(copied, 1)





def stage_patches(nc, pool, K, H, x, ps):
    NT, TH, STEP, PATCH = 64, 72, 8, 16
    with ExitStack() as ctx:
        wt = ctx.enter_context(nc.sbuf_tensor("tok_wt", [2 * (PATCH // 2 + 1), D, 2 * D], F32))
        dft = ctx.enter_context(nc.sbuf_tensor("tok_dft", [2 * (PATCH // 2 + 1), PATCH], F32))
        w = ctx.enter_context(nc.sbuf_tensor("tok_w", [P, PATCH, P], F32))
        xt = ctx.enter_context(nc.sbuf_tensor("tok_x", [P, 2, TH, NT], F32))
        E = ctx.enter_context(nc.sbuf_tensor("tok_e", [P, 2, NT, PATCH], F32))
        names, other = pool.stage()
        w_in, zeroed, w_made, w_out, x_free, padded, summed, e_ready, row_ready, row_free = (
            next(names) for _ in range(10))
        x_in = [next(names), next(names)]
        with nc.Block(no_gpsimd_drain=True) as block:
            @block.sync
            def _(sync):
                pool.clear(sync, other)
                load(sync, w_in, [(wt[:, :, :], K["tok_W"]), (dft[:, :], K["tok_dft"])])
                with sync.Fori(0, HALF) as i:
                    for h in range(2):
                        sync.wait_ge(x_free, 2 * i + h + 1)
                        b = x[bass.ds(i + HALF * h, 1)].rearrange("o c t v -> (o c) t v")
                        sync.dma_start(xt[0:D, h], b[:, 0:TH]).then_inc(x_in[h], 16)
                        sync.dma_start(xt[D:P, h, 0:64], b[:, 64:128]).then_inc(x_in[h], 16)

            @block.gpsimd
            def _(g):
                g.memset(E[:, :, :, :], 0.0)
                g.memset(w[:, :, :], 0.0).then_inc(zeroed, 1)
                g.wait_ge(zeroed, 1)

            @block.tensor
            def _(pe):
                pe.sem_inc(x_free, 2)
                pe.wait_ge(w_in, 32)
                for o in range(D):
                    mm = pe.matmul(ps[:, o // 32, PATCH * (o % 32):PATCH * (o % 32 + 1)], wt[:, o, :], dft[:, :],
                                   start=True, stop=True)
                mm.then_inc(w_made, 1)
                pe.wait_ge(w_out, 4)
                with pe.Fori(0, HALF) as i:
                    for h in range(2):
                        pe.wait_ge(padded, 2 * i + h + 1)
                        for p in range(PATCH):
                            rhs = xt[:, h, p:p + STEP * 7 + 1:STEP, :]
                            mm = pe.matmul(ps[:, h], w[:, p, :], rhs, start=(p == 0), stop=(p == PATCH - 1))
                        mm.then_inc(summed, 1)
                    for h in range(2):
                        pe.wait_ge(e_ready, 2 * i + h + 1)
                        pe.wait_ge(row_free, 2 * i + h + 1)
                        for j in range(NB):
                            mm = pe.matmul(ps[:, 2 + h, D * j:D * (j + 1)],
                                           E[:, h, 8 * j:8 * (j + 1), :], K["fold_halves"],
                                           start=True, stop=True)
                        mm.then_inc(row_ready, 1)

            @block.scalar
            def _(act):
                act.wait_ge(w_made, 1)
                act.wait_ge(zeroed, 1)
                for k in range(2):
                    h = slice(D * k, D * (k + 1))
                    for q in range(2):
                        src = ps[h, q].rearrange("p (o t) -> p t o", t=PATCH)
                        act.activation(w[h, :, D * k + 32 * q:D * k + 32 * (q + 1)], src,
                                       ACT.Copy).then_inc(w_out, 1)

                with act.Fori(0, HALF) as i:
                    for h in range(2):
                        act.wait_ge(summed, 2 * i + h + 1)
                        for k in range(2):
                            q = slice(D * k, D * (k + 1))
                            src = ps[q, h].rearrange("p (n v) -> p v n", v=NT)
                            act.activation(E[q, h, :, 8 * k:8 * (k + 1)], src, ACT.Copy).then_inc(
                                x_free if k == 0 else e_ready, 1)

            @block.vector
            def _(v):
                v.sem_inc(row_free, 2)
                with v.Fori(0, HALF) as i:
                    for h in range(2):
                        v.wait_ge(x_in[h], 32 * i + 32)
                        v.tensor_copy(xt[D:P, h, 64:TH], bcast(xt[D:P, h, 63, :], 1, STEP)).then_inc(padded, 1)
                    for h in range(2):
                        v.wait_ge(row_ready, 2 * i + h + 1)
                        v.tensor_copy(H[:, :, bass.ds(P * i + D * h, D)],
                                      ps[:, 2 + h].rearrange("p (j d) -> p j d", d=D)).then_inc(row_free, 1)
                v.wait_ge(row_free, 2 + 2 * HALF)


def stage_zero_pads(nc, pool, XF):
    names, other = pool.stage()
    zeroed = next(names)
    with nc.Block(no_gpsimd_drain=True) as block:
        @block.sync
        def _(sync):
            pool.clear(sync, other)

        @block.vector
        def _(v):
            v.memset(XF[:, :, 0:PAD], 0.0).then_inc(zeroed, 1)
            v.memset(XF[:, :, PAD + L:LF], 0.0).then_inc(zeroed, 1)
            v.wait_ge(zeroed, 2)



def stage_attention(nc, pool, K, H, ps):
    ident = K["ident"]
    with ExitStack() as ctx:
        def sb(name, shape):
            return ctx.enter_context(nc.sbuf_tensor(name, shape, F32))

        wl = sb("at_wl", [P, 2, P])
        wr = sb("at_wr", [P, 5, P])
        wp = sb("at_wp", [P, 5, P])
        rope = sb("at_rope", [P, 2, L])
        mask = sb("at_mask", [P, P])
        Hb, Xb = sb("at_hb", [P, NB, P]), sb("at_xb", [P, L])
        QZ, Kb, Vb = sb("at_qz", [P, 2, L]), sb("at_k", [P, L]), sb("at_v", [P, NB, P])
        tmp = sb("at_tmp", [P, 2, 512])
        Pr, Pt = sb("at_p", [P, 2, L]), sb("at_pt", [P, 2, L])
        nmax, rsum = sb("at_nmax", [P, 16]), sb("at_rsum", [P, 16])

        names, other = pool.stage()
        w_in, w_made, w_out, zeroed = (next(names) for _ in range(4))
        with nc.Block(no_gpsimd_drain=True) as block:
            @block.sync
            def _(sync):
                pool.clear(sync, other)
                load(sync, w_in, [(wl[:, :, :], K["at_wl"]), (wr[:, :, :], K["at_wr"]),
                                  (rope[:, :, :], K["at_rope"]), (mask[:, :], K["at_mask"])])
                sync.wait_ge(w_in, 64)

            @block.gpsimd
            def _(g):
                g.memset(QZ[:, :, :], 0.0).then_inc(zeroed, 1)
                g.wait_ge(zeroed, 1)

            @block.tensor
            def _(pe):
                pe.wait_ge(w_in, 64)
                for n in range(5):
                    mm = pe.matmul(ps[:, n // 4, P * (n % 4):P * (n % 4 + 1)], wl[:, 0 if n < 2 else 1, :],
                                   wr[:, n, :], start=True, stop=True)
                mm.then_inc(w_made, 1)

            @block.scalar
            def _(act):
                act.wait_ge(w_made, 1)
                act.activation(wp[:, 0:4, :].rearrange("p a b -> p (a b)"), ps[:, 0, :], ACT.Copy).then_inc(w_out, 1)
                act.activation(wp[:, 4, :], ps[:, 1, 0:P], ACT.Copy).then_inc(w_out, 1)
                act.wait_ge(w_out, 2)

        with nc.Fori(0, HALF) as b4:
            names, other = pool.stage()
            taken, turned, x_ready, roped, proj, v_made, v_ready, q_step = (next(names) for _ in range(8))
            with nc.Block(no_gpsimd_drain=True) as block:
                @block.sync
                def _(sync):
                    pool.clear(sync, other)

                @block.scalar
                def _(act):
                    act.activation(Hb[:, :, :], H[:, :, bass.ds(P * b4, P)], ACT.Copy).then_inc(taken, 1)
                    for k in range(2):
                        act.wait_ge(turned, k + 1)
                        act.activation(Xb[:, 512 * k:512 * (k + 1)], ps[:, k], ACT.Copy).then_inc(x_ready, 1)
                    for k in range(2):
                        act.wait_ge(v_made, k + 1)
                        act.activation(Vb[:, 4 * k:4 * (k + 1), :].rearrange("p a b -> p (a b)"), ps[:, k],
                                       ACT.Copy).then_inc(v_ready, 1)
                    act.wait_ge(v_ready, 2)

                @block.tensor
                def _(pe):
                    pe.wait_ge(taken, 1)
                    for j in range(NB):
                        mm = pe.transpose(ps[:, j // 4, P * (j % 4):P * (j % 4 + 1)], Hb[:, j, :], ident)
                        if j % 4 == 3:
                            mm.then_inc(turned, 1)
                    pe.wait_ge(x_ready, 2)
                    for j in range(NB):
                        mm = pe.matmul(ps[:, j // 4, P * (j % 4):P * (j % 4 + 1)], Xb[:, P * j:P * (j + 1)],
                                       wp[:, 4, :], start=True, stop=True)
                        if j % 4 == 3:
                            mm.then_inc(v_made, 1)
                    for n in range(4):
                        c, w = n % 2, 2 * (n // 2)
                        if n >= 2:
                            pe.wait_ge(roped, n - 1)
                        for s in range(2):
                            mm = pe.matmul(ps[:, 2 + 2 * c + s], wp[:, w + s, :], Xb[:, 512 * c:512 * (c + 1)],
                                           start=True, stop=True)
                        mm.then_inc(proj, 1)

                @block.vector
                def _(v):
                    st = Steps(v, q_step)
                    for n in range(4):
                        c, cols = n % 2, slice(512 * (n % 2), 512 * (n % 2 + 1))
                        v.wait_ge(proj, n + 1)
                        st.go(v.tensor_tensor(tmp[:, 0], ps[:, 2 + 2 * c], rope[:, 0, cols], ALU.mult))
                        st.do(v.tensor_tensor(tmp[:, 1], ps[:, 3 + 2 * c], rope[:, 1, cols], ALU.mult))
                        if n < 2:
                            st.go(v.tensor_tensor(QZ[0:D, 0, cols], tmp[0:D, 0], tmp[0:D, 1], ALU.add))
                            st.tell(v.tensor_tensor(QZ[D:P, 1, cols], tmp[D:P, 0], tmp[D:P, 1], ALU.add),
                                      roped, "r")
                        else:
                            st.tell(v.tensor_tensor(Kb[:, cols], tmp[:, 0], tmp[:, 1], ALU.add), roped, "r")
                        st.join()

            names, other = pool.stage()
            scored, maxed, exped, p_turned, pt_out, pv, o_read, m_step = (next(names) for _ in range(8))
            tiles = [(q, h) for q in range(NB) for h in range(2)]
            banks = [q // 4 + 1 for q, _ in tiles]
            before = [sum(banks[:n]) for n in range(len(tiles) + 1)]
            S = [ps[:, 0:2], ps[:, 2:4]]
            with nc.Block(no_gpsimd_drain=True) as block:
                @block.sync
                def _(sync):
                    pool.clear(sync, other)

                @block.tensor
                def _(pe):
                    def scores(n):
                        q, h = tiles[n]
                        keys = P * (q + 1)
                        if n >= 2:
                            pe.wait_ge(exped, n - 1)
                        d = keys - P
                        qz = QZ[:, h, P * q:P * (q + 1)]
                        for lo in range(0, d, 512):
                            hi = min(d, lo + 512)
                            pe.matmul(S[n % 2][:, lo // 512, 0:hi - lo], qz, Kb[:, lo:hi], start=True, stop=True)
                        out = S[n % 2][:, d // 512, d % 512:d % 512 + P]
                        pe.matmul(out, qz, Kb[:, d:keys], start=True, stop=False)
                        mm = pe.matmul(out, ident, mask[:, :], start=False, stop=True)
                        mm.then_inc(scored, 1)

                    def turn(n):
                        q, h = tiles[n]
                        pe.wait_ge(exped, n + 1)
                        for c in range(banks[n]):
                            k = before[n] + c
                            if k >= 2:
                                pe.wait_ge(pt_out, k - 1)
                            for b in range(4 * c, min(4 * c + 4, q + 1)):
                                mm = pe.transpose(ps[:, 4 + k % 2, P * (b % 4):P * (b % 4 + 1)],
                                                  Pr[:, n % 2, P * b:P * (b + 1)], ident)
                            mm.then_inc(p_turned, 1)

                    def output(n):
                        q, h = tiles[n]
                        pe.wait_ge(pt_out, before[n + 1])
                        if n >= 2:
                            pe.wait_ge(o_read, n - 1)
                        for b in range(q + 1):
                            mm = pe.matmul(ps[:, 6 + n % 2, 0:P], Pt[:, n % 2, P * b:P * (b + 1)], Vb[:, b, :],
                                           start=(b == 0), stop=(b == q))
                        mm.then_inc(pv, 1)

                    scores(0)
                    for n in range(len(tiles)):
                        if n + 1 < len(tiles):
                            scores(n + 1)
                        turn(n)
                        if n >= 1:
                            output(n - 1)
                    output(len(tiles) - 1)

                @block.scalar
                def _(act):
                    for n, (q, h) in enumerate(tiles):
                        act.wait_ge(maxed, n + 1)
                        if n >= 2:
                            act.wait_ge(p_turned, before[n - 1])
                        src = S[n % 2].rearrange("p a b -> p (a b)")[:, 0:P * (q + 1)]
                        act.activation(Pr[:, n % 2, 0:P * (q + 1)], src, ACT.Exp, bias=nmax[:, n:n + 1],
                                       scale=1 / math.sqrt(D), accum_out=rsum[:, n:n + 1]).then_inc(exped, 1)

                @block.vector
                def _(v):
                    st = Steps(v, m_step)

                    def top(n):
                        q, h = tiles[n]
                        v.wait_ge(scored, n + 1)
                        src = S[n % 2].rearrange("p a b -> p (a b)")[:, 0:P * (q + 1)]
                        st.do(v.tensor_reduce(nmax[:, n:n + 1], src, AX, ALU.max))
                        st.tell(v.tensor_scalar(nmax[:, n:n + 1], nmax[:, n:n + 1], -1 / math.sqrt(D), None,
                                                  ALU.mult), maxed, "m")

                    def copy(n):
                        q, h = tiles[n]
                        for c in range(banks[n]):
                            k = before[n] + c
                            v.wait_ge(p_turned, k + 1)
                            if c == 0 and n >= 2:
                                v.wait_ge(pv, n - 1)
                            w = P * (min(4 * c + 4, q + 1) - 4 * c)
                            st.tell(v.tensor_copy(Pt[:, n % 2, 512 * c:512 * c + w], ps[:, 4 + k % 2, 0:w]),
                                      pt_out, "p")

                    def finish(n):
                        q, h = tiles[n]
                        v.wait_ge(exped, n + 1)
                        st.do(v.reciprocal(rsum[:, n:n + 1], rsum[:, n:n + 1]))
                        v.wait_ge(pv, n + 1)
                        o = H[:, q, bass.ds(P * b4 + D * h, D)]
                        st.tell(v.scalar_tensor_tensor(out=o, in0=ps[:, 6 + n % 2, D * h:D * (h + 1)],
                                                         scalar=rsum[:, n:n + 1], in1=Hb[:, q, D * h:D * (h + 1)],
                                                         op0=ALU.mult, op1=ALU.add), o_read, "o")

                    top(0)
                    for n in range(len(tiles)):
                        if n + 1 < len(tiles):
                            top(n + 1)
                        copy(n)
                        if n >= 2:
                            finish(n - 2)
                    finish(len(tiles) - 2)
                    finish(len(tiles) - 1)



def stage_routed(nc, pool, K, H, XF, ps):
    HID, EXPERTS, NL = 128, 16, 2
    GROUPS = 2 * NB
    wr_dram = K["f0_wr"]
    with ExitStack() as ctx:
        def sb(name, shape, dt=F32):
            return ctx.enter_context(nc.sbuf_tensor(name, shape, dt))

        ri, rf, rm = sb("f0_ri", [1, 64], I32), sb("f0_rf", [1, 64]), sb("f0_rm", [1, 2, 64])
        wi = sb("f0_wi", [P, 2, HID])
        ws, wo = sb("f0_ws", [P, NL, HID]), sb("f0_wo", [P, D])
        bi, bs, bo = sb("f0_bi", [P, 1]), sb("f0_bs", [P, NL]), sb("f0_bo", [P, D])
        wrs = [sb("f0_wr0", [P, NL, GROUPS, HID + 1]), sb("f0_wr1", [P, NL, GROUPS, HID + 1])]
        bias = sb("f0_bias", [P, NL, GROUPS])
        h0, h1 = sb("f0_h0", [P, GROUPS, P]), sb("f0_h1", [P, GROUPS, P])

        names, other = pool.stage()
        w_in, r_step = (next(names) for _ in range(2))
        with nc.Block(no_gpsimd_drain=True) as block:
            @block.sync
            def _(sync):
                pool.clear(sync, other)
                load(sync, w_in, [(ri[:, :], K["f0_route"]), (wi[:, :, :], K["f0_wi"]), (ws[:, :, :], K["f0_ws"]),
                                  (wo[:, :], K["f0_wo"]), (bi[:, :], K["f0_bi"]), (bs[:, :], K["f0_bs"]),
                                  (bo[:, :], K["f0_bo"].partition_broadcast(P))])
                sync.wait_ge(w_in, 7 * 16)

            @block.vector
            def _(v):
                st = Steps(v, r_step)
                v.wait_ge(w_in, 7 * 16)
                st.do(v.tensor_copy(rf[:, :], ri[:, :]))
                st.go(v.tensor_scalar(rm[:, 0], rf[:, :], 0.0, None, ALU.is_ge))
                st.do(v.tensor_scalar(rm[:, 1], rf[:, :], float(EXPERTS - 1), None, ALU.is_le))
                st.go(v.tensor_tensor(rm[:, 0], rm[:, 0], rm[:, 1], ALU.mult))
                st.do(v.tensor_scalar(rf[:, :], rf[:, :], -float(EXPERTS), None, ALU.add))
                st.do(v.tensor_tensor(rf[:, :], rf[:, :], rm[:, 0], ALU.mult))
                st.do(v.tensor_scalar(rf[:, :], rf[:, :], float(EXPERTS), None, ALU.add))
                st.do(v.tensor_copy(ri[:, :], rf[:, :]))
                for l in range(NL):
                    st.do(v.tensor_tensor(ws[:, l, :], ws[:, l, :], K["ident"], ALU.add))

        def load_experts(sync, b4, wr, r_in):
            for g in range(GROUPS):
                at = b4 * NB + (g // NB) * HALF * NB + g % NB
                e = sync.value_load(ri[0:1, bass.ds(at, 1)], min_val=0, max_val=EXPERTS)
                for l in range(NL):
                    sync.dma_start(wr[:, l, g, :], wr_dram[bass.ds(e + l * (EXPERTS + 1), 1)].rearrange(
                        "o d h -> (o d) h")).then_inc(r_in, 16)
            return 16 * NL * GROUPS

        def stage_first_experts():
            names, other = pool.stage()
            r_in = next(names)
            with nc.Block(no_gpsimd_drain=True) as block:
                @block.sync
                def _(sync):
                    pool.clear(sync, other)
                    sync.wait_ge(r_in, load_experts(sync, 0, wrs[0], r_in))

        def stage_pair(b4, wr, next_b4, next_wr):
            names, other = pool.stage()
            hid, h_out, biased, outs, o_step, r_in = (next(names) for _ in range(6))
            with nc.Block(no_gpsimd_drain=True) as block:
                @block.sync
                def _(sync):
                    pool.clear(sync, other)
                    if next_wr is not None:
                        sync.wait_ge(r_in, load_experts(sync, next_b4, next_wr, r_in))

                @block.tensor
                def _(pe):
                    def bank(n):
                        return ps[:, n % 4]

                    for n in range(4):
                        x = XF[:, bass.ds(b4, 1), PAD + 512 * (n % 2):PAD + 512 * (n % 2 + 1)]
                        pe.matmul(bank(n), wi[:, n // 2, :], x.rearrange("p o t -> p (o t)"),
                                  start=True, stop=True).then_inc(hid, 1)
                    for l in range(NL):
                        src = h0 if l == 0 else h1
                        for n in range(4):
                            pe.wait_ge(h_out, 4 + 16 * (l - 1) + 4 * n + 4 if l else n + 1)
                            pe.matmul(bank(n), ws[:, l, :], src[:, 4 * n:4 * n + 4, :].rearrange("p g t -> p (g t)"),
                                      start=True, stop=False)
                            for g in range(4 * n, 4 * n + 4):
                                mm = pe.matmul(bank(n)[:, P * (g % 4):P * (g % 4 + 1)], wr[:, l, g, 0:HID],
                                               src[:, g, :], start=False, stop=(g % 4 == 3))
                            mm.then_inc(hid, 1)
                    for g in range(GROUPS):
                        if g % 4 == 0:
                            pe.wait_ge(h_out, 4 + 16 + g + 4)
                        mm = pe.matmul(ps[:, 4 + g // NB, D * (g % NB):D * (g % NB + 1)], h0[:, g, :], wo[:, :],
                                       start=True, stop=True)
                        if g % NB == NB - 1:
                            mm.then_inc(outs, 1)

                @block.scalar
                def _(act):
                    for n in range(4):
                        act.wait_ge(hid, n + 1)
                        act.activation(h0[:, 4 * n:4 * n + 4, :].rearrange("p g t -> p (g t)"), ps[:, n % 4],
                                       ACT.Relu, bias=bi[:, 0:1]).then_inc(h_out, 1)
                    act.wait_ge(biased, NL)
                    for l in range(NL):
                        dst = h1 if l == 0 else h0
                        for g in range(GROUPS):
                            if g % 4 == 0:
                                act.wait_ge(hid, 4 * (l + 1) + g // 4 + 1)
                            act.activation(dst[:, g, :], ps[:, (g // 4) % 4, P * (g % 4):P * (g % 4 + 1)],
                                           ACT.Relu, bias=bias[:, l, g:g + 1]).then_inc(h_out, 1)

                @block.vector
                def _(v):
                    st = Steps(v, o_step)
                    for l in range(NL):
                        st.tell(v.tensor_scalar(bias[:, l, :], wr[:, l, :, HID], bs[:, l:l + 1], None, ALU.add),
                                  biased, "b")
                    for h in range(2):
                        x = H[:, :, bass.ds(P * b4 + D * h, D)]
                        v.wait_ge(outs, h + 1)
                        st.do(v.tensor_tensor(x, x, ps[:, 4 + h].rearrange("p (j d) -> p j d", d=D), ALU.add))
                        st.do(v.tensor_tensor(x, x, bcast(bo[:, :], 1, NB), ALU.add))

        stage_first_experts()
        pool.open_loop()
        with nc.Fori(0, HALF // 2 - 1) as pair:
            stage_pair(pair * 2, wrs[0], pair * 2 + 1, wrs[1])
            stage_pair(pair * 2 + 1, wrs[1], pair * 2 + 2, wrs[0])
            pool.even(nc)
        stage_pair(HALF - 2, wrs[0], HALF - 1, wrs[1])
        stage_pair(HALF - 1, wrs[1], None, None)



TWO_PI = 6.2831845
ROUND = 1.5 * 2.0 ** 23


def stage_state_parameters(nc, pool, K, Q, S, T, C):
    NPAR = 5
    NL = Q.shape[2] // D
    WQ = NL * D
    a = T[:, 0:NB].rearrange("p a b -> p (a b)").rearrange("p (k w) -> p k w", w=WQ)
    sc = T[:, NB:NB + 2].rearrange("p a b -> p (a b)").rearrange("p (k w) -> p k w", w=WQ)
    par = S[:, 0:NB].rearrange("p a b -> p (a b)").rearrange("p (k w) -> p k w", w=WQ)
    names, other = pool.stage()
    p_in, v_step, a_step, asked = (next(names) for _ in range(4))
    lr, t0, x, y = (Q[:, k] for k in range(4))
    dt, are, tr, er, ei, cr, ci, den, z, em1, hs = (a[:, k] for k in range(11))
    aim, cre, cim = par[:, 2], par[:, 3], par[:, 4]
    sg = C["cols"][:, 2:3]
    with nc.Block(no_gpsimd_drain=True) as block:
        @block.sync
        def _(sync):
            pool.clear(sync, other)
            load(sync, p_in, [(par[:, 0:NPAR, D * n:D * (n + 1)], K["s4_par"][n]) for n in range(NL)])

        @block.scalar
        def _(act):
            act.wait_ge(asked, 1)
            act.activation(y, tr, ACT.Sin, scale=-TWO_PI, bias=C["quarter"]).then_inc(a_step, 1)
            act.activation(z, x, ACT.Sin, scale=-TWO_PI).then_inc(a_step, 1)
            act.activation(hs, x, ACT.Sin, scale=-TWO_PI / 2).then_inc(a_step, 1)

        @block.vector
        def _(v):
            st = Steps(v, v_step)

            def tt(out, p, q, op):
                st.do(v.tensor_tensor(out, p, q, op))

            def ts(out, p, s1, s2, op0, op1=None):
                st.do(v.tensor_scalar(out, p, s1, s2, op0, op1) if op1 is not None
                      else v.tensor_scalar(out, p, s1, None, op0))

            def reduce_turns(out, n, q, phase):
                ts(n, q, phase, ROUND, ALU.add, ALU.add)
                st.do(v.scalar_tensor_tensor(out=out, in0=n, scalar=-ROUND, in1=q, op0=ALU.add,
                                             op1=ALU.subtract))

            def exponential(q, e, m1):
                n, r, p = sc[:, 0], sc[:, 1], sc[:, 2]
                two_n = sc[:, 3]
                ts(n, q, 1 / math.log(2), ROUND, ALU.mult, ALU.add)
                ts(n, n, -ROUND, None, ALU.add)
                st.do(v.scalar_tensor_tensor(out=r, in0=n, scalar=-0.693359375, in1=q, op0=ALU.mult, op1=ALU.add))
                st.do(v.scalar_tensor_tensor(out=r, in0=n, scalar=2.12194440e-4, in1=r, op0=ALU.mult, op1=ALU.add))
                ts(p, r, 1 / math.factorial(8), None, ALU.mult)
                for k in range(7, 0, -1):
                    st.do(v.scalar_tensor_tensor(out=p, in0=p, scalar=1 / math.factorial(k), in1=r,
                                                 op0=ALU.add, op1=ALU.mult))
                ts(n, n, -126.0, None, ALU.max)
                ts(two_n.bitcast(I32), n, 127.0, 2.0 ** 23, ALU.add, ALU.mult)
                tt(p, p, two_n, ALU.mult)
                if m1 is not None:
                    st.do(v.scalar_tensor_tensor(out=m1, in0=two_n, scalar=-1.0, in1=p, op0=ALU.add, op1=ALU.add))
                tt(e, p, two_n, ALU.add)

            v.wait_ge(p_in, 16 * NL)
            exponential(par[:, 0], dt, None)
            exponential(par[:, 1], x, None)
            ts(are, x, -1.0, None, ALU.mult)
            tt(lr, are, dt, ALU.mult)
            exponential(lr, den, em1)
            tt(tr, aim, dt, ALU.mult)
            ts(tr, tr, 1 / (2 * math.pi), None, ALU.mult)
            reduce_turns(y, x, tr, 0.0)
            ts(t0, y, -1.0, None, ALU.mult)
            reduce_turns(tr, z, t0, 0.25)
            reduce_turns(x, z, t0, 0.0)
            v.sem_inc(asked, 1)
            v.wait_ge(a_step, 3)
            tt(er, em1, y, ALU.mult)
            tt(hs, hs, hs, ALU.mult)
            st.do(v.scalar_tensor_tensor(out=er, in0=hs, scalar=-2.0, in1=er, op0=ALU.mult, op1=ALU.add))
            tt(ei, den, z, ALU.mult)
            tt(den, are, are, ALU.mult)
            tt(x, aim, aim, ALU.mult)
            tt(den, den, x, ALU.add)
            st.do(v.reciprocal(den, den))
            tt(cr, er, are, ALU.mult)
            tt(x, ei, aim, ALU.mult)
            tt(cr, cr, x, ALU.add)
            tt(cr, cr, den, ALU.mult)
            tt(ci, ei, are, ALU.mult)
            tt(x, er, aim, ALU.mult)
            tt(ci, ci, x, ALU.subtract)
            tt(ci, ci, den, ALU.mult)
            tt(x, cre, cr, ALU.mult)
            tt(z, cim, ci, ALU.mult)
            tt(x, x, z, ALU.subtract)
            tt(y, cre, ci, ALU.mult)
            tt(z, cim, cr, ALU.mult)
            tt(y, y, z, ALU.add)
            ts(x, x, sg, None, ALU.mult)

def stage_state_filter(nc, pool, K, layer, Q, Kt, table, big, XF, ps, C):
    with ExitStack() as ctx:
        def sb(name, shape):
            return ctx.enter_context(nc.sbuf_tensor(name + "_" + str(pool.fresh()), shape, F32))

        dk, own = sb("s4_d", [1, D]), sb("s4_own", [P, 4, D])
        rj = sb("s4_rj", [P, 4, D, NB])
        names, other = pool.stage()
        p_in, v_step, a_step, prod, reduced, sines, decays, t_ready, k_made, k_out, asked = (
            next(names) for _ in range(11))
        lr, t0, x, y = (own[:, k] for k in range(4))
        lv, jv = C["lv"], C["jv"]
        ph, ph2 = C["cols"][:, 0:1], C["cols"][:, 1:2]
        ph_a, ph2_a = C["cols"][:, 3:4], C["cols"][:, 4:5]
        CH = 16
        XCH = L // P
        HG = HALF * XCH

        def decay(h):
            h = h % HG
            return XF[:, h // XCH, PAD + P * (h % XCH):PAD + P * (h % XCH + 1)]

        def decays_of(c):
            at = CH * c % HG // XCH
            return XF[:, at:at + CH // XCH, PAD:PAD + L]

        with nc.Block(no_gpsimd_drain=True) as block:
            @block.sync
            def _(sync):
                pool.clear(sync, other)
                load(sync, p_in, [(dk[:, :], K["s4_D"][bass.ds(layer, 1)])])

            @block.scalar
            def _(act):
                def decay_group(g):
                    for h in range(HG * g, HG * (g + 1)):
                        act.activation(decay(h), lv, ACT.Exp, scale=lr[:, h:h + 1]).then_inc(decays, 1)

                act.wait_ge(asked, 1)
                decay_group(0)
                act.wait_ge(asked, 2)
                act.activation(rj[:, 2], rj[:, 2], ACT.Exp).then_inc(a_step, 1)
                act.wait_ge(asked, 3)
                act.activation(rj[:, 0], rj[:, 0], ACT.Sin, scale=-TWO_PI, bias=ph_a).then_inc(a_step, 1)
                act.activation(rj[:, 1], rj[:, 1], ACT.Sin, scale=-TWO_PI, bias=ph2_a).then_inc(a_step, 1)
                for c in range(D // CH):
                    if c and CH * c % HG == 0:
                        act.wait_ge(t_ready, c)
                        decay_group(CH * c // HG)
                    act.wait_ge(reduced, c + 1)
                    cols = table[:, CH * c:CH * (c + 1), :]
                    act.activation(cols, cols, ACT.Sin, scale=-TWO_PI, bias=ph_a).then_inc(sines, 1)
                act.wait_ge(k_made, 1)
                act.activation(Kt[:, :, bass.ds(D * layer, D)], ps[:, 0].rearrange("p (h j) -> p j h", j=NB), ACT.Copy,
                               scale=2.0).then_inc(k_out, 1)

            @block.gpsimd
            def _(g):
                g.wait_ge(asked, 1)
                for c in range(D // CH):
                    if c >= 2:
                        g.wait_ge(reduced, c - 1)
                    g.tensor_tensor(big[:, c % 2], bcast(t0[:, CH * c:CH * (c + 1)], 2, P), bcast(lv, 1, CH),
                                    ALU.mult).then_inc(prod, 1)

            @block.vector
            def _(v):
                st = Steps(v, v_step)

                def tt(out, p, q, op):
                    st.do(v.tensor_tensor(out, p, q, op))

                def ts(out, p, s1, s2, op0, op1=None):
                    st.do(v.tensor_scalar(out, p, s1, s2, op0, op1) if op1 is not None
                          else v.tensor_scalar(out, p, s1, None, op0))

                def reduce_turns(out, n, q, phase):
                    ts(n, q, phase, ROUND, ALU.add, ALU.add)
                    st.do(v.scalar_tensor_tensor(out=out, in0=n, scalar=-ROUND, in1=q, op0=ALU.add,
                                                 op1=ALU.subtract))

                st.do(v.tensor_copy(own[:, :, :], Q[:, :, bass.ds(D * layer, D)]))
                v.sem_inc(asked, 1)
                tt(rj[:, 2], bcast(lr, 2, NB), bcast(jv, 1, D), ALU.mult)
                v.sem_inc(asked, 1)
                tt(rj[:, 3], bcast(t0, 2, NB), bcast(jv, 1, D), ALU.mult)
                reduce_turns(rj[:, 0], rj[:, 1], rj[:, 3], ph)
                ts(rj[:, 1], rj[:, 3], ph2, ROUND, ALU.add, ALU.add)
                st.do(v.scalar_tensor_tensor(out=rj[:, 1], in0=rj[:, 1], scalar=-ROUND, in1=rj[:, 3],
                                             op0=ALU.add, op1=ALU.subtract))
                v.sem_inc(asked, 1)
                v.wait_ge(a_step, 3)
                tt(rj[:, 0], rj[:, 0], rj[:, 2], ALU.mult)
                tt(rj[:, 1], rj[:, 1], rj[:, 2], ALU.mult)
                tt(rj[:, 0], rj[:, 0], bcast(x, 2, NB), ALU.mult)
                tt(rj[:, 1], rj[:, 1], bcast(y, 2, NB), ALU.mult)
                tt(rj[:, 0], rj[:, 0], rj[:, 1], ALU.subtract)

                def reduce_piece(c):
                    cols = table[:, CH * c:CH * (c + 1), :]
                    v.wait_ge(prod, c + 1)
                    ts(cols, big[:, c % 2], ph, ROUND, ALU.add, ALU.add)
                    st.tell(v.scalar_tensor_tensor(out=cols, in0=cols, scalar=-ROUND, in1=big[:, c % 2],
                                                   op0=ALU.add, op1=ALU.subtract), reduced, "s")

                reduce_piece(0)
                for c in range(D // CH):
                    if c + 1 < D // CH:
                        reduce_piece(c + 1)
                    cols = table[:, CH * c:CH * (c + 1), :].rearrange("p (b h) l -> p b (h l)", h=XCH)
                    v.wait_ge(sines, c + 1)
                    v.wait_ge(decays, HG * (CH * c // HG + 1))
                    st.tell(v.tensor_tensor(cols, cols, decays_of(c), ALU.mult), t_ready, "t")
                v.wait_ge(k_out, 1)
                v.wait_ge(p_in, 16)
                first = Kt[0:1, 0, bass.ds(D * layer, D)]
                tt(first, first, dk[:, :], ALU.add)

            @block.tensor
            def _(pe):
                for h in range(D):
                    if h % CH == 0:
                        pe.wait_ge(t_ready, h // CH + 1)
                    mm = pe.matmul(ps[:, 0, NB * h:NB * (h + 1)], table[:, h, :], rj[:, 0, h, :],
                                   start=True, stop=True)
                mm.then_inc(k_made, 1)


def stage_glu(nc, pool, K, C, layer, U, X, XF, Wout, bout, ident, ps):
    names, other = pool.stage()
    acted, turned, copied, w_in, made, gated, t_free, v_step = (next(names) for _ in range(8))

    def slot(n):
        return C["glu"][:, n % 4].rearrange("p (k z c) -> p k z c", k=2, z=2)

    with nc.Block(no_gpsimd_drain=True) as block:
        @block.sync
        def _(sync):
            pool.clear(sync, other)
            load(sync, w_in, [(Wout, K["s4_wout"][bass.ds(layer, 1)].rearrange("o p n -> (o p) n")),
                              (bout, K["s4_bout"][bass.ds(layer, 1)].rearrange("o n -> (o n)").partition_broadcast(P))])

        @block.tensor
        def _(pe):
            def turn(j):
                pe.wait_ge(acted, j + 1)
                if j >= 2:
                    pe.wait_ge(copied, j - 1)
                for b4 in range(HALF):
                    mm = pe.transpose(ps[:, j % 2, P * b4:P * (b4 + 1)], U[:, j, P * b4:P * (b4 + 1)], ident)
                mm.then_inc(turned, 1)

            turn(0)
            turn(1)
            pe.wait_ge(w_in, 32)
            for n in range(2 * NB):
                j, b = n // 2, 2 * (n % 2)
                pe.wait_ge(copied, j + 1)
                if n >= 6:
                    pe.wait_ge(t_free, n - 5)
                for k in range(2):
                    lhs = XF[:, b + k, PAD + P * j:PAD + P * (j + 1)]
                    mm = pe.matmul(ps[:, 2 + n % 6, 256 * k:256 * (k + 1)], lhs, Wout, start=True, stop=True)
                mm.then_inc(made, 1)
                if n % 2 and j + 2 < NB:
                    turn(j + 2)

        @block.vector
        def _(v):
            st = Steps(v, v_step)

            def gate(n):
                j, b = n // 2, 2 * (n % 2)
                v.wait_ge(gated, n + 1)
                x = X[:, j, P * b:P * (b + 2)].rearrange("p (k c) -> p k c", k=2)
                st.do(v.tensor_tensor(slot(n)[:, :, 0], slot(n)[:, :, 0], slot(n)[:, :, 1], ALU.mult))
                st.do(v.tensor_tensor(x, x, slot(n)[:, :, 0], ALU.add))

            v.wait_ge(w_in, 32)
            for n in range(2 * NB):
                v.wait_ge(made, n + 1)
                st.tell(v.tensor_tensor(C["glu"][:, n % 4].rearrange("p (k c) -> p k c", k=2),
                                        ps[:, 2 + n % 6].rearrange("p (k c) -> p k c", k=2),
                                        bcast(bout, 1, 2), ALU.add), t_free, "t")
                if n >= 2:
                    gate(n - 2)
            gate(2 * NB - 2)
            gate(2 * NB - 1)

        @block.scalar
        def _(act):
            def copy(j):
                act.wait_ge(turned, j + 1)
                act.activation(XF[:, :, PAD + P * j:PAD + P * (j + 1)],
                               ps[:, j % 2].rearrange("p (b t) -> p b t", b=HALF), ACT.Copy).then_inc(copied, 1)

            for j in range(NB):
                act.activation(U[:, j], U[:, j], ACT.Gelu_apprx_tanh).then_inc(acted, 1)
                if j in (2, 3):
                    copy(j - 2)
            for n in range(2 * NB):
                if n % 2 == 0 and n // 2 + 2 < NB:
                    copy(n // 2 + 2)
                act.wait_ge(t_free, n + 1)
                act.activation(slot(n)[:, :, 1], slot(n)[:, :, 1], ACT.Sigmoid).then_inc(gated, 1)


def stages_state_space(nc, pool, K, H, X, XF, U, S, T, KH, MF, MI, stats, ident, ps):
    LAYERS = KH.shape[1]
    with ExitStack() as ctx:
        def sb(name, shape):
            return ctx.enter_context(nc.sbuf_tensor(name, shape, F32))

        lv, jv, cols = sb("s4_lv", [P, P]), sb("s4_jv", [P, NB]), sb("s4_cols", [P, 6])
        Wout, bout, gb = sb("s4_wout", [P, 256]), sb("s4_bout", [P, 256]), sb("s4_gb", [P, 2, D])
        C = {"lv": lv[:, :], "jv": jv[:, :], "cols": cols, "quarter": cols[:, 5:6], "glu": T}
        stage_load(nc, pool, [(lv[:, :], K["s4_lv"]), (jv[:, :], K["s4_jv"]), (cols[:, :], K["s4_cols"])])
        stage_copy(nc, pool, X, H)
        Q = sb("s4_q", [P, 4, LAYERS * D])
        stage_state_parameters(nc, pool, K, Q, S, T, C)
        table = S[:, :, :].rearrange("p a (b l) -> p (a b) l", l=P)
        big = T[:, 0:NB].rearrange("p (k a) (b l) -> p k (a b) l", k=2, l=P)
        pool.open_loop()
        with nc.Fori(0, LAYERS) as layer:
            stage_state_filter(nc, pool, K, layer, Q, U, table, big, XF, ps, C)
            pool.even(nc)
        stage_filter_spectrum(nc, pool, U[:, :, 0:LAYERS * D], KH, S, T, MF, ps)
        pool.open_loop()
        with nc.Fori(0, LAYERS) as layer:
            stage_load(nc, pool, [(gb[:, :, :], K["s4_gb"][bass.ds(layer, 1)].rearrange("o k d -> (o k d)")
                                   .partition_broadcast(P).rearrange("p (k d) -> p k d", k=2))])
            stage_layernorm(nc, pool, X, U, stats, T, gain=gb[:, 0], bias=gb[:, 1])
            stage_long_conv(nc, pool, U, XF, KH, layer, S, T, MF, MI, ps)
            stage_glu(nc, pool, K, C, layer, U, X, XF, Wout[:, :], bout[:, :], ident, ps)
            pool.even(nc)
        stage_layernorm(nc, pool, X, H, stats, T, add=H, features=(XF, ident, ps, None, None))


def stage_copy(nc, pool, dst, src):
    names, other = pool.stage()
    copied = next(names)
    with nc.Block(no_gpsimd_drain=True) as block:
        @block.sync
        def _(sync):
            pool.clear(sync, other)

        @block.vector
        def _(v):
            v.tensor_copy(dst[:, :, :], src[:, :, :]).then_inc(copied, 1)
            v.wait_ge(copied, 1)



GATE_PARTS = 3


def stage_top2(nc, pool, XF, router, rbias, rank, gates, parts, part16, gF, gB, sel, sel16, sc, ident, ps,
               on_probs):
    E = 8
    G = NB * B
    R = GATE_PARTS * 2 * E
    names, other = pool.stage()
    made, v_step, centred, exped, weighed, turned, copied, zeroed = (next(names) for _ in range(8))
    with nc.Block(no_gpsimd_drain=True) as block:
        @block.sync
        def _(sync):
            pool.clear(sync, other)

        @block.gpsimd
        def _(g):
            g.memset(gF[:, :, :], 0.0).then_inc(zeroed, 1)
            g.memset(gB[:, :, :], 0.0).then_inc(zeroed, 1)
            g.wait_ge(zeroed, 2)

        @block.tensor
        def _(pe):
            for n in range(NB * HALF):
                j, b4 = n // HALF, n % HALF
                mm = pe.matmul(ps[:, 0, 2 * E * n:2 * E * (n + 1)], XF[:, b4, PAD + P * j:PAD + P * (j + 1)],
                               router, start=True, stop=True)
            mm.then_inc(made, 1)
            pe.wait_ge(weighed, 1)
            for n in range(NB * HALF):
                j, b4 = n // HALF, n % HALF
                if n >= 28:
                    pe.wait_ge(copied, 2 * (n // 4 - 6))
                mm = pe.transpose(ps[0:R, 1 + (n // 4) % 7, P * b4:P * (b4 + 1)],
                                  parts[:, n].rearrange("p k e -> p (k e)"), ident)
                if b4 == HALF - 1:
                    mm.then_inc(turned, 1)

        @block.scalar
        def _(act):
            act.wait_ge(centred, 1)
            act.activation(sc[:, 1], sc[:, 1], ACT.Exp).then_inc(exped, 1)
            act.wait_ge(zeroed, 2)
            for j in range(NB):
                act.wait_ge(turned, j + 1)
                src = ps[0:R, 1 + j % 7].rearrange("p (b t) -> p b t", b=HALF)
                for dst in (gF, gB):
                    act.activation(dst[0:R, :, P * j:P * (j + 1)], src, ACT.Copy).then_inc(copied, 1)
            act.wait_ge(copied, 2 * NB)

        @block.vector
        def _(v):
            st = Steps(v, v_step)

            def g8(k):
                return sc[:, k].rearrange("p (g e) -> p g e", e=E)

            def tt(out, a, b, op):
                st.do(v.tensor_tensor(out, a, b, op))

            def top(out, a, op=ALU.max):
                st.do(v.tensor_reduce(out, a, AX, op))

            m, r = sc[:, 6, 0:G], sc[:, 6, G:2 * G]
            st.go(v.tensor_copy(sel16[:, :, :, :], sel[:, :, :, :]))
            v.wait_ge(made, 1)
            if rbias is None:
                st.do(v.tensor_copy(sc[:, 0], ps[:, 0]))
            else:
                tt(g8(0), ps[:, 0].rearrange("p (g e) -> p g e", e=E), bcast(rbias, 1, G), ALU.add)
            top(m, g8(0))
            st.tell(v.tensor_tensor(g8(1), g8(0), bcast(m, 2, E), ALU.subtract), centred, "c")
            v.wait_ge(exped, 1)
            if on_probs:
                top(m, g8(1), ALU.add)
                st.do(v.reciprocal(m, m))
                tt(g8(1), g8(1), bcast(m, 2, E), ALU.mult)
            val = g8(1) if on_probs else g8(0)
            for k in (2, 3):
                top(m, val)
                tt(g8(4), val, bcast(m, 2, E), ALU.is_equal)
                tt(g8(4), g8(4), bcast(rank, 1, G), ALU.mult)
                top(r, g8(4))
                tt(g8(k), g8(4), bcast(r, 2, E), ALU.is_equal)
                if k == 2:
                    st.do(v.scalar_tensor_tensor(out=g8(5), in0=g8(2), scalar=-1e30, in1=val, op0=ALU.mult,
                                                 op1=ALU.add))
                    val = g8(5)
            tt(g8(2), g8(2), g8(3), ALU.add)
            tt(g8(1), g8(1), g8(2), ALU.mult)
            top(m, g8(1), ALU.add)
            if on_probs:
                st.do(v.tensor_scalar(m, m, 1e-12, None, ALU.max))
            st.do(v.reciprocal(m, m))
            tt(gates[:, :].rearrange("p (g e) -> p g e", e=E), g8(1), bcast(m, 2, E), ALU.mult)
            rest = gates[:, :].rearrange("p (n e) -> p n e", e=2 * E)
            for k in range(GATE_PARTS - 1):
                st.do(v.tensor_copy(part16[:, :, :], rest))
                st.do(v.tensor_copy(parts[:, :, k], part16[:, :, :]))
                tt(rest, rest, parts[:, :, k], ALU.subtract)
            st.tell(v.tensor_copy(parts[:, :, GATE_PARTS - 1], rest), weighed, "w")


def stage_experts(nc, pool, H, XF, gF, w1, b1, w2, b2, ident, ps, buf, nq, alpha, func, middle=None,
                  spread=None, gate_of=None):
    GA, GB_, OF = buf
    units = [(c, h, q) for c in range(2) for q in range(nq) for h in range(2)]
    NU = len(units)
    per = 2 * nq
    FIRST, OTHER = (0, 1, 6), (2, 3, 7)
    pool.open_loop()
    with nc.Fori(0, HALF) as b4:
        names, other = pool.stage()
        hid, hid2, acted, mid_done, gated, used, o_done, of_out, o_turned, h_out = (
            next(names) for _ in range(10))

        def gates_of(g, c):
            return g[:, bass.ds(b4, 1), 512 * c:512 * (c + 1)].rearrange("p o t -> p (o t)")

        with nc.Block(no_gpsimd_drain=True) as block:
            @block.sync
            def _(sync):
                pool.clear(sync, other)

            @block.tensor
            def _(pe):
                def first(n):
                    c, h, q = units[n]
                    if n >= 3:
                        pe.wait_ge(acted, n - 2)
                    x = XF[:, bass.ds(b4, 1), PAD + 512 * c:PAD + 512 * (c + 1)].rearrange("p o t -> p (o t)")
                    pe.matmul(ps[:, FIRST[n % 3]], w1[:, h, q], x, start=True, stop=True).then_inc(hid, 1)
                    if gate_of is None:
                        if n >= 3:
                            pe.wait_ge(gated, n - 2)
                        pe.matmul(ps[:, OTHER[n % 3]], spread[1][:, h, q], gates_of(spread[0], c), start=True,
                                  stop=True).then_inc(hid2, 1)

                def mid(n):
                    pe.wait_ge(acted, n + 1)
                    if n >= 3:
                        pe.wait_ge(mid_done, n - 2)
                    pe.matmul(ps[:, OTHER[n % 3]], middle[0][:, units[n][2]], GA[:, n % 4], start=True,
                              stop=True).then_inc(hid2, 1)

                def second(p):
                    pe.wait_ge(gated, 2 * p + 2)
                    k = 2 * p % per
                    for n in (2 * p, 2 * p + 1):
                        c, h, q = units[n]
                        pe.matmul(ps[D * h:D * (h + 1), 4 + c], w2[:, q], GB_[:, n % 4], start=(k == 0),
                                  stop=False).then_inc(used, 1)
                    if k == per - 2:
                        g = gF[:, 512 * c:512 * (c + 1)] if gate_of is not None else gates_of(gF, c)
                        pe.matmul(ps[:, 4 + c], b2, g, start=False, stop=True).then_inc(o_done, 1)

                def back(c):
                    pe.wait_ge(of_out, c + 1)
                    for k in range(4):
                        mm = pe.transpose(ps[:, 4 + c, P * k:P * (k + 1)], OF[:, c, P * k:P * (k + 1)], ident)
                    mm.then_inc(o_turned, 1)

                lag = 2 if middle is not None else 1
                for p in range(NU // 2 + lag):
                    if p < NU // 2:
                        first(2 * p)
                        first(2 * p + 1)
                    if middle is not None and 1 <= p <= NU // 2:
                        mid(2 * p - 2)
                        mid(2 * p - 1)
                    if p >= lag:
                        second(p - lag)
                    if p == nq + lag + 1:
                        back(0)
                back(1)

            @block.scalar
            def _(act):
                def middle_act(n):
                    act.wait_ge(hid2, n + 1)
                    q = units[n][2]
                    if n >= 2:
                        act.wait_ge(gated, n - 1)
                    act.activation(OFX(buf)[:, n % 2], ps[:, OTHER[n % 3]], ACT.Relu, bias=middle[2][:, q:q + 1],
                                   scale=middle[1][:, q:q + 1]).then_inc(mid_done, 1)

                def out(c):
                    act.wait_ge(o_done, c + 1)
                    act.activation(OF[:, c], ps[:, 4 + c], ACT.Copy).then_inc(of_out, 1)

                for n, (c, h, q) in enumerate(units):
                    act.wait_ge(hid, n + 1)
                    if n >= 4:
                        act.wait_ge(gated if middle is None else mid_done, n - 3)
                    if middle is None:
                        act.activation(GA[:, n % 4], ps[:, FIRST[n % 3]], func, bias=b1[:, q:q + 1]).then_inc(acted, 1)
                    else:
                        act.activation(GA[:, n % 4], ps[:, FIRST[n % 3]], func, bias=b1[1][:, q:q + 1],
                                       scale=b1[0][:, q:q + 1]).then_inc(acted, 1)
                        if n % 2 and n >= 3:
                            middle_act(n - 3)
                            middle_act(n - 2)
                    if n == per + 3:
                        out(0)
                if middle is not None:
                    middle_act(NU - 2)
                    middle_act(NU - 1)
                out(1)

            @block.vector
            def _(v):
                st = Steps(v, None)

                def update(c):
                    v.wait_ge(o_turned, c + 1)
                    x = H[:, 4 * c:4 * (c + 1), bass.ds(P * b4, P)]
                    st.tell(v.scalar_tensor_tensor(out=x, in0=x, scalar=float(alpha),
                                                     in1=ps[:, 4 + c].rearrange("p (j d) -> p j d", d=P),
                                                     op0=ALU.mult, op1=ALU.add), h_out, "h")

                for n, (c, h, q) in enumerate(units):
                    if middle is None:
                        v.wait_ge(acted, n + 1)
                        v.wait_ge(hid2, n + 1)
                        g, src = ps[:, OTHER[n % 3]], GA[:, n % 4]
                    else:
                        v.wait_ge(mid_done, n + 1)
                        g, src = gate_of[:, q, 512 * c:512 * (c + 1)], OFX(buf)[:, n % 2]
                    if n >= 4:
                        v.wait_ge(used, n - 3)
                    st.tell(v.tensor_tensor(GB_[:, n % 4], src, g, ALU.mult), gated, "g")
                    if n == per + 6:
                        update(0)
                if per + 6 >= NU:
                    update(0)
                update(1)
        pool.even(nc)


def OFX(buf):
    return buf[2][:, 2:4]


def stage_gate_spread(nc, pool, gF, sel, GT, nq, ps):
    names, other = pool.stage()
    made, out = next(names), next(names)
    with nc.Block(no_gpsimd_drain=True) as block:
        @block.sync
        def _(sync):
            pool.clear(sync, other)

        @block.tensor
        def _(pe):
            for n in range(2 * nq):
                q, c = n // 2, n % 2
                pe.matmul(ps[:, n], sel[:, 0, q], gF[:, 512 * c:512 * (c + 1)], start=True,
                          stop=True).then_inc(made, 1)

        @block.scalar
        def _(act):
            for n in range(2 * nq):
                q, c = n // 2, n % 2
                act.wait_ge(made, n + 1)
                act.activation(GT[:, q, 512 * c:512 * (c + 1)], ps[:, n], ACT.Copy).then_inc(out, 1)
            act.wait_ge(out, 2 * nq)


def stages_moe(nc, pool, K, pre, H, XF, ident, ps, nq, on_probs, alpha):
    with ExitStack() as ctx:
        def sb(name, shape):
            return ctx.enter_context(nc.sbuf_tensor(pre + name, shape, F32))

        router, rb, rank = sb("rt", [P, 16]), sb("rb", [P, 8]), sb("rank", [P, 8])
        w1, w2 = sb("w1", [P, 2, nq, P]), sb("w2", [P, nq, D])
        sel, b1, b2 = sb("sel", [P, 2, nq, P]), sb("b1", [P, nq]), sb("b2", [P, P])
        gates, gF, sc = sb("gates", [P, 512]), sb("gf", [P, HALF, L]), sb("sc", [P, 7, 512])
        GA, GB_, OF = sb("ga", [P, 4, 512]), sb("gb", [P, 4, 512]), sb("of", [P, 4, 512])
        parts = sb("parts", [P, NB * HALF, GATE_PARTS, 16])
        part16 = ctx.enter_context(nc.sbuf_tensor(pre + "part16", [P, NB * HALF, 16], BF16))
        gB = ctx.enter_context(nc.sbuf_tensor(pre + "gb16", [P, HALF, L], BF16))
        sel16 = ctx.enter_context(nc.sbuf_tensor(pre + "sel16", [P, 2, nq, P], BF16))
        pairs = [(router[:, :], K[pre + "router"]), (rank[:, :], K["rank"]), (w1[:, :, :, :], K[pre + "w1"]),
                 (w2[:, :, :], K[pre + "w2"]), (sel[:, :, :, :], K[pre + "sel"]), (b1[:, :], K[pre + "b1"]),
                 (b2[:, :], K[pre + "b2"])]
        if not on_probs:
            pairs.append((rb[:, :], K[pre + "rb"].partition_broadcast(P)))
        stage_load(nc, pool, pairs)
        stage_top2(nc, pool, XF, router[:, :], None if on_probs else rb[:, :], rank[:, :], gates, parts, part16, gF,
                   gB, sel, sel16, sc, ident, ps, on_probs)
        stage_experts(nc, pool, H, XF, gF, w1, b1, w2, b2[:, :], ident, ps, (GA, GB_, OF), nq, alpha,
                      ACT.Gelu, spread=(gB, sel16))



def stage_hyena_filter(nc, pool, K, Kt, ps):
    with ExitStack() as ctx:
        def sb(name, shape):
            return ctx.enter_context(nc.sbuf_tensor("hy_" + name, shape, F32))

        z, w0, w12, w3 = sb("z", [3, L]), sb("w0", [3, D]), sb("w12", [D, 2, D]), sb("w3", [D, D])
        bf, decay, fb = sb("bf", [D, 4]), sb("decay", [P, NB, D]), sb("fb", [1, D])
        h, q, n = sb("h", [D, L]), sb("q", [D, L]), sb("n", [D, L])
        names, other = pool.stage()
        w_in, made, reduced, sined, v_step, k_made = (next(names) for _ in range(6))
        with nc.Block(no_gpsimd_drain=True) as block:
            @block.sync
            def _(sync):
                pool.clear(sync, other)
                load(sync, w_in, [(z[:, :], K["hy_z"]), (w0[:, :], K["hy_w0"]), (w12[:, :, :], K["hy_w12"]),
                                  (w3[:, :], K["hy_w3"]), (bf[:, :], K["hy_bf"]), (fb[:, :], K["hy_fb"]),
                                  (decay[:, :, :], K["hy_decay"].rearrange("p (j d) -> p j d", j=NB))])

            @block.tensor
            def _(pe):
                pe.wait_ge(w_in, 7 * 16)
                for k in range(3):
                    if k >= 1:
                        pe.wait_ge(sined, k)
                    for c in range(2):
                        cols = slice(512 * c, 512 * (c + 1))
                        mm = (pe.matmul(ps[0:D, c], w0[:, :], z[:, cols], start=True, stop=True) if k == 0 else
                              pe.matmul(ps[0:D, c], w12[:, k - 1], h[:, cols], start=True, stop=True))
                    mm.then_inc(made, 1)
                pe.wait_ge(sined, 3)
                for j in range(NB):
                    mm = pe.matmul(ps[:, 2, D * j:D * (j + 1)], h[:, P * j:P * (j + 1)], w3[:, :],
                                   start=True, stop=True)
                mm.then_inc(k_made, 1)

            @block.scalar
            def _(act):
                for k in range(3):
                    act.wait_ge(reduced, k + 1)
                    act.activation(h[:, :], q[:, :], ACT.Sin).then_inc(sined, 1)

            @block.vector
            def _(v):
                st = Steps(v, v_step)
                for k in range(3):
                    v.wait_ge(made, k + 1)
                    src = ps[0:D, 0:2].rearrange("p a b -> p (a b)")
                    st.do(v.tensor_scalar(n[:, :], src, bf[:, k:k + 1], bf[:, 3:4], ALU.add, ALU.mult))
                    if k >= 1:
                        v.wait_ge(sined, k)
                    st.do(v.tensor_scalar(q[:, :], n[:, :], 1 / (2 * math.pi), ROUND, ALU.mult, ALU.add))
                    st.do(v.tensor_scalar(q[:, :], q[:, :], -ROUND, None, ALU.add))
                    st.do(v.scalar_tensor_tensor(out=n[:, :], in0=q[:, :], scalar=-6.28125, in1=n[:, :],
                                                 op0=ALU.mult, op1=ALU.add))
                    st.do(v.scalar_tensor_tensor(out=q[:, :], in0=q[:, :], scalar=-(2 * math.pi - 6.28125),
                                                 in1=n[:, :], op0=ALU.mult, op1=ALU.add))
                    st.tell(v.tensor_scalar(q[:, :], q[:, :], -3.1415925, 3.1415925, ALU.max, ALU.min),
                              reduced, "r")
                v.wait_ge(k_made, 1)
                st.do(v.tensor_tensor(Kt[:, :, :], ps[:, 2].rearrange("p (j d) -> p j d", j=NB), decay[:, :, :],
                                      ALU.mult))
                st.do(v.tensor_tensor(Kt[0:1, 0, :], Kt[0:1, 0, :], fb[:, :], ALU.add))


def stage_hyena_weights(nc, pool, K, Win, Bin, Wout, Bout, ps):
    NI = 3 * P
    with ExitStack() as ctx:
        def sb(name, shape):
            return ctx.enter_context(nc.sbuf_tensor("hw_" + name, shape, F32))

        w, wo = sb("w", [P, NI]), sb("wo", [P, P])
        taps, otaps = sb("taps", [P, 3, NI]), sb("otaps", [P, 3, P])
        rows, orow, edge, t = sb("rows", [P, 2, NI]), sb("orow", [P, P]), sb("edge", [P, 4]), sb("t", [P, NI])
        names, other = pool.stage()
        w_in, v_step = next(names), next(names)
        with nc.Block(no_gpsimd_drain=True) as block:
            @block.sync
            def _(sync):
                pool.clear(sync, other)
                load(sync, w_in, [(w[:, :], K["hw_w"]), (wo[:, :], K["hw_wo"]), (edge[:, :], K["hw_edge"])] +
                     [(d[:, :, :], K[k].partition_broadcast(P)) for d, k in
                      ((taps, "hw_taps"), (otaps, "hw_otaps"), (rows, "hw_rows"))] +
                     [(orow[:, :], K["hw_orow"].partition_broadcast(P))])

            @block.vector
            def _(v):
                st = Steps(v, v_step)

                def tt(out, a, b, op):
                    st.do(v.tensor_tensor(out, a, b, op))

                def fma(out, a, col, b):
                    st.do(v.scalar_tensor_tensor(out=out, in0=a, scalar=edge[:, col:col + 1], in1=b, op0=ALU.mult,
                                                 op1=ALU.add))

                v.wait_ge(w_in, 7 * 16)
                tt(Win[:, :, :], bcast(w[:, :], 1, 3), taps[:, :, :], ALU.mult)
                tt(Wout[:, :, :], bcast(wo[:, :], 1, 3), otaps[:, :, :], ALU.mult)
                tt(taps[:, :, :], bcast(rows[:, 0], 1, 3), taps[:, :, :], ALU.mult)
                tt(t[:, :], taps[:, 2], rows[:, 1], ALU.add)
                fma(Bin[:, 0], taps[:, 1], 0, t[:, :])
                fma(Bin[:, 0], taps[:, 0], 1, Bin[:, 0])
                tt(Bin[:, 1], t[:, :], taps[:, 1], ALU.add)
                tt(Bin[:, 1], Bin[:, 1], taps[:, 0], ALU.add)
                tt(otaps[:, :, :], bcast(orow[:, :], 1, 3), otaps[:, :, :], ALU.mult)
                tt(t[:, 0:P], otaps[:, 1], otaps[:, 2], ALU.add)
                fma(Bout[:, 0], otaps[:, 0], 0, t[:, 0:P])
                tt(Bout[:, 1], t[:, 0:P], otaps[:, 0], ALU.add)
                tt(t[:, 0:P], otaps[:, 0], otaps[:, 1], ALU.add)
                fma(Bout[:, 2], otaps[:, 2], 2, t[:, 0:P])


def stage_gates_in(nc, pool, XN, XF, U, X1, V, Win, Bin, gb, ident, ps):
    names, other = pool.stage()
    turned, copied, made, taken, v_step = (next(names) for _ in range(5))
    with nc.Block(no_gpsimd_drain=True) as block:
        @block.sync
        def _(sync):
            pool.clear(sync, other)

        @block.tensor
        def _(pe):
            def turn(j):
                if j >= 2:
                    pe.wait_ge(copied, j - 1)
                for b4 in range(HALF):
                    mm = pe.transpose(ps[:, j % 2, P * b4:P * (b4 + 1)], XN[:, j, P * b4:P * (b4 + 1)], ident)
                mm.then_inc(turned, 1)

            def project(j):
                pe.wait_ge(copied, j + 1)
                for pair in range(2):
                    n = 2 * j + pair
                    if n >= 3:
                        pe.wait_ge(taken, n - 2)
                    for k in range(2):
                        b4 = 2 * pair + k
                        for tap in range(3):
                            at = PAD + P * j - 2 + tap
                            mm = pe.matmul(ps[:, 2 + 2 * (n % 3) + k, 0:3 * P], XF[:, b4, at:at + P],
                                           Win[:, tap], start=(tap == 0), stop=(tap == 2))
                    mm.then_inc(made, 1)

            turn(0)
            for j in range(NB):
                if j + 1 < NB:
                    turn(j + 1)
                project(j)

        @block.scalar
        def _(act):
            for j in range(NB):
                act.wait_ge(turned, j + 1)
                act.activation(XF[:, :, PAD + P * j:PAD + P * (j + 1)],
                               ps[:, j % 2].rearrange("p (b t) -> p b t", b=HALF), ACT.Identity,
                               bias=gb[:, 1:2], scale=gb[:, 0:1]).then_inc(copied, 1)

        @block.vector
        def _(v):
            st = Steps(v, v_step)
            for n in range(2 * NB):
                j, b = n // 2, 2 * (n % 2)
                v.wait_ge(made, n + 1)
                src = ps[:, 2 + 2 * (n % 3):4 + 2 * (n % 3)]
                bias = Bin[:, 0 if j == 0 else 1]
                cols = slice(P * b, P * (b + 2))
                st.go(v.tensor_tensor(X1[:, j, cols].rearrange("p (k c) -> p k c", k=2), src[:, :, 0:P],
                                      bcast(bias[:, 0:P], 1, 2), ALU.add))
                t = V[:, n % 2]
                st.tell(v.tensor_tensor(t, src[:, :, P:3 * P], bcast(bias[:, P:3 * P], 1, 2), ALU.add), taken, "t")
                st.do(v.tensor_tensor(U[:, j, cols].rearrange("p (k c) -> p k c", k=2), t[:, :, 0:P],
                                      t[:, :, P:2 * P], ALU.mult))
            st.join()


def stage_gates_out(nc, pool, U, X1, X, XF, Wout, Bout, V, ident, ps):
    names, other = pool.stage()
    gated, turned, copied, made, biased, acted, v_step = (next(names) for _ in range(7))
    with nc.Block(no_gpsimd_drain=True) as block:
        @block.sync
        def _(sync):
            pool.clear(sync, other)

        @block.tensor
        def _(pe):
            def turn(j):
                pe.wait_ge(gated, j + 1)
                if j >= 3:
                    pe.wait_ge(copied, j - 2)
                for b4 in range(HALF):
                    mm = pe.transpose(ps[:, j % 3, P * b4:P * (b4 + 1)], U[:, j, P * b4:P * (b4 + 1)], ident)
                mm.then_inc(turned, 1)

            def project(j):
                pe.wait_ge(copied, min(j + 2, NB))
                if j >= 4:
                    pe.wait_ge(biased, j - 3)
                for b4 in range(HALF):
                    for tap in range(3):
                        at = PAD + P * j - 1 + tap
                        mm = pe.matmul(ps[:, 3 + j % 4, P * b4:P * (b4 + 1)], XF[:, b4, at:at + P],
                                       Wout[:, tap], start=(tap == 0), stop=(tap == 2))
                mm.then_inc(made, 1)

            turn(0)
            turn(1)
            for j in range(NB):
                if j + 2 < NB:
                    turn(j + 2)
                project(j)

        @block.scalar
        def _(act):
            def gelu(j):
                act.wait_ge(biased, j + 1)
                t = V[:, j % 4]
                act.activation(t, t, ACT.Gelu).then_inc(acted, 1)
                act.wait_ge(acted, 2 * j + 1)
                act.activation(t, t, ACT.Gelu).then_inc(acted, 1)

            for j in range(NB):
                act.wait_ge(turned, j + 1)
                act.activation(XF[:, :, PAD + P * j:PAD + P * (j + 1)],
                               ps[:, j % 3].rearrange("p (b t) -> p b t", b=HALF), ACT.Copy).then_inc(copied, 1)
                if j >= 2:
                    gelu(j - 2)
            gelu(NB - 2)
            gelu(NB - 1)

        @block.vector
        def _(v):
            st = Steps(v, v_step)
            for j in range(NB):
                st.tell(v.tensor_tensor(U[:, j], U[:, j], X1[:, j], ALU.mult), gated, "g")

            def finish(j):
                v.wait_ge(acted, 2 * j + 2)
                st.do(v.tensor_tensor(X[:, j], X[:, j], V[:, j % 4], ALU.add))

            for j in range(NB):
                v.wait_ge(made, j + 1)
                bias = Bout[:, 0 if j == 0 else 2 if j == NB - 1 else 1]
                st.tell(v.tensor_tensor(V[:, j % 4].rearrange("p (b c) -> p b c", b=HALF),
                                          ps[:, 3 + j % 4].rearrange("p (b c) -> p b c", b=HALF),
                                          bcast(bias, 1, HALF), ALU.add), biased, "b")
                if j >= 2:
                    finish(j - 2)
            finish(NB - 2)
            finish(NB - 1)


def stage_between_layers(nc, pool, U, X1, X, XF, Wout, Bout, Win, Bin, gb, stats, T, ident, ps):
    NG = NB // 2
    V, V2 = T[:, 0:4], T[:, 4:6].rearrange("p n (k c) -> p n k c", k=2)
    SQ = T[:, 10:12].rearrange("p j (g d) -> p (j g) d", d=D)
    names, other = pool.stage()
    (gated, o_turned, o_copied, o_made, biased, acted, centred, squared, var_ready, std_ready, normalised, i_turned,
     i_copied, i_made, taken, v_step) = (next(names) for _ in range(16))

    def XN(g):
        return T[:, 6 + 2 * (g % 2):8 + 2 * (g % 2)]

    def tokens(t):
        return t.rearrange("p j (g d) -> p (j g) d", d=D)

    def mean(g):
        return stats[:, 2 * B * g:2 * B * (g + 1)]

    def var(g):
        return stats[:, NB * B + 2 * B * g:NB * B + 2 * B * (g + 1)]

    with nc.Block(no_gpsimd_drain=True) as block:
        @block.sync
        def _(sync):
            pool.clear(sync, other)

        @block.tensor
        def _(pe):
            def turn_out(j):
                pe.wait_ge(gated, j + 1)
                if j >= 2:
                    pe.wait_ge(o_copied, j - 1)
                if j == NB - 1:
                    pe.wait_ge(i_copied, 2)
                for b4 in range(HALF):
                    mm = pe.transpose(ps[:, j % 2, P * b4:P * (b4 + 1)], U[:, j, P * b4:P * (b4 + 1)], ident)
                mm.then_inc(o_turned, 1)

            def project_out(j):
                pe.wait_ge(o_copied, min(j + 2, NB))
                if j >= 2:
                    pe.wait_ge(biased, j - 1)
                for b4 in range(HALF):
                    for tap in range(3):
                        at = PAD + P * j - 1 + tap
                        mm = pe.matmul(ps[:, 2 + j % 2, P * b4:P * (b4 + 1)], XF[:, b4, at:at + P],
                                       Wout[:, tap], start=(tap == 0), stop=(tap == 2))
                mm.then_inc(o_made, 1)

            def turn_in(j):
                pe.wait_ge(normalised, j // 2 + 1)
                pe.wait_ge(o_copied, min(2 * (j // 2) + 7, NB))
                if j >= 2:
                    pe.wait_ge(i_copied, j - 1)
                for b4 in range(HALF):
                    mm = pe.transpose(ps[:, j % 2, P * b4:P * (b4 + 1)], XN(j // 2)[:, j % 2, P * b4:P * (b4 + 1)],
                                      ident)
                mm.then_inc(i_turned, 1)

            def project_in(j):
                pe.wait_ge(i_copied, j + 1)
                for n in (2 * j, 2 * j + 1):
                    if n >= 2:
                        pe.wait_ge(taken, n - 1)
                    for k in range(2):
                        for tap in range(3):
                            at = PAD + P * j - 2 + tap
                            mm = pe.matmul(ps[:, 4 + 2 * (n % 2) + k, 0:3 * P], XF[:, 2 * (n % 2) + k, at:at + P],
                                           Win[:, tap], start=(tap == 0), stop=(tap == 2))
                    mm.then_inc(i_made, 1)

            turn_out(0)
            turn_out(1)
            for j in range(5):
                turn_out(j + 2)
                project_out(j)
            for g in range(NG):
                turn_in(2 * g)
                turn_in(2 * g + 1)
                project_in(2 * g)
                project_in(2 * g + 1)
                for j in (2 * g + 5, 2 * g + 6):
                    if j + 2 < NB:
                        turn_out(j + 2)
                    if j < NB:
                        project_out(j)

        @block.scalar
        def _(act):
            def copy_out(j):
                act.wait_ge(o_turned, j + 1)
                act.activation(XF[:, :, PAD + P * j:PAD + P * (j + 1)],
                               ps[:, j % 2].rearrange("p (b t) -> p b t", b=HALF), ACT.Copy).then_inc(o_copied, 1)

            def gelu(j):
                act.wait_ge(biased, j + 1)
                t = V[:, j % 4]
                act.activation(t, t, ACT.Gelu).then_inc(acted, 1)
                act.wait_ge(acted, 2 * j + 1)
                act.activation(t, t, ACT.Gelu).then_inc(acted, 1)

            def copy_in(j):
                act.wait_ge(i_turned, j + 1)
                act.wait_ge(o_made, min(j // 2 * 2 + 4, NB))
                act.activation(XF[:, :, PAD + P * j:PAD + P * (j + 1)],
                               ps[:, j % 2].rearrange("p (b t) -> p b t", b=HALF), ACT.Identity,
                               bias=gb[:, 1:2], scale=gb[:, 0:1]).then_inc(i_copied, 1)

            def deviation(g):
                act.wait_ge(centred, g + 1)
                act.activation(SQ, tokens(XN(g)), ACT.Square).then_inc(squared, 1)
                act.wait_ge(var_ready, g + 1)
                act.activation(var(g), var(g), ACT.Sqrt).then_inc(std_ready, 1)

            for j in range(4):
                copy_out(j)
            gelu(0)
            copy_out(4)
            gelu(1)
            copy_out(5)
            deviation(0)
            gelu(2)
            gelu(3)
            copy_out(6)
            for g in range(NG):
                copy_in(2 * g)
                copy_in(2 * g + 1)
                if g + 1 < NG:
                    deviation(g + 1)
                if g == 0:
                    copy_out(7)
                for j in (2 * g + 4, 2 * g + 5):
                    if j < NB:
                        gelu(j)

        @block.vector
        def _(v):
            st = Steps(v, v_step)

            def bias_out(j):
                v.wait_ge(o_made, j + 1)
                bias = Bout[:, 0 if j == 0 else 2 if j == NB - 1 else 1]
                st.tell(v.tensor_tensor(V[:, j % 4].rearrange("p (b c) -> p b c", b=HALF),
                                        ps[:, 2 + j % 2].rearrange("p (b c) -> p b c", b=HALF),
                                        bcast(bias, 1, HALF), ALU.add), biased, "b")

            def finish(g):
                for j in (2 * g, 2 * g + 1):
                    v.wait_ge(acted, 2 * j + 2)
                    st.go(v.tensor_tensor(X[:, j], X[:, j], V[:, j % 4], ALU.add))
                st.join()

            def centre(g):
                x = tokens(X[:, 2 * g:2 * g + 2])
                st.do(v.tensor_reduce(mean(g), x, AX, ALU.add))
                st.do(v.tensor_scalar(mean(g), mean(g), 1.0 / D, None, ALU.mult))
                if g >= 2:
                    v.wait_ge(i_turned, 2 * g - 2)
                st.tell(v.tensor_tensor(tokens(XN(g)), x, bcast(mean(g), 2, D), ALU.subtract), centred, "c")

            def variance(g):
                v.wait_ge(squared, g + 1)
                st.do(v.tensor_reduce(var(g), SQ, AX, ALU.add))
                st.tell(v.tensor_scalar(var(g), var(g), 1.0 / D, EPS, ALU.mult, ALU.add), var_ready, "v")

            def normalise(g):
                v.wait_ge(std_ready, g + 1)
                st.do(v.reciprocal(var(g), var(g)))
                st.tell(v.tensor_tensor(tokens(XN(g)), tokens(XN(g)), bcast(var(g), 2, D), ALU.mult), normalised, "n")

            def gates_in(n):
                j, b = n // 2, 2 * (n % 2)
                v.wait_ge(i_made, n + 1)
                src = ps[:, 4 + 2 * (n % 2):6 + 2 * (n % 2)]
                bias = Bin[:, 0 if j == 0 else 1]
                cols = slice(P * b, P * (b + 2))
                st.go(v.tensor_tensor(X1[:, j, cols].rearrange("p (k c) -> p k c", k=2), src[:, :, 0:P],
                                      bcast(bias[:, 0:P], 1, 2), ALU.add))
                t = V2[:, n % 2]
                st.tell(v.tensor_tensor(t, src[:, :, P:3 * P], bcast(bias[:, P:3 * P], 1, 2), ALU.add), taken, "t")
                st.go(v.tensor_tensor(U[:, j, cols].rearrange("p (k c) -> p k c", k=2), t[:, :, 0:P],
                                      t[:, :, P:2 * P], ALU.mult))

            for j in range(NB):
                st.tell(v.tensor_tensor(U[:, j], U[:, j], X1[:, j], ALU.mult), gated, "g")
            bias_out(0)
            bias_out(1)
            finish(0)
            centre(0)
            bias_out(2)
            bias_out(3)
            variance(0)
            normalise(0)
            finish(1)
            for g in range(NG):
                if g + 1 < NG:
                    centre(g + 1)
                gates_in(4 * g)
                if g + 1 < NG:
                    variance(g + 1)
                gates_in(4 * g + 1)
                if g + 1 < NG:
                    normalise(g + 1)
                gates_in(4 * g + 2)
                gates_in(4 * g + 3)
                if 2 * g + 5 < NB:
                    bias_out(2 * g + 4)
                    bias_out(2 * g + 5)
                    finish(g + 2)
            st.join()


def stages_hyena(nc, pool, K, H, X, XF, U, S, T, KH, MF, MI, stats, ident, ps):
    DEPTH = 12
    with ExitStack() as ctx:
        def sb(name, shape):
            return ctx.enter_context(nc.sbuf_tensor("hs_" + name, shape, F32))

        Kt, Win, Bin = sb("kt", [P, NB, D]), sb("win", [P, 3, 3 * P]), sb("bin", [P, 2, 3 * P])
        Wout, Bout, gb, X1 = sb("wout", [P, 3, P]), sb("bout", [P, 3, P]), sb("gb", [P, 2]), sb("x1", [P, NB, W])
        stage_load(nc, pool, [(gb[:, :], K["hy_gb"])])
        stage_hyena_filter(nc, pool, K, Kt, ps)
        stage_filter_spectrum(nc, pool, Kt, KH, S, T, MF, ps)
        stage_hyena_weights(nc, pool, K, Win, Bin, Wout, Bout, ps)
        stage_copy(nc, pool, X, H)
        V = T[:, 0:4]
        V2 = T[:, 0:2].rearrange("p n (k c) -> p n k c", k=2)
        stage_layernorm(nc, pool, X, U, stats, T)
        stage_gates_in(nc, pool, U, XF, U, X1, V2, Win, Bin, gb, ident, ps)
        pool.open_loop()
        with nc.Fori(0, DEPTH - 1) as _:
            stage_long_conv(nc, pool, U, XF, KH, 0, S, T, MF, MI, ps)
            stage_between_layers(nc, pool, U, X1, X, XF, Wout, Bout, Win, Bin, gb, stats, T, ident, ps)
            pool.even(nc)
        stage_long_conv(nc, pool, U, XF, KH, 0, S, T, MF, MI, ps)
        stage_gates_out(nc, pool, U, X1, X, XF, Wout, Bout, V, ident, ps)
        stage_layernorm(nc, pool, X, H, stats, T, add=H, features=(XF, ident, ps, None, None))



def stages_mean_gated(nc, pool, K, H, XF, ident, ps):
    E, NQ = 8, 4
    with ExitStack() as ctx:
        def sb(name, shape):
            return ctx.enter_context(nc.sbuf_tensor("f2_" + name, shape, F32))

        wr, br = sb("wr", [P, E]), sb("br", [P, E])
        w1, wm, w2 = sb("w1", [P, 2, NQ, P]), sb("wm", [P, NQ, P]), sb("w2", [P, NQ, D])
        sel, b2 = sb("sel", [P, 2, NQ, P]), sb("b2", [P, P])
        bn, aff = sb("bn", [P, 2, 5, NQ]), sb("aff", [P, 2, 3, NQ])
        g, m = sb("g", [P, NB, E]), sb("m", [P, NB])
        gF, GT = sb("gf", [P, L]), sb("gt", [P, NQ, L])
        GA, GB_, OF = sb("ga", [P, 4, 512]), sb("gb", [P, 4, 512]), sb("of", [P, 4, 512])
        names, other = pool.stage()
        w_in, made, v_step, for_sqrt, rooted, centred, exped, weighed, turned, copied, zeroed = (
            next(names) for _ in range(11))
        with nc.Block(no_gpsimd_drain=True) as block:
            @block.sync
            def _(sync):
                pool.clear(sync, other)
                load(sync, w_in, [(wr[:, :], K["f2_wr"]), (br[:, :], K["f2_br"].partition_broadcast(P)),
                                  (bn[:, :, :, :], K["f2_bn"]), (w1[:, :, :, :], K["f2_w1"]),
                                  (wm[:, :, :], K["f2_wm"]), (w2[:, :, :], K["f2_w2"]),
                                  (sel[:, :, :, :], K["m1_sel"]), (b2[:, :], K["f2_b2"])])
                sync.wait_ge(w_in, 8 * 16)

            @block.gpsimd
            def _(gp):
                gp.memset(gF[:, :], 0.0).then_inc(zeroed, 1)
                gp.wait_ge(zeroed, 1)

            @block.tensor
            def _(pe):
                pe.wait_ge(w_in, 8 * 16)
                for j in range(NB):
                    for b4 in range(HALF):
                        mm = pe.matmul(ps[:, 0, E * j:E * (j + 1)], XF[:, b4, PAD + P * j:PAD + P * (j + 1)],
                                       wr[:, :], start=(b4 == 0), stop=(b4 == HALF - 1))
                mm.then_inc(made, 1)
                pe.wait_ge(weighed, 1)
                for j in range(NB):
                    mm = pe.transpose(ps[0:E, 1 + j // 4, P * (j % 4):P * (j % 4 + 1)], g[:, j], ident)
                mm.then_inc(turned, 1)

            @block.scalar
            def _(act):
                act.wait_ge(for_sqrt, 1)
                act.activation(aff[:, :, 0], aff[:, :, 0], ACT.Sqrt).then_inc(rooted, 1)
                act.wait_ge(centred, 1)
                act.activation(g[:, :, :], g[:, :, :], ACT.Exp).then_inc(exped, 1)
                act.wait_ge(turned, 1)
                act.wait_ge(zeroed, 1)
                for k in range(2):
                    act.activation(gF[0:E, 512 * k:512 * (k + 1)], ps[0:E, 1 + k], ACT.Copy).then_inc(copied, 1)
                act.wait_ge(copied, 2)

            @block.vector
            def _(v):
                st = Steps(v, v_step)

                def tt(out, a, b, op):
                    st.do(v.tensor_tensor(out, a, b, op))

                v.wait_ge(w_in, 8 * 16)
                scale, shift = aff[:, :, 1], aff[:, :, 2]
                st.tell(v.tensor_scalar(aff[:, :, 0], bn[:, :, 4], 1e-3, None, ALU.add), for_sqrt, "s")
                v.wait_ge(rooted, 1)
                st.do(v.reciprocal(scale, aff[:, :, 0]))
                tt(scale, scale, bn[:, :, 1], ALU.mult)
                tt(shift, bn[:, :, 0], bn[:, :, 3], ALU.subtract)
                tt(shift, shift, scale, ALU.mult)
                tt(shift, shift, bn[:, :, 2], ALU.add)
                v.wait_ge(made, 1)
                src = ps[:, 0, 0:E * NB].rearrange("p (j e) -> p j e", e=E)
                st.do(v.scalar_tensor_tensor(out=g[:, :, :], in0=src, scalar=1.0 / B, in1=bcast(br[:, :], 1, NB),
                                             op0=ALU.mult, op1=ALU.add))
                st.do(v.tensor_reduce(m[:, :], g[:, :, :], AX, ALU.max))
                st.tell(v.tensor_tensor(g[:, :, :], g[:, :, :], bcast(m[:, :], 2, E), ALU.subtract), centred, "c")
                v.wait_ge(exped, 1)
                st.do(v.tensor_reduce(m[:, :], g[:, :, :], AX, ALU.add))
                st.do(v.reciprocal(m[:, :], m[:, :]))
                st.tell(v.tensor_tensor(g[:, :, :], g[:, :, :], bcast(m[:, :], 2, E), ALU.mult), weighed, "w")

        stage_gate_spread(nc, pool, gF, sel, GT, NQ, ps)
        stage_experts(nc, pool, H, XF, gF, w1, (aff[:, 0, 1], aff[:, 0, 2]), w2, b2[:, :], ident, ps,
                      (GA, GB_, OF), NQ, 1.0, ACT.Relu, middle=(wm, aff[:, 1, 1], aff[:, 1, 2]), gate_of=GT)



def stages_fast_weights(nc, pool, K, H, X, XF, stats, T, ident, ps):
    S, NH, DH = B, 8, 32
    C = NH * DH
    NE = 5 * C + 2 * NH
    with ExitStack() as ctx:
        def sb(name, shape):
            return ctx.enter_context(nc.sbuf_tensor("fw_" + name, shape, F32))

        wq, wo, gb = sb("wq", [P, 2, NE]), sb("wo", [P, 2, D]), sb("gb", [P, 2])
        QKV = [sb("qkv0", [P, S, NE]), sb("qkv1", [P, S, NE])]
        XJ = sb("xj", [P, HALF, P])
        G = sb("g", [P, S, S, 3, NH])
        GQ = sb("gq", [P, S, NH])
        M, MZ = sb("m", [P, S - 1, 2 * C]), sb("mz", [P, S, C])
        ns, mx = sb("ns", [P, 2, 3 * NH]), sb("mx", [P, NH])
        qs, hm, E = sb("qs", [P, C]), sb("hm", [P, 2, NH]), sb("e", [P, 2, 2 * C])
        hT = sb("ht", [P, 2, 2, P])
        stage_load(nc, pool, [(gb[:, :], K["fw_gb"]), (wq[:, :, :], K["fw_wq"]), (wo[:, :, :], K["fw_wo"])])
        stage_layernorm(nc, pool, H, X, stats, T, features=(XF, ident, ps, gb[:, 0:1], gb[:, 1:2]))
        slot = [(s % HALF, s // HALF) for s in range(S)]
        parts = [(0, 512), (512, 1024), (1024, NE)]
        PROJ, AB_BANK, OUT_BANK = 4, 3, 7
        QK_PROD = X
        RK_PROD = T[:, 0:NB // 2].rearrange("p a (b c) -> p (a b) c", c=C)
        H_PROD = T[:, NB // 2:NB].rearrange("p a (b c) -> p (a b) c", c=C)

        def heads(ap):
            n = len(ap.shape)
            return ap.rearrange("p (h d) -> p h d", d=DH) if n == 2 else ap.rearrange("p s (h d) -> p s h d", d=DH)

        def h_bank(t):
            return ps[:, t % 3, 0:C]

        def project(pe, s, made, copied, readied):
            b4, h = slot[s]
            for i, (lo, hi) in enumerate(parts):
                if s >= 1:
                    pe.wait_ge(copied, 4 * (s - 1) + (1, 3, 4)[i])
                    if i == 0:
                        pe.wait_ge(readied, 2 * (s - 1) + 1)
                pe.matmul(ps[:, PROJ + i, 0:hi - lo], XJ[:, b4], wq[:, h, lo:hi], start=True,
                          stop=True).then_inc(made, 1)

        def take(act, j, taken):
            act.activation(XJ[:, :, :], XF[:, :, bass.ds(PAD + P * j, P)], ACT.Copy).then_inc(taken, 1)

        def keep(act, Q, s, made, copied, readied):
            act.wait_ge(made, 3 * s + 1)
            if s >= 2:
                act.wait_ge(readied, 2 * (s - 2) + 1)
            e = E[:, s % 2]
            act.activation(e, ps[:, PROJ, 0:2 * C], ACT.Relu, scale=-1.0).then_inc(copied, 1)
            act.wait_ge(copied, 4 * s + 1)
            act.activation(e, e, ACT.Exp, scale=-1.0).then_inc(copied, 1)
            for i, (lo, hi) in list(enumerate(parts))[1:]:
                act.wait_ge(made, 3 * s + i + 1)
                act.activation(Q[:, s, lo:hi], ps[:, PROJ + i, 0:hi - lo], ACT.Copy).then_inc(copied, 1)

        def exp_rk(act, Q, s, readied, rk_exped):
            act.wait_ge(readied, 2 * s + 2)
            rk = Q[:, s, 2 * C:3 * C]
            act.activation(rk, rk, ACT.Exp).then_inc(rk_exped, 1)

        def ready(v, st, Q, s, copied, readied):
            rk = heads(Q[:, s, 2 * C:3 * C])
            v.wait_ge(copied, 4 * s + 2)
            st.tell(v.scalar_tensor_tensor(out=Q[:, s, 0:2 * C], in0=ps[:, PROJ, 0:2 * C], scalar=0.0,
                                           in1=E[:, s % 2], op0=ALU.max, op1=ALU.add), readied, "readied")
            v.wait_ge(copied, 4 * s + 3)
            st.do(v.tensor_reduce(mx[:, :], rk, AX, ALU.max))
            st.tell(v.tensor_tensor(rk, rk, bcast(mx[:, :], 2, DH), ALU.subtract), readied, "readied")

        def normalise(v, st, Q, s, rk_exped):
            v.wait_ge(rk_exped, s + 1)
            qkr, n = heads(Q[:, s, 0:3 * C]), ns[:, s % 2]
            st.do(v.tensor_reduce(n, qkr, AX, ALU.add))
            st.do(v.reciprocal(n, n))
            st.do(v.tensor_tensor(qkr, qkr, bcast(n, 2, DH), ALU.mult))

        def stage_project(Q):
            names, other = pool.stage()
            taken, made, copied, readied, rk_exped, v_step = (next(names) for _ in range(6))
            with nc.Block(no_gpsimd_drain=True) as block:
                @block.sync
                def _(sync):
                    pool.clear(sync, other)

                @block.tensor
                def _(pe):
                    pe.wait_ge(taken, 1)
                    for s in range(S):
                        project(pe, s, made, copied, readied)

                @block.scalar
                def _(act):
                    take(act, 0, taken)
                    for s in range(S):
                        keep(act, Q, s, made, copied, readied)
                        exp_rk(act, Q, s, readied, rk_exped)
                    act.wait_ge(copied, 4 * S)

                @block.vector
                def _(v):
                    st = Steps(v, v_step)
                    for s in range(S):
                        ready(v, st, Q, s, copied, readied)
                        normalise(v, st, Q, s, rk_exped)

        def stage_memories(Q, j, Qn, jn):
            names, other = pool.stage()
            (taken, made, copied, turned, in_sbuf, kept, projected, acted, shifted, g_made, dots, weighted, summed,
             corrected, read_ready, h_made, v_step, readied, rk_exped) = (next(names) for _ in range(19))
            qk, q_, k_, rk = Q[:, :, 0:2 * C], Q[:, :, 0:C], Q[:, :, C:2 * C], Q[:, :, 2 * C:3 * C]
            vv, v_, rv = Q[:, :, 3 * C:5 * C], Q[:, :, 3 * C:4 * C], Q[:, :, 4 * C:5 * C]
            betas = Q[:, :, 5 * C:NE]
            hs = q_
            with nc.Block(no_gpsimd_drain=True) as block:
                @block.sync
                def _(sync):
                    pool.clear(sync, other)

                @block.scalar
                def _(act):
                    if Qn is not None:
                        take(act, jn, taken)
                    act.activation(betas, betas, ACT.Sigmoid).then_inc(acted, 1)

                    def to_sbuf(t):
                        act.wait_ge(h_made, t + 1)
                        act.activation(hs[:, t], h_bank(t), ACT.Copy).then_inc(in_sbuf, 1)

                    def keep_turned(t):
                        act.wait_ge(turned, t + 1)
                        if t >= 2:
                            act.wait_ge(projected, t - 1)
                        act.activation(hT[:, t % 2].rearrange("p k t -> p (k t)"),
                                       ps[:, t % 3, C:2 * C], ACT.Copy).then_inc(kept, 1)

                    for t in range(S):
                        if t >= 1:
                            act.wait_ge(shifted, t)
                            act.activation(qs[:, :], qs[:, :], ACT.Exp).then_inc(acted, 1)
                            to_sbuf(t - 1)
                        if t >= 1 and Qn is not None:
                            exp_rk(act, Qn, t - 1, readied, rk_exped)
                        if Qn is not None:
                            keep(act, Qn, t, made, copied, readied)
                        if t >= 2:
                            keep_turned(t - 2)
                    if Qn is not None:
                        exp_rk(act, Qn, S - 1, readied, rk_exped)
                    to_sbuf(S - 1)
                    keep_turned(S - 2)
                    keep_turned(S - 1)

                @block.gpsimd
                def _(g):
                    def products(t):
                        if t >= 1:
                            g.wait_ge(g_made, t)
                        g.tensor_tensor(QK_PROD[:, 0:t + 1].rearrange("p s (n c) -> p s n c", n=2),
                                        bcast(k_[:, 0:t + 1], 2, 2),
                                        bcast(qk[:, t].rearrange("p (n c) -> p n c", n=2), 1, t + 1),
                                        ALU.mult).then_inc(dots, 1)
                        if t:
                            g.tensor_tensor(RK_PROD[:, 0:t], rk[:, 0:t], bcast(rk[:, t], 1, t),
                                            ALU.mult).then_inc(dots, 1)

                    def weigh_old(t):
                        g.wait_ge(g_made, t + 1)
                        if t >= 2:
                            g.wait_ge(summed, 2 * (t - 1))
                        g.tensor_tensor(heads(M[:, 0:t]), heads(vv[:, 0:t]),
                                        bcast(G[:, 0:t, t, 1:3].rearrange("p s n h -> p s (n h)"), 3, DH),
                                        ALU.mult).then_inc(weighted, 1)

                    def weigh_read(t):
                        g.wait_ge(corrected, t + 1)
                        if t:
                            g.wait_ge(summed, 2 * t - 1)
                        g.tensor_tensor(heads(MZ[:, 0:t + 1]), heads(v_[:, 0:t + 1]),
                                        bcast(G[:, 0:t + 1, t, 0], 3, DH), ALU.mult).then_inc(weighted, 1)

                    products(0)
                    products(1)
                    for t in range(S):
                        if t + 2 < S:
                            products(t + 2)
                        weigh_read(t)
                        if t + 1 < S:
                            weigh_old(t + 1)

                @block.tensor
                def _(pe):
                    def sum_old(t):
                        pe.wait_ge(weighted, 2 * t)
                        for s in range(t):
                            mm = pe.matmul(ps[:, AB_BANK], ident, M[:, s], start=(s == 0), stop=(s == t - 1))
                        mm.then_inc(summed, 1)

                    def sum_read(t):
                        pe.wait_ge(weighted, 2 * t + 1)
                        if t >= 3:
                            pe.wait_ge(kept, t - 2)
                            pe.wait_ge(shifted, t - 2)
                        for s in range(t + 1):
                            mm = pe.matmul(h_bank(t), ident, MZ[:, s], start=(s == 0), stop=False)
                        mm.then_inc(summed, 1)

                    def sum_recurrent(t):
                        pe.wait_ge(read_ready, t + 1)
                        for s in range(t + 1):
                            mm = pe.matmul(h_bank(t), ident, H_PROD[:, s], start=False, stop=(s == t))
                        mm.then_inc(h_made, 1)

                    def turn(t):
                        pe.wait_ge(in_sbuf, t + 1)
                        for k in range(2):
                            at = C + P * k
                            mm = pe.transpose(ps[:, t % 3, at:at + P], hs[:, t, P * k:P * (k + 1)], ident)
                        mm.then_inc(turned, 1)

                    def out(t):
                        pe.wait_ge(kept, t + 1)
                        b4, h = slot[t]
                        at = P * b4 + D * h
                        for k in range(2):
                            mm = pe.matmul(ps[:, OUT_BANK, at:at + D], hT[:, t % 2, k], wo[:, k], start=(k == 0),
                                           stop=(k == 1))
                        mm.then_inc(projected, 1)

                    if Qn is not None:
                        pe.wait_ge(taken, 1)
                        project(pe, 0, made, copied, readied)
                    for t in range(S):
                        sum_read(t)
                        sum_recurrent(t)
                        if t >= 1:
                            turn(t - 1)
                        if Qn is not None and t + 1 < S:
                            project(pe, t + 1, made, copied, readied)
                        if t + 1 < S:
                            sum_old(t + 1)
                        if t >= 2:
                            out(t - 2)
                    turn(S - 1)
                    out(S - 2)
                    out(S - 1)

                @block.vector
                def _(v):
                    st = Steps(v, v_step)

                    def tt(out, a, b, op):
                        st.do(v.tensor_tensor(out, a, b, op))

                    def sum_dots(t):
                        v.wait_ge(dots, max(2 * t, 1))
                        qk_dots = v.tensor_reduce(G[:, 0:t + 1, t, 0:2].rearrange("p s n h -> p s (n h)"),
                                                  heads(QK_PROD[:, 0:t + 1]), AX, ALU.add)
                        if t:
                            st.do(qk_dots)
                            v.wait_ge(dots, 2 * t + 1)
                            st.tell(v.tensor_reduce(G[:, 0:t, t, 2], heads(RK_PROD[:, 0:t]), AX, ALU.add), g_made, "g")
                        else:
                            st.tell(qk_dots, g_made, "g")

                    def correct(t):
                        if t:
                            v.wait_ge(summed, 2 * t)
                            tt(vv[:, t], vv[:, t], ps[:, AB_BANK], ALU.subtract)
                        st.tell(v.tensor_tensor(heads(vv[:, t]), heads(vv[:, t]), bcast(betas[:, t], 2, DH),
                                                ALU.mult), corrected, "corrected")

                    sum_dots(0)
                    v.wait_ge(acted, 1)
                    sum_dots(1)
                    for t in range(S):
                        if t == 0:
                            st.do(v.memset(qs[:, :], 1.0))
                        else:
                            v.wait_ge(h_made, t)
                            h = heads(h_bank(t - 1))
                            st.do(v.tensor_reduce(hm[:, 0], h, AX, ALU.max))
                            st.tell(v.tensor_tensor(heads(qs[:, :]), h, bcast(hm[:, 0], 2, DH), ALU.subtract),
                                    shifted, "shifted")
                            v.wait_ge(acted, 1 + t)
                        st.do(v.tensor_reduce(hm[:, 1], heads(qs[:, :]), AX, ALU.add))
                        st.go(v.reciprocal(hm[:, 1], hm[:, 1]))
                        tt(H_PROD[:, 0:t + 1], rk[:, 0:t + 1], bcast(qs[:, :], 1, t + 1), ALU.mult)
                        g = GQ[:, 0:t + 1]
                        st.do(v.tensor_reduce(g, heads(H_PROD[:, 0:t + 1]), AX, ALU.add))
                        tt(g, g, bcast(hm[:, 1], 1, t + 1), ALU.mult)
                        correct(t)
                        st.tell(v.tensor_tensor(heads(H_PROD[:, 0:t + 1]), heads(rv[:, 0:t + 1]), bcast(g, 3, DH),
                                                ALU.mult), read_ready, "read")
                        if Qn is not None:
                            ready(v, st, Qn, t, copied, readied)
                        if t + 2 < S:
                            sum_dots(t + 2)
                        if t >= 1 and Qn is not None:
                            normalise(v, st, Qn, t - 1, rk_exped)
                    if Qn is not None:
                        normalise(v, st, Qn, S - 1, rk_exped)
                    v.wait_ge(projected, S)
                    hh = H[:, bass.ds(j, 1)].rearrange("p o c -> p (o c)")
                    st.do(v.scalar_tensor_tensor(out=hh, in0=hh, scalar=2.0, in1=ps[:, OUT_BANK], op0=ALU.mult,
                                                 op1=ALU.add))

        stage_project(QKV[0])
        pool.open_loop()
        with nc.Fori(0, NB // 2 - 1) as pair:
            stage_memories(QKV[0], pair * 2, QKV[1], pair * 2 + 1)
            stage_memories(QKV[1], pair * 2 + 1, QKV[0], pair * 2 + 2)
            pool.even(nc)
        stage_memories(QKV[0], NB - 2, QKV[1], NB - 1)
        stage_memories(QKV[1], NB - 1, None, None)



def stage_store(nc, pool, H, out):
    names, other = pool.stage()
    stored = next(names)
    with nc.Block() as block:
        @block.sync
        def _(sync):
            pool.clear(sync, other)
            for b in range(B):
                at = P * (b % HALF) + D * (b // HALF)
                sync.dma_start(out[b].rearrange("(j p) d -> p j d", p=P), H[:, :, at:at + D]).then_inc(stored, 16)
            sync.wait_ge(stored, 16 * B)


def tower(nc, K, out):
    with ExitStack() as ctx:
        def sb(name, shape):
            return ctx.enter_context(nc.sbuf_tensor(name, shape, F32))

        H, X, XF = sb("H", [P, NB, W]), sb("X", [P, NB, W]), sb("XF", [P, HALF, LF])
        stats, ident_t, fold = sb("stats", [P, 2 * NB * B]), sb("ident", [P, P]), sb("fold_halves", [P, D])
        ps = ctx.enter_context(nc.psum_tensor("ps", [P, 8, 512], F32))
        pool = Pool2(nc, ctx)
        K = dict(K)
        stage_load(nc, pool, [(ident_t[:, :], K["ident"]), (fold[:, :], K["fold_halves"])])
        ident = K["ident"] = ident_t[:, :]
        K["fold_halves"] = fold[:, :]
        stage_zero_pads(nc, pool, XF)
        plain = (XF, ident, ps, None, None)

        stage_patches(nc, pool, K, H, K["x"], ps)
        stage_attention(nc, pool, K, H, ps)
        with ExitStack() as inner:
            T = inner.enter_context(nc.sbuf_tensor("T0", [P, NB, W], F32))
            stage_layernorm(nc, pool, H, H, stats, T, features=plain)
            stage_routed(nc, pool, K, H, XF, ps)
            stage_layernorm(nc, pool, H, H, stats, T)
        with ExitStack() as inner:
            def sb2(name, shape):
                return inner.enter_context(nc.sbuf_tensor(name, shape, F32))

            T, U, S, KH = sb2("T", [P, 12, W]), sb2("U", [P, NB, W]), sb2("S", [P, 16, W]), sb2("KH", [P, 4, NF, 3, D])
            MF, MI = sb2("MF", [P, 3 * NF, P]), sb2("MI", [P, 3 * NF, P])
            matrices = [(m[:, :, :], K[k].rearrange("p (a b) -> p a b", b=P)) for m, k in ((MF, "fwd"), (MI, "inv"))]
            stage_load(nc, pool, matrices)
            stages_state_space(nc, pool, K, H, X, XF, U, S, T, KH, MF, MI, stats, ident, ps)
        with ExitStack() as inner:
            T = inner.enter_context(nc.sbuf_tensor("T1", [P, NB, W], F32))
            stages_moe(nc, pool, K, "m1_", H, XF, ident, ps, 4, True, 2.0)
            stage_layernorm(nc, pool, H, H, stats, T)
        with ExitStack() as inner:
            def sb3(name, shape):
                return inner.enter_context(nc.sbuf_tensor(name, shape, F32))

            T, U, S, KH = sb3("T_", [P, 12, W]), sb3("U_", [P, NB, W]), sb3("S_", [P, 16, W]), sb3("KH_", [P, 1, NF, 3, D])
            MF, MI = sb3("MF_", [P, 3 * NF, P]), sb3("MI_", [P, 3 * NF, P])
            matrices = [(m[:, :, :], K[k].rearrange("p (a b) -> p a b", b=P)) for m, k in ((MF, "fwd"), (MI, "inv"))]
            stage_load(nc, pool, matrices)
            stages_hyena(nc, pool, K, H, X, XF, U, S, T, KH, MF, MI, stats, ident, ps)
        with ExitStack() as inner:
            T = inner.enter_context(nc.sbuf_tensor("T2", [P, NB, W], F32))
            gb = inner.enter_context(nc.sbuf_tensor("gb3", [P, 2], F32))
            stages_mean_gated(nc, pool, K, H, XF, ident, ps)
            stage_layernorm(nc, pool, H, H, stats, T)
            stages_fast_weights(nc, pool, K, H, X, XF, stats, T, ident, ps)
            stage_layernorm(nc, pool, H, H, stats, T)
            stage_load(nc, pool, [(gb[:, :], K["m3_gb"])])
            stage_layernorm(nc, pool, H, X, stats, T, features=(XF, ident, ps, gb[:, 0:1], gb[:, 1:2]))
            stages_moe(nc, pool, K, "m3_", H, XF, ident, ps, 8, False, 1.0)
            stage_layernorm(nc, pool, H, H, stats, T)
        stage_store(nc, pool, H, out)



def block_diagonal(a):
    k, n = a.shape[-2:]
    out = np.zeros(a.shape[:-2] + (2 * k, 2 * n), a.dtype)
    out[..., :k, :n], out[..., k:, n:] = a, a
    return out


def constants():
    f32 = np.float32
    c = {}
    c["ident"] = np.eye(P, dtype=f32)
    c["fold_halves"] = np.concatenate([np.eye(D), np.eye(D)]).astype(f32)
    f, p = np.arange(9)[:, None], np.arange(16)[None, :]
    a = 2 * np.pi * ((f * p) % 16) / 16
    c["tok_dft"] = (np.concatenate([np.cos(a), -np.sin(a)]) / 4).astype(f32)
    c["fwd"], c["inv"] = transform_constants()
    attention_constants(c)
    state_constants(c)
    moe_constants(c)
    hyena_constants(c)
    return c


def lay_out(i):
    o = {}
    w = i["L0_tok_W"].reshape(D, 2 * 9, D).transpose(1, 0, 2)
    o["tok_W"] = np.concatenate([w, w], 2)
    o["x"] = i["x"]
    attention_layout(i, o)
    routed_layout(i, o)
    state_layout(i, o)
    moe1_layout(i, o)
    hyena_layout(i, o)
    mean_gated_layout(i, o)
    fast_weights_layout(i, o)
    return o


def rope_tables():
    half = 8
    theta = (np.float32(1.0) / np.float32(10000.0) ** (np.arange(half, dtype=np.float32) / np.float32(half)))
    a = np.arange(L, dtype=np.float32)[None, :] * theta.astype(np.float32)[:, None]
    cos, sin = np.ones((D, L), np.float32), np.zeros((D, L), np.float32)
    cos[48::2], cos[49::2] = np.cos(a), np.cos(a)
    sin[48::2], sin[49::2] = -np.sin(a), np.sin(a)
    t = np.stack([cos, sin], 1)
    return np.concatenate([t, t]).astype(np.float32)


def attention_constants(c):
    c["at_rope"] = rope_tables()
    c["at_mask"] = np.triu(np.full((P, P), -1e30, np.float32), 1)


def attention_layout(i, o):
    swap = np.arange(D)
    swap[48::2], swap[49::2] = np.arange(49, D, 2), np.arange(48, D, 2)
    q = np.concatenate([i["L0_attn_Wqc"], i["L0_attn_Wqr"]], 1)
    k = np.concatenate([i["L0_attn_Wkc"], i["L0_attn_Wkr"]], 1)
    o["at_wl"] = np.stack([block_diagonal(i["L0_attn_Wq_comp"].T), block_diagonal(i["L0_attn_Wkv_comp"].T)], 1)
    o["at_wr"] = np.stack([block_diagonal(m) for m in (q, q[:, swap], k, k[:, swap], i["L0_attn_Wv"])], 1)


def halves(a):
    z = np.zeros_like(a)
    return np.stack([np.concatenate([a, z]), np.concatenate([z, a])], 1)


def routed_layout(i, o):
    wr, br = i["L0_ffn_Wr"], i["L0_ffn_br"]
    w = np.concatenate([wr.transpose(0, 1, 3, 2), br[..., None]], 3)
    w = np.concatenate([w, np.zeros_like(w[:, :1])], 1)
    o["f0_wr"] = w.reshape(-1, 128, 129)
    o["f0_route"] = i["L0_ffn_route_id"].reshape(1, 64)
    o["f0_wi"] = halves(i["L0_ffn_Wi"].T)
    o["f0_ws"] = i["L0_ffn_Ws"][:, 0].transpose(2, 0, 1)
    o["f0_wo"] = i["L0_ffn_Wo"].T
    o["f0_bi"], o["f0_bs"] = i["L0_ffn_bi"][:, None], i["L0_ffn_bs"][:, 0].T
    o["f0_bo"] = i["L0_ffn_bo"]


def state_constants(c):
    c["s4_lv"] = np.tile(np.arange(P, dtype=np.float32), (P, 1))
    c["s4_jv"] = np.tile(P * np.arange(NB, dtype=np.float32), (P, 1))
    cos_rows = (np.arange(P) < D).astype(np.float32)
    ph, ph2 = 0.25 * cos_rows, 0.25 * (1 - cos_rows)
    a = 0.25 * 6.2831845
    c["s4_cols"] = np.stack([ph, ph2, 2 * cos_rows - 1, a * cos_rows, a * (1 - cos_rows),
                             np.full(P, a)], 1).astype(np.float32)


def state_layout(i, o):
    n = 4
    dt = np.broadcast_to(i["L1_attn_log_dt"][:, None, :], (n, D, D))
    par = [dt] + [i["L1_attn_" + k].transpose(0, 2, 1) for k in ("Alog", "Aim", "Cre", "Cim")]
    par = np.stack(par, 2)
    o["s4_par"] = np.concatenate([par, par], 1)
    o["s4_D"] = i["L1_attn_D"]
    w, b = i["L1_attn_Wout"], i["L1_attn_bout"]
    w1, w2 = (block_diagonal(w[:, D * k:D * (k + 1)].transpose(0, 2, 1)) for k in range(2))
    o["s4_wout"] = np.concatenate([w1, w2], 2)
    o["s4_bout"] = np.concatenate([b[:, :D], b[:, :D], b[:, D:], b[:, D:]], 1)
    o["s4_gb"] = np.stack([i["L1_attn_ln_scale"], i["L1_attn_ln_bias"]], 1)


def spread(per):
    s = np.zeros((P, 2, 8 // per, P), np.float32)
    for h in range(2):
        for e in range(8):
            w = P // per
            s[h * 8 + e:16 * GATE_PARTS:16, h, e // per, w * (e % per):w * (e % per + 1)] = 1
    return s


def experts_layout(o, pre, w1, b1, w2, b2):
    k = w1.shape[2]
    per = P // k
    nq = 8 // per
    a = w1.reshape(nq, per, D, k).transpose(0, 2, 1, 3).reshape(nq, D, P)
    o[pre + "w1"] = np.stack([halves(m) for m in a], 2)
    o[pre + "w2"] = w2.reshape(nq, P, D).transpose(1, 0, 2)
    o[pre + "b1"] = b1.reshape(nq, P).T
    z = np.zeros((P, P), np.float32)
    for k in range(GATE_PARTS):
        z[16 * k:16 * k + 8, 0:D], z[16 * k + 8:16 * k + 16, D:] = b2, b2
    o[pre + "b2"] = z


def moe1_layout(i, o):
    experts_layout(o, "m1_", i["L1_ffn_w1"], i["L1_ffn_b1"], i["L1_ffn_w2"], i["L1_ffn_b2"])
    o["m1_router"] = block_diagonal(i["L1_ffn_router_w"].T)
    experts_layout(o, "m3_", i["L3_ffn_W1"], i["L3_ffn_b1"], i["L3_ffn_W2"], i["L3_ffn_b2"])
    o["m3_router"] = block_diagonal(i["L3_ffn_Wr"])
    o["m3_rb"] = i["L3_ffn_br"]
    o["m3_gb"] = np.stack([np.tile(i["L3_ffn_gamma"], 2), np.tile(i["L3_ffn_beta"], 2)], 1)


def moe_constants(c):
    c["rank"] = np.tile(np.arange(8, 0, -1, dtype=np.float32), (P, 1))
    c["m1_sel"], c["m3_sel"] = spread(2), spread(1)


def hyena_constants(c):
    f32 = np.float32
    t01 = np.linspace(0.0, 1.0, L).astype(f32)
    tr = np.linspace(0.0, float(L - 1), L).astype(f32)
    ang = (f32(2.0 * np.pi / L) * tr * f32(0.0001)).astype(f32)
    c["hy_z"] = np.stack([t01, np.cos(ang), -np.sin(ang)]).astype(f32)
    deltas = np.linspace(math.log(0.01) / 1.5, math.log(0.01) / 0.3, D).astype(f32)
    decay = np.exp(-t01[:, None] * np.abs(deltas)).astype(f32)
    c["hy_decay"] = decay.reshape(NB, P, D).transpose(1, 0, 2).reshape(P, -1)
    p = np.arange(P)
    c["hw_edge"] = np.stack([p >= 1, p >= 2, p < P - 1, p >= 0], 1).astype(f32)


def hyena_layout(i, o):
    g = {k[8:]: v for k, v in i.items() if k.startswith("L2_attn_")}
    o["hy_w0"] = g["mlp_w0"].T
    o["hy_w12"] = np.stack([g["mlp_w1"].T, g["mlp_w2"].T], 1)
    o["hy_w3"] = g["mlp_w3"].T
    o["hy_bf"] = np.stack([g["mlp_b0"], g["mlp_b1"], g["mlp_b2"], g["sin_freq"]], 1)
    o["hy_fb"] = g["filt_bias"][None]
    o["hy_gb"] = np.stack([np.tile(g["ln_g"], 2), np.tile(g["ln_b"], 2)], 1)

    def both(a):
        a = a.reshape(a.shape[:-1] + (3, 1, D))
        return np.concatenate([a, a], -2).reshape(a.shape[:-3] + (3 * P,))

    w = [block_diagonal(g["in_w"][D * k:D * (k + 1)].T) for k in range(3)]
    o["hw_w"] = np.concatenate(w, 1)
    o["hw_wo"] = block_diagonal(g["out_w"].T)
    o["hw_taps"] = both(np.ascontiguousarray(g["sf_w"][:, 0].T))
    o["hw_otaps"] = np.tile(g["conv_w"][:, 0].T, (1, 2))
    o["hw_rows"] = both(np.stack([g["in_b"], g["sf_b"]]))
    o["hw_orow"] = np.tile(g["out_b"], 2)


def mean_gated_layout(i, o):
    g = {k[7:]: v for k, v in i.items() if k.startswith("L2_ffn_")}
    experts_layout(o, "f2_", g["W1"], g["b1"], g["Wo"], g["bo"])
    z = np.zeros((P, P), np.float32)
    z[0:8] = np.tile(g["bo"], (1, 2))
    o["f2_b2"] = z
    o["f2_wr"], o["f2_br"] = np.tile(g["Wr"], (2, 1)), g["br"]
    w = g["W2"].reshape(4, 2, D, D)
    wm = np.zeros((P, 4, P), np.float32)
    for k in range(2):
        wm[D * k:D * (k + 1), :, D * k:D * (k + 1)] = w[:, k].transpose(1, 0, 2)
    o["f2_wm"] = wm
    o["f2_bn"] = np.stack([np.stack([g[k + n].reshape(4, P).T for k in ("b", "g", "be", "m", "v")], 1)
                           for n in "12"], 1)


def fast_weights_layout(i, o):
    g = {k[8:]: v for k, v in i.items() if k.startswith("L3_attn_")}
    w = g["slow_W"].reshape(8, 162, D)
    w = np.concatenate([w[:, 32 * n:32 * (n + 1)].reshape(-1, D) for n in (0, 1, 3, 2, 4)] + [w[:, 160], w[:, 161]])
    o["fw_wq"] = halves(w.T)
    o["fw_wo"] = g["out_W"].T.reshape(2, P, D).transpose(1, 0, 2)
    o["fw_gb"] = np.stack([np.tile(g["ln_g"], 2), np.tile(g["ln_b"], 2)], 1)




def kernel(**inputs):
    import concourse.bacc as _bacc
    from concourse.bass_utils import run_bass_kernel_spmd as _run

    nc = _bacc.Bacc("TRN2", target_bir_lowering=False, num_devices=1)
    host = lay_out({k: np.asarray(v) for k, v in inputs.items()})
    host.update(constants())
    arrays, K = {}, {}
    for name, a in host.items():
        a = np.ascontiguousarray(a)
        arrays["in_" + name] = a
        K[name] = nc.dram_tensor("in_" + name, a.shape, mybir.dt.from_np(a.dtype), kind="ExternalInput").ap()
    out = nc.dram_tensor("out_0", (B, L, D), F32, kind="ExternalOutput").ap()
    tower(nc, K, out)
    r = _run(nc, [arrays], core_ids=[0])
    return r.results[0]["out_0"]
```
